# Optimizing a Trainium2 kernel written in Bass

```python
import numpy as np
import jax
import jax.numpy as jnp

def _softmax(x, axis=-1):
    return jax.nn.softmax(x, axis=axis)

def _gelu(x):
    return jax.nn.gelu(x, approximate=True)

def _silu(x):
    return jax.nn.silu(x)

def _sigmoid(x):
    return jax.nn.sigmoid(x)

def _layernorm(x, axis=-1, eps=1e-05):
    m = jnp.mean(x, axis=axis, keepdims=True)
    v = jnp.var(x, axis=axis, keepdims=True)
    return (x - m) / jnp.sqrt(v + eps)

def _scatter_add(tgt, idx, src, axis=0):
    return tgt.at[idx].add(src)

def _segment_sum(src, seg, n):
    return jax.ops.segment_sum(src, seg, n)
kernel_name = 'mk_decoder_preln_d1_seqx_r4_8250ce'

def setup_inputs(seed: int=0):
    np.random.seed(seed)
    _w = jnp.asarray

    def _rec_inputs():
        import jax
        import jax.numpy as jnp
        _rk = jax.random.key(seed)
        x = -0.0003929 + 0.9999 * jax.random.normal(jax.random.fold_in(_rk, 1), (2, 1024, 256), jnp.float32)
        _lenS = 1024 - jax.random.randint(jax.random.fold_in(_rk, 7), (2,), 0, max(1, 1024 // 4) + 1, jnp.int32)
        _lenS2 = 77 - jax.random.randint(jax.random.fold_in(_rk, 8), (2,), 0, max(1, 77 // 4) + 1, jnp.int32)
        _ctx_1024P = jax.random.normal(jax.random.fold_in(_rk, 11), (2, 16, 256), jnp.float32)
        _ctx_1024c = jax.random.dirichlet(jax.random.fold_in(_rk, 511), 0.3 * jnp.ones((16,), jnp.float32), (2, 77))
        _ctx_1024t = jnp.einsum('bsk,bkd->bsd', _ctx_1024c, _ctx_1024P)
        _ctx_1024t = _ctx_1024t * jax.lax.rsqrt(jnp.mean(jnp.square(_ctx_1024t)) + 1e-12) * 0.953939
        ctx_1024 = 4.13588e-05 + 0.999923 * (_ctx_1024t + 0.3 * jax.random.normal(jax.random.fold_in(_rk, 611), (2, 77, 256), jnp.float32))
        return (x, ctx_1024)
    x, ctx_1024 = _rec_inputs()

    def _L0_attn_setup():
        import jax, jax.numpy as jnp
        import numpy as np
        D_MODEL = 256
        D_STATE = 64
        D_CONV = 4
        EXPAND = 2
        HEADDIM = 64
        NGROUPS = 1
        D_INNER = EXPAND * D_MODEL
        NHEADS = D_INNER // HEADDIM
        CONV_DIM = D_INNER + 2 * NGROUPS * D_STATE
        D_IN_PROJ = 2 * D_INNER + 2 * NGROUPS * D_STATE + NHEADS
        BATCH, SEQLEN = (2, 1024)
        CHUNK = 64
        LN_EPS = 1e-05
        RMS_EPS = 1e-05

        def _segsum(a):
            q = a.shape[-1]
            cs = jnp.cumsum(a, axis=-1)
            seg = cs[..., :, None] - cs[..., None, :]
            mask = jnp.tril(jnp.ones((q, q), dtype=bool))
            return jnp.where(mask, seg, -jnp.inf)

        def _ssd(xdt, Adt, Bm, Cm):
            b, l, h, p = xdt.shape
            c = l // CHUNK
            X = xdt.reshape(b, c, CHUNK, h, p)
            A = Adt.reshape(b, c, CHUNK, h).transpose(0, 3, 1, 2)
            Bq = Bm.reshape(b, c, CHUNK, -1)
            Cq = Cm.reshape(b, c, CHUNK, -1)
            A_cum = jnp.cumsum(A, -1)
            Lmat = jnp.exp(_segsum(A))
            Y_diag = jnp.einsum('bcln,bcsn,bhcls,bcshp->bclhp', Cq, Bq, Lmat, X)
            decay_states = jnp.exp(A_cum[..., -1:] - A_cum)
            states = jnp.einsum('bcln,bhcl,bclhp->bchpn', Bq, decay_states, X)
            chunk_decay = jnp.exp(A_cum[..., -1])

            def step(hprev, inp):
                s, dec = inp
                return (dec[..., None, None] * hprev + s, hprev)
            h0 = jnp.zeros((b, h, p, states.shape[-1]), xdt.dtype)
            _, prev = jax.lax.scan(step, h0, (jnp.moveaxis(states, 1, 0), jnp.moveaxis(chunk_decay, 2, 0)))
            prev = jnp.moveaxis(prev, 0, 1)
            Y_off = jnp.einsum('bcln,bchpn,bhcl->bclhp', Cq, prev, jnp.exp(A_cum))
            return (Y_diag + Y_off).reshape(b, l, h, p)
        key = jax.random.key(seed)
        ks = jax.random.split(key, 8)
        dt = jnp.exp(jax.random.uniform(ks[3], (NHEADS,)) * (np.log(0.1) - np.log(0.001)) + np.log(0.001))
        dt_bias = dt + jnp.log(-jnp.expm1(-dt))
        return {'x': jax.random.normal(ks[0], (BATCH, SEQLEN, D_MODEL), jnp.float32), 'ln_w': jnp.ones((D_MODEL,), jnp.float32), 'ln_b': jnp.zeros((D_MODEL,), jnp.float32), 'in_proj_w': 0.02 * jax.random.normal(ks[1], (D_IN_PROJ, D_MODEL), jnp.float32), 'conv_w': 0.2 * jax.random.normal(ks[2], (CONV_DIM, 1, D_CONV), jnp.float32), 'conv_b': jnp.zeros((CONV_DIM,), jnp.float32), 'dt_bias': dt_bias, 'A_log': jnp.log(1.0 + 15.0 * jax.random.uniform(ks[4], (NHEADS,), jnp.float32)), 'D_skip': jnp.ones((NHEADS,), jnp.float32), 'norm_w': jnp.ones((D_INNER,), jnp.float32), 'out_proj_w': 0.02 * jax.random.normal(ks[5], (D_MODEL, D_INNER), jnp.float32)}
    _L0_attn_all = _L0_attn_setup()
    _L0_attn_in = {k: v for k, v in _L0_attn_all.items() if k in ('ln_w', 'ln_b', 'in_proj_w', 'conv_w', 'conv_b', 'dt_bias', 'A_log', 'D_skip', 'norm_w', 'out_proj_w')}
    del _L0_attn_all

    def _L0_xattn_setup():
        import jax, jax.numpy as jnp
        import numpy as np
        key = jax.random.key(seed)
        k1, k2 = jax.random.split(key)
        B, L, V, D = (8, 512, 256, 256)
        hidden_states = jax.random.normal(k1, (B, L, D), dtype=jnp.float32)
        visual_hidden_state = jax.random.normal(k2, (B, V, D), dtype=jnp.float32)
        return {'hidden_states': hidden_states, 'visual_hidden_state': visual_hidden_state}
    _L0_xattn_all = _L0_xattn_setup()
    _L0_xattn_in = {k: v for k, v in _L0_xattn_all.items() if k in ()}
    del _L0_xattn_all

    def _L0_ffn_setup():
        import jax, jax.numpy as jnp
        import numpy as np
        E = 64
        K = 6
        CAP = 128
        ROUTE_SCALE = 1.0
        key = jax.random.key(seed)
        ks = jax.random.split(key, 9)
        B, S, D, I = (2, 256, 256, 176)
        SI = 2 * I
        s = 0.02
        return {'x': jax.random.normal(ks[0], (B, S, D), jnp.float32), 'gate_w': jax.random.normal(ks[1], (E, D), jnp.float32) * s, 'gate_b': jnp.zeros((E,), jnp.float32), 'w1': jax.random.normal(ks[2], (E, I, D), jnp.float32) * s, 'w2': jax.random.normal(ks[3], (E, D, I), jnp.float32) * s, 'w3': jax.random.normal(ks[4], (E, I, D), jnp.float32) * s, 'ws1': jax.random.normal(ks[5], (SI, D), jnp.float32) * s, 'ws2': jax.random.normal(ks[6], (D, SI), jnp.float32) * s, 'ws3': jax.random.normal(ks[7], (SI, D), jnp.float32) * s}
    _L0_ffn_all = _L0_ffn_setup()
    _L0_ffn_in = {k: v for k, v in _L0_ffn_all.items() if k in ('gate_w', 'gate_b', 'w1', 'w2', 'w3', 'ws1', 'ws2', 'ws3')}
    del _L0_ffn_all
    return {'x': x, 'ctx_1024': ctx_1024, 'L0_attn_ln_w': _L0_attn_in['ln_w'], 'L0_attn_ln_b': _L0_attn_in['ln_b'], 'L0_attn_in_proj_w': _L0_attn_in['in_proj_w'], 'L0_attn_conv_w': _L0_attn_in['conv_w'], 'L0_attn_conv_b': _L0_attn_in['conv_b'], 'L0_attn_dt_bias': _L0_attn_in['dt_bias'], 'L0_attn_A_log': _L0_attn_in['A_log'], 'L0_attn_D_skip': _L0_attn_in['D_skip'], 'L0_attn_norm_w': _L0_attn_in['norm_w'], 'L0_attn_out_proj_w': _L0_attn_in['out_proj_w'], 'L0_ffn_gate_w': _L0_ffn_in['gate_w'], 'L0_ffn_gate_b': _L0_ffn_in['gate_b'], 'L0_ffn_w1': _L0_ffn_in['w1'], 'L0_ffn_w2': _L0_ffn_in['w2'], 'L0_ffn_w3': _L0_ffn_in['w3'], 'L0_ffn_ws1': _L0_ffn_in['ws1'], 'L0_ffn_ws2': _L0_ffn_in['ws2'], 'L0_ffn_ws3': _L0_ffn_in['ws3']}

def reference(x, ctx_1024, L0_attn_ln_w, L0_attn_ln_b, L0_attn_in_proj_w, L0_attn_conv_w, L0_attn_conv_b, L0_attn_dt_bias, L0_attn_A_log, L0_attn_D_skip, L0_attn_norm_w, L0_attn_out_proj_w, L0_ffn_gate_w, L0_ffn_gate_b, L0_ffn_w1, L0_ffn_w2, L0_ffn_w3, L0_ffn_ws1, L0_ffn_ws2, L0_ffn_ws3):
    import jax
    import jax.numpy as jnp

    def _L0_attn_ref(x, ln_w, ln_b, in_proj_w, conv_w, conv_b, dt_bias, A_log, D_skip, norm_w, out_proj_w):
        import jax, jax.numpy as jnp
        import numpy as np
        D_MODEL = 256
        D_STATE = 64
        D_CONV = 4
        EXPAND = 2
        HEADDIM = 64
        NGROUPS = 1
        D_INNER = EXPAND * D_MODEL
        NHEADS = D_INNER // HEADDIM
        CONV_DIM = D_INNER + 2 * NGROUPS * D_STATE
        D_IN_PROJ = 2 * D_INNER + 2 * NGROUPS * D_STATE + NHEADS
        BATCH, SEQLEN = (2, 1024)
        CHUNK = 64
        LN_EPS = 1e-05
        RMS_EPS = 1e-05

        def _segsum(a):
            q = a.shape[-1]
            cs = jnp.cumsum(a, axis=-1)
            seg = cs[..., :, None] - cs[..., None, :]
            mask = jnp.tril(jnp.ones((q, q), dtype=bool))
            return jnp.where(mask, seg, -jnp.inf)

        def _ssd(xdt, Adt, Bm, Cm):
            b, l, h, p = xdt.shape
            c = l // CHUNK
            X = xdt.reshape(b, c, CHUNK, h, p)
            A = Adt.reshape(b, c, CHUNK, h).transpose(0, 3, 1, 2)
            Bq = Bm.reshape(b, c, CHUNK, -1)
            Cq = Cm.reshape(b, c, CHUNK, -1)
            A_cum = jnp.cumsum(A, -1)
            Lmat = jnp.exp(_segsum(A))
            Y_diag = jnp.einsum('bcln,bcsn,bhcls,bcshp->bclhp', Cq, Bq, Lmat, X)
            decay_states = jnp.exp(A_cum[..., -1:] - A_cum)
            states = jnp.einsum('bcln,bhcl,bclhp->bchpn', Bq, decay_states, X)
            chunk_decay = jnp.exp(A_cum[..., -1])

            def step(hprev, inp):
                s, dec = inp
                return (dec[..., None, None] * hprev + s, hprev)
            h0 = jnp.zeros((b, h, p, states.shape[-1]), xdt.dtype)
            _, prev = jax.lax.scan(step, h0, (jnp.moveaxis(states, 1, 0), jnp.moveaxis(chunk_decay, 2, 0)))
            prev = jnp.moveaxis(prev, 0, 1)
            Y_off = jnp.einsum('bcln,bchpn,bhcl->bclhp', Cq, prev, jnp.exp(A_cum))
            return (Y_diag + Y_off).reshape(b, l, h, p)
        b, l, _ = x.shape
        mu = jnp.mean(x, -1, keepdims=True)
        var = jnp.mean(jnp.square(x - mu), -1, keepdims=True)
        xn = (x - mu) * jax.lax.rsqrt(var + LN_EPS) * ln_w + ln_b
        zxbcdt = xn @ in_proj_w.T
        z = zxbcdt[..., :D_INNER]
        xBC = zxbcdt[..., D_INNER:D_INNER + CONV_DIM]
        dt = zxbcdt[..., D_INNER + CONV_DIM:]
        xBC_t = jnp.transpose(xBC, (0, 2, 1))
        xBC_c = jax.lax.conv_general_dilated(xBC_t, conv_w, (1,), [(D_CONV - 1, 0)], dimension_numbers=('NCH', 'OIH', 'NCH'), feature_group_count=CONV_DIM)
        xBC = jax.nn.silu(jnp.transpose(xBC_c, (0, 2, 1)) + conv_b)
        xs = xBC[..., :D_INNER].reshape(b, l, NHEADS, HEADDIM)
        Bm = xBC[..., D_INNER:D_INNER + D_STATE]
        Cm = xBC[..., D_INNER + D_STATE:]
        dt = jax.nn.softplus(dt + dt_bias)
        A = -jnp.exp(A_log)
        y = _ssd(xs * dt[..., None], dt * A, Bm, Cm)
        y = y + D_skip[None, None, :, None] * xs
        y = y.reshape(b, l, D_INNER)
        yg = y * jax.nn.silu(z)
        yg = yg * jax.lax.rsqrt(jnp.mean(jnp.square(yg), -1, keepdims=True) + RMS_EPS) * norm_w
        return x + yg @ out_proj_w.T

    def _L0_xattn_ref(hidden_states, visual_hidden_state):
        import jax, jax.numpy as jnp
        import numpy as np
        scores = jnp.einsum('bld,bvd->blv', hidden_states, visual_hidden_state)
        probs = jax.nn.softmax(scores, axis=-1)
        return jnp.einsum('blv,bvd->bld', probs, visual_hidden_state)

    def _L0_ffn_ref(x, gate_w, gate_b, w1, w2, w3, ws1, ws2, ws3):
        import jax, jax.numpy as jnp
        import numpy as np
        E = 64
        K = 6
        CAP = 128
        ROUTE_SCALE = 1.0
        shape = x.shape
        D = shape[-1]
        xf = x.reshape(-1, D)
        T = xf.shape[0]
        scores = jax.nn.softmax(xf @ gate_w.T, axis=-1)
        _, idx = jax.lax.top_k(scores + gate_b, K)
        weights = jnp.take_along_axis(scores, idx, axis=1) * ROUTE_SCALE
        flat_e = idx.reshape(-1)
        order = jnp.argsort(flat_e)
        se = flat_e[order]
        counts = jnp.bincount(flat_e, length=E)
        starts = jnp.cumsum(counts) - counts
        pos = jnp.arange(T * K) - starts[se]
        tok = order // K
        xb = jnp.zeros((E, CAP, D), xf.dtype).at[se, pos].set(xf[tok], mode='drop')
        h = jax.nn.silu(jnp.einsum('ecd,eid->eci', xb, w1)) * jnp.einsum('ecd,eid->eci', xb, w3)
        yb = jnp.einsum('eci,edi->ecd', h, w2)
        valid = (pos < CAP).astype(xf.dtype)
        contrib = yb[se, jnp.minimum(pos, CAP - 1)]
        wf = weights.reshape(-1)[order] * valid
        y = jnp.zeros_like(xf).at[tok].add(contrib * wf[:, None])
        z = jax.nn.silu(xf @ ws1.T) * (xf @ ws3.T) @ ws2.T
        return (y + z).reshape(shape)
    x = x + _L0_attn_ref(_layernorm(x, axis=-1), L0_attn_ln_w, L0_attn_ln_b, L0_attn_in_proj_w, L0_attn_conv_w, L0_attn_conv_b, L0_attn_dt_bias, L0_attn_A_log, L0_attn_D_skip, L0_attn_norm_w, L0_attn_out_proj_w)
    x = x + _L0_xattn_ref(_layernorm(x, axis=-1), ctx_1024)
    x = x + _L0_ffn_ref(_layernorm(x, axis=-1), L0_ffn_gate_w, L0_ffn_gate_b, L0_ffn_w1, L0_ffn_w2, L0_ffn_w3, L0_ffn_ws1, L0_ffn_ws2, L0_ffn_ws3)
    return x

_drawn_inputs = setup_inputs


def setup_inputs(seed=0):
    import zlib

    import numpy as np

    out = dict(_drawn_inputs(seed))
    spreads = {'L0_attn_ln_w': (1.0, 0.2),
     'L0_attn_ln_b': (0.0, 0.1),
     'L0_attn_conv_b': (0.0, 0.1),
     'L0_attn_D_skip': (1.0, 0.2),
     'L0_attn_norm_w': (1.0, 0.2),
     'L0_ffn_gate_b': (0.0, 0.8)}
    factors = {'L0_attn_dt_bias': 8.0,
     'L0_attn_A_log': 8.0,
     'L0_ffn_gate_w': 8.0,
     'L0_ffn_w1': 8.0,
     'L0_ffn_w2': 8.0,
     'L0_ffn_w3': 8.0,
     'L0_ffn_ws1': 7.154,
     'L0_ffn_ws2': 7.028,
     'L0_ffn_ws3': 7.008}
    for name, (base, spread) in spreads.items():
        noise = np.random.default_rng([zlib.crc32(name.encode()), seed]).standard_normal(out[name].shape)
        drawn = base * np.exp(spread * noise) if base else spread * noise
        out[name] = jnp.asarray(drawn.astype(out[name].dtype))
    for name, factor in factors.items():
        out[name] = (out[name] * factor).astype(out[name].dtype)
    return out
```

```python
from contextlib import ExitStack

import numpy as np

import concourse.bass as bass
from concourse import mybir

F32 = mybir.dt.float32
I32 = mybir.dt.int32
U32 = mybir.dt.uint32
ALU = mybir.AluOpType
ACT = mybir.ActivationFunctionType
AX = mybir.AxisListType

P = 128
TOKENS, D = 2048, 256
SEQ = 1024
KD = D // P
TILES = 4
GROUP = TILES * P
GROUPS = TOKENS // GROUP
INNER, STATE, HEADS, HEAD = 512, 64, 8, 64
CONV_DIM, TAPS = INNER + 2 * STATE, 4
CB = CONV_DIM // P
PROJ = 2 * INNER + 2 * STATE + HEADS
CTX = 77
EXPERTS, TOP, CAP, FF = 64, 6, 128, 176
FH = FF // 2
SHARED = 2 * FF
SB = [(0, 128), (128, 256), (256, SHARED)]
EPS = 1e-5
NOWHERE = 1 << 20
ATANH = [1.0 / 17, 1.0 / 15, 1.0 / 13, 1.0 / 11, 1.0 / 9, 1.0 / 7, 1.0 / 5, 1.0 / 3]

C_ID, C_LE, C_LT, C_ONE, C_IOTA, C_TOK, C_CARRY, C_PART = 0, 128, 256, 384, 512, 576, 592, 596
C_ALL = 600


def constants():
    c = np.zeros((P, C_ALL), np.float32)
    i = np.arange(P)
    c[:, C_ID:C_ID + P] = i[:, None] == i[None, :]
    c[:, C_LE:C_LE + P] = i[:, None] <= i[None, :]
    c[:, C_LT:C_LT + P] = i[:, None] < i[None, :]
    c[:, C_ONE:C_ONE + P] = 1.0
    c[:, C_IOTA:C_IOTA + EXPERTS] = np.arange(EXPERTS)[None, :]
    c[:, C_TOK:C_TOK + TOKENS // P] = i[:, None] + P * np.arange(TOKENS // P)[None, :]
    c[:, C_CARRY:C_CARRY + GROUPS] = (np.arange(GROUPS) * GROUP % SEQ != 0)[None, :]
    c[:, C_PART] = i
    return c


class Signal:

    def __init__(self, nc, ctx, name, per, unit=1):
        self.sem, self.per, self.unit, self.raised = ctx.enter_context(nc.semaphore(name)), per, unit, 0

    def by(self, instruction):
        self.raised += 1
        return instruction.then_inc(self.sem, self.unit)


class Turn:

    def __init__(self, engine, g):
        self.engine, self.g, self.seen = engine, g, {}

    def need(self, signal, k=None):
        k = signal.per if k is None else k
        if self.seen.get(signal, 0) < k:
            self.seen[signal] = k
            self.engine.wait_ge(signal.sem, self.g * (signal.per * signal.unit) + k * signal.unit)


def decoder_layer(nc, x, cst, lnwb, w_in, conv_w, conv_b, rows8, rows_d, norm_w, w_out, ctx_in, ctx_t,
                  gate_t, gate_b, w13, w2, ws1, ws3, ws2, out):
    xf_dram = nc.dram_tensor("xf_scratch", (TOKENS, D), F32, kind="Internal").ap()
    slots = nc.dram_tensor("slot_table", ((EXPERTS + 1) * CAP, 2), I32, kind="Internal").ap()
    x_v = x.rearrange("(g t p) d -> g p t d", p=P, t=TILES)
    xf_v = xf_dram.rearrange("(g t p) d -> g p t d", p=P, t=TILES)
    out_v = out.rearrange("(g t p) d -> g p t d", p=P, t=TILES)
    slots_v = slots.rearrange("(e c) w -> e c w", c=CAP)

    with ExitStack() as ctx:
        def sb(name, shape, dt=F32):
            return ctx.enter_context(nc.sbuf_tensor(name, shape, dt))

        def signal(name, per, unit=1):
            return Signal(nc, ctx, name, per, unit)

        bank = [ctx.enter_context(nc.psum_tensor(f"bank{i}", [P, 512], F32)) for i in range(8)]
        A, B, C, DD = bank[0:2], bank[2:4], bank[4:6], bank[6:8]

        cs = sb("cs", [P, C_ALL])
        ident, le, lt, ones = (cs[:, c:c + P] for c in (C_ID, C_LE, C_LT, C_ONE))
        iota = cs[:, C_IOTA:C_IOTA + EXPERTS]
        lnwb_s = sb("lnwb_s", [P, 2, KD])
        w_in_s = sb("w_in_s", [P, KD, PROJ])
        conv_w_s = sb("conv_w_s", [P, CB, TAPS])
        conv_b_s = sb("conv_b_s", [P, CB])
        rows8_s = sb("rows8_s", [P, 2, HEADS])
        neg_a = sb("neg_a", [P, HEADS])
        rows_d_s = sb("rows_d_s", [P, INNER])
        norm_w_s = sb("norm_w_s", [P, INNER // P])
        w_out_raw = sb("w_out_raw", [P, INNER // P, D])
        w_out_s = w_out_raw
        gate_s = sb("gate_s", [P, KD, EXPERTS])
        gate_b_s = sb("gate_b_s", [P, EXPERTS])
        ws1_s = sb("ws1_s", [P, KD, SHARED])
        ws3_s = sb("ws3_s", [P, KD, SHARED])
        ws2_s = sb("ws2_s", [P, len(SB), D])
        minus_half = sb("minus_half", [P, TILES])
        blank = sb("blank", [P, (EXPERTS + 1) * 2], I32)

        x_s = sb("x_s", [P, TILES, D])
        y1 = sb("y1", [P, TILES, D])
        res = sb("res", [P, TILES, D])
        xh = sb("xh", [P, TILES, D])
        stats = sb("stats", [P, TILES, 6])
        mv = sb("mv", [P, 4, TILES, 2])
        var_eps = sb("var_eps", [P, 5, TILES])
        rstd = sb("rstd", [P, 5, TILES])
        xnt = sb("xnt", [P, KD, GROUP])
        zs = sb("zs", [P, TILES, INNER])
        raw = sb("raw", [P, CB, GROUP + TAPS - 1])
        conv = sb("conv", [P, CB, GROUP])
        act_c = conv
        c_t = sb("c_t", [STATE, GROUP])
        dt_v = sb("dt_v", [P, TILES * HEADS])
        dt_abs = sb("dt_abs", [P, TILES * HEADS])
        dt_u = sb("dt_u", [P, TILES * HEADS])
        dt_den = sb("dt_den", [P, TILES * HEADS])
        dt_s = sb("dt_s", [P, TILES * HEADS])
        dt_q = sb("dt_q", [P, TILES * HEADS])
        dt_p = sb("dt_p", [P, TILES * HEADS])
        dt_relu = sb("dt_relu", [P, TILES * HEADS])
        dt = sb("dt", [P, TILES, HEADS])
        a_s = sb("a_s", [P, TILES, HEADS])
        cum = sb("cum", [P, TILES, HEADS])
        to_end = sb("to_end", [P, TILES, HEADS])
        e_cum = sb("e_cum", [P, TILES, HEADS])
        e_end = sb("e_end", [P, TILES, HEADS])
        e_tot = sb("e_tot", [P, TILES, HEADS])
        xs = sb("xs", [P, TILES, INNER])
        b_tok = sb("b_tok", [P, TILES, STATE])
        xdt = sb("xdt", [P, TILES, INNER])
        xdec = sb("xdec", [P, TILES, INNER])
        gm = sb("gm", [P, TILES, P])
        m_s = sb("m_s", [P, TILES, HEADS, P])
        state = sb("state", [STATE, TILES + 1, INNER])
        y_off = sb("y_off", [P, TILES, INNER])
        yg = y_off
        square = sb("square", [P, INNER])
        sumsq = sb("sumsq", [P, TILES])
        yg_t = sb("yg_t", [P, 2, INNER // P, P])
        x1 = sb("x1", [P, TILES, D])
        xl = sb("xl", [P, TILES, D])
        xl_t = sb("xl_t", [P, 2, KD, P])
        ctx_s = sb("ctx_s", [CTX, D])
        ctx_t_s = sb("ctx_t_s", [P, KD, CTX])
        neg_max = sb("neg_max", [P, 2, TILES])
        exp_sum = sb("exp_sum", [P, 2, TILES])
        inv_sum = sb("inv_sum", [P, 2, TILES])
        probs = sb("probs", [P, TILES, CTX])
        probs_t = sb("probs_t", [CTX, TILES, P])
        x2 = sb("x2", [P, TILES, D])
        xf = sb("xf", [P, TILES, D])
        xf_t = sb("xf_t", [P, KD, GROUP])
        scores = sb("scores", [P, TILES, EXPERTS])
        biased = sb("biased", [P, TILES, EXPERTS])
        top8 = sb("top8", [P, TILES, 8])
        top_i = sb("top_i", [P, TILES, 8], U32)
        top_f = sb("top_f", [P, TILES, TOP])
        wide = m_s[:].rearrange("p t h l -> p (t h l)")[:, 0:8 * TOP * EXPERTS].rearrange(
            "p (n k e) -> p n k e", n=8, k=TOP)
        hot, picked, placed = wide[:, 0:TILES], wide[:, 4:6], wide[:, 6:8]
        chosen = sb("chosen", [P, TILES, EXPERTS])
        counts = sb("counts", [P, TILES + 1, EXPERTS])
        place = sb("place", [P, TILES, TOP])
        over = sb("over", [P, TILES, TOP])
        base = sb("base", [P, TILES, TOP])
        slot_f = sb("slot_f", [P, TILES, TOP])
        slot_i = sb("slot_i", [P, TILES, TOP], I32)
        pay = sb("pay", [P, TILES, TOP, 2], I32)
        hs = hm = conv
        o_s = xl

        e_num = sb("e_num", [EXPERTS, 4])
        e_hot = sb("e_hot", [EXPERTS, EXPERTS])
        e_list = sb("e_list", [1, 2 * EXPERTS + 1])
        e_list_i = sb("e_list_i", [1, 2 * EXPERTS + 1], I32)
        tab = sb("tab", [P, 2, 2], I32)
        xb = sb("xb", [P, 2, D])
        xb_t = sb("xb_t", [P, 2, KD, P])
        w13_s = sb("w13_s", [P, 2, KD, 2 * FF])
        w2_s = sb("w2_s", [FH, 2, 2, D])
        h1 = sb("h1", [FH, 2, 2 * P])
        hx = sb("hx", [FH, 2, 2, P])
        yo = sb("yo", [P, 2, D])

        s_const = signal("s_const", 1, 16)
        s_weights = signal("s_weights", 10, 16)
        s_shared = signal("s_shared", 8, 16)
        s_blank = signal("s_blank", 1)
        s_table = signal("s_table", 1, 16)
        s_zero = signal("s_zero", 5)
        s_exp_a = signal("s_exp_a", 1)
        s_neg_a = signal("s_neg_a", 1)
        s_wout = signal("s_wout", INNER // P)
        s_half = signal("s_half", 2)

        x_in = signal("x_in", 1, 16)
        ctx_loaded = signal("ctx_loaded", 2, 16)
        s_stats = signal("s_stats", 4 * TILES)
        s_mv = signal("s_mv", 4 * TILES)
        s_var = signal("s_var", 5)
        s_rstd = signal("s_rstd", 5)
        s_y1 = signal("s_y1", TILES)
        s_res = signal("s_res", 1)
        s_xh = signal("s_xh", TILES)
        t_xh = signal("t_xh", TILES)
        s_xnt = signal("s_xnt", TILES)
        m_z = signal("m_z", TILES)
        s_z = signal("s_z", TILES)
        m_dt = signal("m_dt", 1)
        m_x = signal("m_x", CB)
        s_halo = signal("s_halo", 1)
        s_raw = signal("s_raw", CB)
        s_tap = signal("s_tap", CB * TAPS)
        s_conv = signal("s_conv", CB)
        c_moved = signal("c_moved", 1, 16)
        s_dtv = signal("s_dtv", 3)
        s_u = signal("s_u", 1)
        s_sq = signal("s_sq", 4)
        s_poly = signal("s_poly", len(ATANH) + 1)
        s_dt = signal("s_dt", 2)
        m_cum = signal("m_cum", 2)
        s_ncum = signal("s_ncum", 2)
        s_ecum = signal("s_ecum", 3)
        t_x = signal("t_x", TILES)
        t_b = signal("t_b", 1)
        s_xs = signal("s_xs", TILES)
        s_btok = signal("s_btok", 1)
        s_xdt = signal("s_xdt", TILES)
        s_xd = signal("s_xd", TILES)
        s_xdec = signal("s_xdec", TILES)
        m_g = signal("m_g", 1)
        s_gm = signal("s_gm", 1)
        m_rows = signal("m_rows", 2 * TILES)
        s_drop = signal("s_drop", 2 * TILES)
        s_decay = signal("s_decay", 2 * TILES)
        s_m = signal("s_m", TILES)
        m_y = signal("m_y", TILES)
        m_off = signal("m_off", TILES)
        m_state = signal("m_state", TILES)
        s_sdec = signal("s_sdec", TILES)
        s_state = signal("s_state", TILES + 1)
        s_yoff = signal("s_yoff", TILES)
        s_skip = signal("s_skip", TILES)
        s_ysum = signal("s_ysum", TILES)
        s_yg = signal("s_yg", TILES)
        s_sumsq = signal("s_sumsq", TILES)
        t_yg = signal("t_yg", TILES)
        s_ygt = signal("s_ygt", TILES)
        m_out = signal("m_out", TILES)
        s_x1 = signal("s_x1", TILES)
        s_xl = signal("s_xl", TILES)
        t_xl = signal("t_xl", TILES)
        s_xlt = signal("s_xlt", TILES)
        m_sc = signal("m_sc", TILES)
        s_max = signal("s_max", 2 * TILES)
        s_probs = signal("s_probs", TILES)
        s_inv = signal("s_inv", 2 * TILES)
        t_pr = signal("t_pr", TILES)
        s_prt = signal("s_prt", TILES)
        m_att = signal("m_att", TILES)
        s_x2 = signal("s_x2", TILES)
        s_xf = signal("s_xf", TILES)
        xf_out = signal("xf_out", 1, 16)
        t_xf = signal("t_xf", TILES)
        s_xft = signal("s_xft", TILES)
        m_lg = signal("m_lg", TILES)
        s_elg = signal("s_elg", TILES)
        s_scores = signal("s_scores", TILES)
        s_biased = signal("s_biased", TILES)
        s_top = signal("s_top", 3 * TILES)
        s_hot = signal("s_hot", TILES)
        s_chosen = signal("s_chosen", TILES)
        s_counts = signal("s_counts", TILES + 1)
        s_picked = signal("s_picked", TILES)
        s_pay = signal("s_pay", 2 * TILES)
        m_rank = signal("m_rank", TILES)
        s_placed = signal("s_placed", TILES)
        s_place = signal("s_place", TILES)
        s_over = signal("s_over", 3 * TILES)
        s_slot = signal("s_slot", TILES)
        sent = signal("sent", TOP * TILES, 16)
        m_s1 = signal("m_s1", len(SB))
        m_s3 = signal("m_s3", len(SB))
        s_hs = signal("s_hs", len(SB))
        s_hm = signal("s_hm", len(SB))
        m_sh = signal("m_sh", TILES)
        s_o = signal("s_o", TILES)
        o_out = signal("o_out", 1, 16)

        m_cnt = signal("m_cnt", 3)
        s_elist = signal("s_elist", 7)
        tab_in = [signal(f"tab_in{q}", 1, 16) for q in range(2)]
        w13_in = [signal(f"w13_in{q}", 1, 16) for q in range(2)]
        w2_in = [signal(f"w2_in{q}", 1, 16) for q in range(2)]
        xb_in = [signal(f"xb_in{q}", 1, 16) for q in range(2)]
        t_xb = signal("t_xb", 2)
        s_xbt = signal("s_xbt", 2)
        m_h = signal("m_h", 2)
        s_h1 = signal("s_h1", 2)
        s_hx = signal("s_hx", 2)
        m_yo = signal("m_yo", 2)
        s_yo = signal("s_yo", 2)
        added = signal("added", 2, 16)
        wait_done = signal("wait_done", 9)

        block = ctx.enter_context(nc.Block())
        PAIRS = EXPERTS // 2

        def heads(ap):
            return ap.unsqueeze(2).to_broadcast([ap.shape[0], HEADS, HEAD])

        def per_head(ap):
            return ap.rearrange("p (h c) -> p h c", h=HEADS)

        def group_end(turn):
            for s in (s_o, s_hs, m_sh, sent, o_out, xf_out, x_in_next):
                turn.need(s)

        x_in_next = s_res

        @block.sync
        def _(sp):
            s_const.by(sp.dma_start(cs[:], cst))
            s_weights.by(sp.dma_start(lnwb_s[:], lnwb))
            s_weights.by(sp.dma_start(w_in_s[:], w_in))
            for dst, src in ((conv_w_s, conv_w), (conv_b_s, conv_b), (rows8_s, rows8), (rows_d_s, rows_d),
                             (norm_w_s, norm_w), (w_out_raw, w_out), (gate_s, gate_t), (gate_b_s, gate_b)):
                s_weights.by(sp.dma_start(dst[:], src))
            s_shared.by(sp.dma_start(ws1_s[:], ws1))
            s_shared.by(sp.dma_start(ws3_s[:], ws3))
            for n, (lo, hi) in enumerate(SB):
                s_shared.by(sp.dma_start(ws2_s[0:hi - lo, n, :], ws2[lo:hi, :]))
            sp.wait_ge(s_blank.sem, 1)
            s_table.by(sp.dma_start(slots.rearrange("(p n) w -> p (n w)", p=P), blank[:]))
            for g in range(GROUPS):
                turn = Turn(sp, g)
                x_in.by(sp.dma_start(x_s[:], x_v[bass.ds(g, 1)].rearrange("o p t d -> (o p) t d")))
                ctx_loaded.by(sp.dma_start(ctx_s[:], ctx_in[bass.ds(g, 1)].rearrange("o v d -> (o v) d")))
                ctx_loaded.by(sp.dma_start(ctx_t_s[:], ctx_t[bass.ds(g, 1)].rearrange("o p k v -> (o p) k v")))
                turn.need(s_conv)
                c_moved.by(sp.dma_start(c_t[:], act_c[STATE:P, CB - 1, :]))
                turn.need(s_xf)
                xf_out.by(sp.dma_start(xf_v[bass.ds(g, 1)].rearrange("o p t d -> (o p) t d"), xf[:]))
                turn.need(s_o)
                o_out.by(sp.dma_start(out_v[bass.ds(g, 1)].rearrange("o p t d -> (o p) t d"), o_s[:]))
                group_end(turn)
            sp.wait_ge(s_elist.sem, 7)
            n_active = sp.value_load(e_list_i[0:1, 2 * EXPERTS:2 * EXPERTS + 1], min_val=0, max_val=EXPERTS)
            with sp.Fori(0, PAIRS) as i:
                with sp.If(i * 2 < n_active):
                    turn = Turn(sp, i)
                    for q in range(2):
                        e_w = sp.value_load(e_list_i[0:1, bass.ds(i * 2 + q, 1)], min_val=0, max_val=EXPERTS - 1)
                        e_t = sp.value_load(e_list_i[0:1, bass.ds(i * 2 + (q + EXPERTS), 1)], min_val=0, max_val=EXPERTS)
                        tab_in[q].by(sp.dma_start(tab[:, q, :], slots_v[bass.ds(e_t, 1)].rearrange("o c w -> (o c) w")))
                        w13_in[q].by(sp.dma_start(w13_s[:, q], w13[bass.ds(e_w, 1)].rearrange("o p k f -> (o p) k f")))
                        w2_in[q].by(sp.dma_start(w2_s[:, q], w2[bass.ds(e_w, 1)].rearrange("o (c f) d -> (o f) c d", f=FH)))
                    turn.need(added)
                    sp.sem_inc(wait_done.sem, 1)
                with sp.Else():
                    sp.nop()

        @block.gpsimd
        def _(pool):
            s_blank.by(pool.memset(blank[:], NOWHERE))
            s_half.by(pool.memset(minus_half[:], -0.5))
            s_half.by(pool.memset(xb[:], 0.0))
            pool.wait_ge(s_half.sem, 2)
            pool.wait_ge(s_weights.sem, s_weights.per * 16)
            pool.wait_ge(s_table.sem, 16)

            for g in range(GROUPS):
                turn = Turn(pool, g)

                def inverse_root(n, src, scale, *after):
                    turn.need(*after)
                    s_var.by(pool.tensor_scalar(var_eps[:, n, :], src, scale, EPS, ALU.mult, ALU.add))
                    turn.need(s_var, n + 1)
                    s_rstd.by(pool.tensor_tensor(rstd[:, n, :], var_eps[:, n, :], minus_half[:], ALU.pow))

                inverse_root(0, mv[:, 0, :, 1], 1.0, s_mv, TILES)
                inverse_root(1, mv[:, 1, :, 1], 1.0, s_mv, 2 * TILES)
                turn.need(s_y1)
                s_res.by(pool.tensor_tensor(res[:], x_s[:], y1[:], ALU.add))

                def skip(t):
                    turn.need(s_xd, t + 1)
                    turn.need(s_yoff, t + 1)
                    s_skip.by(pool.tensor_tensor(y_off[:, t, :], y_off[:, t, :], xs[:, t, :], ALU.add))

                turn.need(s_ecum)
                for t in range(TILES):
                    turn.need(s_xdt, t + 1)
                    s_xdec.by(pool.tensor_tensor(per_head(xdec[:, t, :]), per_head(xdt[:, t, :]),
                                                 heads(e_end[:, t, :]), ALU.mult))
                    turn.need(s_state, t + 1)
                    s_sdec.by(pool.tensor_tensor(per_head(state[:, t + 1, :]), per_head(state[:, t, :]),
                                                 heads(e_tot[0:STATE, t, :]), ALU.mult))
                    turn.need(s_xs, t + 1)
                    turn.need(s_xdt, t + 1)
                    s_xd.by(pool.tensor_tensor(xs[:, t, :], xs[:, t, :], rows_d_s[:], ALU.mult))
                    if t:
                        skip(t - 1)
                skip(TILES - 1)
                inverse_root(2, sumsq[:], 1.0 / INNER, s_sumsq)
                inverse_root(3, mv[:, 2, :, 1], 1.0, s_mv, 3 * TILES)
                inverse_root(4, mv[:, 3, :, 1], 1.0, s_mv, 4 * TILES)
                for t in range(TILES):
                    turn.need(s_pay, 2 * t + 2)
                    turn.need(s_slot, t + 1)
                    for k in range(TOP):
                        sent.by(pool.indirect_dma_start(
                            out=slots, out_offset=bass.IndirectOffsetOnAxis(ap=slot_i[:, t, k:k + 1], axis=0),
                            in_=pay[:, t, k, :], in_offset=None,
                            bounds_check=EXPERTS * CAP - 1, oob_is_err=False))
                group_end(turn)

            pool.wait_ge(s_elist.sem, 7)
            n_active = pool.value_load(e_list_i[0:1, 2 * EXPERTS:2 * EXPERTS + 1], min_val=0, max_val=EXPERTS)
            with pool.Fori(0, PAIRS) as i:
                with pool.If(i * 2 < n_active):
                    turn = Turn(pool, i)
                    for q in range(2):
                        turn.need(tab_in[q])
                        pool.sem_inc(wait_done.sem, 1)
                        xb_in[q].by(pool.indirect_dma_start(
                            out=xb[:, q, :], out_offset=None, in_=xf_dram,
                            in_offset=bass.IndirectOffsetOnAxis(ap=tab[:, q, 0:1], axis=0),
                            bounds_check=TOKENS - 1, oob_is_err=False))
                    for q in range(2):
                        turn.need(s_yo, q + 1)
                        if q:
                            turn.need(added, q)
                        pool.sem_inc(wait_done.sem, 1)
                        added.by(pool.indirect_dma_start(
                            out=out, out_offset=bass.IndirectOffsetOnAxis(ap=tab[:, q, 0:1], axis=0),
                            in_=yo[:, q, :], in_offset=None, bounds_check=TOKENS - 1, oob_is_err=ACC_OOB,
                            compute_op=ALU.add))
                    turn.need(added)
                    pool.sem_inc(wait_done.sem, 1)
                with pool.Else():
                    pool.nop()

        @block.scalar
        def _(act):
            act.wait_ge(s_weights.sem, s_weights.per * 16)
            s_exp_a.by(act.activation(neg_a[:], rows8_s[:, 1, :], ACT.Exp))
            for g in range(GROUPS):
                turn = Turn(act, g)
                for t in range(TILES):
                    turn.need(t_xh, t + 1)
                    for k in range(KD):
                        ins = act.activation(xnt[:, k, t * P:(t + 1) * P], A[t % 2][:, k * P:(k + 1) * P],
                                             ACT.Identity, scale=lnwb_s[:, 0, k:k + 1], bias=lnwb_s[:, 1, k:k + 1])
                    s_xnt.by(ins)
                for t in range(TILES):
                    turn.need(m_z, t + 1)
                    s_z.by(act.activation(zs[:, t, :], B[t % 2][:], ACT.Silu))
                turn.need(s_halo)
                for c in range(CB):
                    turn.need(m_x, c + 1)
                    s_raw.by(act.activation(raw[:, c, TAPS - 1:], DD[c % 2][:], ACT.Copy))
                for c in range(CB):
                    turn.need(s_tap, TAPS * (c + 1))
                    s_conv.by(act.activation(act_c[:, c, :], conv[:, c, :], ACT.Silu, bias=conv_b_s[:, c:c + 1]))
                turn.need(s_dtv, 2)
                s_u.by(act.activation(dt_u[:], dt_abs[:], ACT.Exp, scale=-1.0))
                for t in range(TILES):
                    turn.need(t_x, t + 1)
                    s_xs.by(act.activation(xs[:, t, :], A[t % 2][:], ACT.Copy))
                turn.need(t_b)
                s_btok.by(act.activation(b_tok[:].rearrange("p t n -> p (t n)"), C[0][:, 0:TILES * STATE], ACT.Copy))
                turn.need(s_ncum, 2)
                s_ecum.by(act.activation(e_cum[:].rearrange("p t h -> p (t h)"), cum[:].rearrange("p t h -> p (t h)"),
                                         ACT.Exp))
                s_ecum.by(act.activation(e_end[:].rearrange("p t h -> p (t h)"), to_end[:].rearrange("p t h -> p (t h)"),
                                         ACT.Exp))
                s_ecum.by(act.activation(e_tot[:].rearrange("p t h -> p (t h)"), C[1][:, 32:64], ACT.Exp))
                for t in range(TILES):
                    for half in range(2):
                        turn.need(m_rows, 2 * t + half + 1)
                        for j in range(HEADS // 2):
                            h = half * (HEADS // 2) + j
                            ins = act.activation(m_s[:, t, h, :], DD[half][:, j * P:(j + 1) * P], ACT.Relu,
                                                 scale=-1.0, bias=cum[:, t, h:h + 1])
                        s_drop.by(ins)
                    for half in range(2):
                        turn.need(s_drop, 2 * t + half + 1)
                        pair = m_s[:, t, half * (HEADS // 2):(half + 1) * (HEADS // 2), :]
                        s_decay.by(act.activation(pair, pair, ACT.Exp, scale=-1.0))
                for t in range(TILES):
                    turn.need(s_yg, t + 1)
                    if t:
                        turn.need(s_sumsq, t)
                    s_sumsq.by(act.activation(square[:], yg[:, t, :], ACT.Square, accum_out=sumsq[:, t:t + 1]))
                    turn.need(t_yg, t + 1)
                    if t >= 2:
                        turn.need(m_out, t - 1)
                    s_ygt.by(act.activation(yg_t[:, t % 2].rearrange("p k c -> p (k c)"), DD[t % 2][:], ACT.Copy))
                def softmax(t):
                    turn.need(s_max, t + 1)
                    s_probs.by(act.activation(probs[:, t, :], C[t % 2][:, 0:CTX], ACT.Exp,
                                              bias=neg_max[:, 0, t:t + 1], accum_out=exp_sum[:, 0, t:t + 1]))

                for t in range(TILES):
                    turn.need(t_xl, t + 1)
                    if t >= 2:
                        turn.need(m_sc, t - 1)
                    s_xlt.by(act.activation(xl_t[:, t % 2].rearrange("p k c -> p (k c)"), B[t % 2][:, 0:D], ACT.Copy))
                    if t:
                        softmax(t - 1)
                softmax(TILES - 1)
                for t in range(TILES):
                    turn.need(t_pr, t + 1)
                    s_prt.by(act.activation(probs_t[:, t, :], DD[t % 2][0:CTX, 0:P], ACT.Copy))
                for t in range(TILES):
                    turn.need(t_xf, t + 1)
                    s_xft.by(act.activation(xf_t[:, :, t * P:(t + 1) * P],
                                            B[t % 2][:, 0:D].rearrange("p (k c) -> p k c", k=KD), ACT.Copy))
                for t in range(TILES):
                    turn.need(s_max, TILES + t + 1)
                    s_elg.by(act.activation(scores[:, t, :], C[t % 2][:, 0:EXPERTS], ACT.Exp,
                                            bias=neg_max[:, 1, t:t + 1], accum_out=exp_sum[:, 1, t:t + 1]))
                for n, (lo, hi) in enumerate(SB):
                    turn.need(m_s1, n + 1)
                    s_hs.by(act.activation(hs[0:hi - lo, n, :], A[n % 2][0:hi - lo, :], ACT.Silu))
                group_end(turn)

            act.wait_ge(s_elist.sem, 7)
            n_active = act.value_load(e_list_i[0:1, 2 * EXPERTS:2 * EXPERTS + 1], min_val=0, max_val=EXPERTS)
            with act.Fori(0, PAIRS) as i:
                with act.If(i * 2 < n_active):
                    turn = Turn(act, i)
                    for q in range(2):
                        turn.need(t_xb, q + 1)
                        s_xbt.by(act.activation(xb_t[:, q].rearrange("p k c -> p (k c)"), A[q][:, 0:D], ACT.Copy))
                    for q in range(2):
                        turn.need(m_h, q + 1)
                        s_h1.by(act.activation(h1[:, q, :], B[q][0:FH, 0:2 * P], ACT.Silu))
                    turn.need(added)
                    act.sem_inc(wait_done.sem, 1)
                with act.Else():
                    act.nop()

        @block.vector
        def _(dve):
            s_zero.by(dve.memset(state[:], 0.0))
            s_zero.by(dve.memset(counts[:], 0.0))
            s_zero.by(dve.memset(raw[:], 0.0))
            s_zero.by(dve.memset(e_list[:], 0.0))
            s_zero.by(dve.memset(yo[:], 0.0))
            dve.wait_ge(s_zero.sem, 5)
            dve.wait_ge(s_const.sem, 16)
            dve.wait_ge(s_weights.sem, s_weights.per * 16)
            dve.wait_ge(s_exp_a.sem, 1)
            s_neg_a.by(dve.tensor_scalar(neg_a[:], neg_a[:], -1.0, None, ALU.mult))
            for k in range(INNER // P):
                s_wout.by(dve.tensor_scalar(w_out_s[:, k, :], w_out_raw[:, k, :], norm_w_s[:, k:k + 1], None, ALU.mult))
            dve.wait_ge(s_neg_a.sem, 1)

            for g in range(GROUPS):
                turn = Turn(dve, g)

                def norm(n, src, dst, done, ready):
                    for t in range(TILES):
                        ready(t)
                        s_stats.by(dve.bn_stats(stats[:, t, :], src[:, t, :]))
                    for t in range(TILES):
                        turn.need(s_stats, n * TILES + t + 1)
                        s_mv.by(dve.bn_aggr(mv[:, n, t, :], stats[:, t, :]))
                    turn.need(s_mv, (n + 1) * TILES)
                    turn.need(s_rstd, {0: 1, 1: 2, 2: 4, 3: 5}[n])
                    r = rstd[:, {0: 0, 1: 1, 2: 3, 3: 4}[n], :]
                    for t in range(TILES):
                        done.by(dve.tensor_scalar(dst[:, t, :], src[:, t, :], mv[:, n, t, 0:1], r[:, t:t + 1],
                                                  ALU.subtract, ALU.mult))

                carry = cs[:, bass.ds(g + C_CARRY, 1)]
                s_state.by(dve.tensor_scalar(state[:, 0, :], state[:, TILES, :], carry[0:STATE], None, ALU.mult))
                s_counts.by(dve.tensor_copy(counts[:, 0, :], counts[:, TILES, :]))
                s_halo.by(dve.tensor_scalar(raw[:, :, 0:TAPS - 1], raw[:, :, GROUP:], carry, None, ALU.mult))

                norm(0, x_s, y1, s_y1, lambda t: turn.need(x_in))
                norm(1, y1, xh, s_xh, lambda t: turn.need(s_y1, t + 1))

                turn.need(m_dt)
                s_dtv.by(dve.tensor_tensor(dt_v[:].rearrange("p (t h) -> p t h", h=HEADS),
                                           C[0][:, 0:TILES * HEADS].rearrange("p (t h) -> p t h", h=HEADS),
                                           rows8_s[:, 0, :].unsqueeze(1).to_broadcast([P, TILES, HEADS]), ALU.add))
                turn.need(s_dtv, 1)
                s_dtv.by(dve.scalar_tensor_tensor(out=dt_abs[:], in0=dt_v[:], scalar=-1.0, in1=dt_v[:],
                                                  op0=ALU.mult, op1=ALU.max))
                s_dtv.by(dve.tensor_scalar(dt_relu[:], dt_v[:], 0.0, None, ALU.max))

                for c in range(CB):
                    turn.need(s_raw, c + 1)
                    s_tap.by(dve.tensor_scalar(conv[:, c, :], raw[:, c, TAPS - 1:], conv_w_s[:, c, TAPS - 1:TAPS],
                                               None, ALU.mult))
                    for j in range(TAPS - 1):
                        turn.need(s_tap, TAPS * c + j + 1)
                        s_tap.by(dve.scalar_tensor_tensor(out=conv[:, c, :], in0=raw[:, c, j:j + GROUP],
                                                          scalar=conv_w_s[:, c, j:j + 1], in1=conv[:, c, :],
                                                          op0=ALU.mult, op1=ALU.add))
                turn.need(s_u)
                s_sq.by(dve.tensor_scalar(dt_den[:], dt_u[:], 2.0, None, ALU.add))
                turn.need(s_sq, 1)
                s_sq.by(dve.reciprocal(dt_den[:], dt_den[:]))
                turn.need(s_sq, 2)
                s_sq.by(dve.tensor_tensor(dt_s[:], dt_u[:], dt_den[:], ALU.mult))
                turn.need(s_sq, 3)
                s_sq.by(dve.tensor_tensor(dt_q[:], dt_s[:], dt_s[:], ALU.mult))
                turn.need(s_sq)
                s_poly.by(dve.tensor_scalar(dt_p[:], dt_q[:], ATANH[0], None, ALU.mult))
                for n, c in enumerate(ATANH[1:]):
                    turn.need(s_poly, n + 1)
                    s_poly.by(dve.scalar_tensor_tensor(out=dt_p[:], in0=dt_p[:], scalar=c, in1=dt_q[:],
                                                        op0=ALU.add, op1=ALU.mult))
                turn.need(s_poly, len(ATANH))
                s_poly.by(dve.scalar_tensor_tensor(out=dt_p[:], in0=dt_p[:], scalar=1.0, in1=dt_s[:],
                                                    op0=ALU.add, op1=ALU.mult))
                turn.need(s_poly)
                turn.need(s_dtv, 3)
                s_dt.by(dve.scalar_tensor_tensor(out=dt[:].rearrange("p t h -> p (t h)"), in0=dt_p[:], scalar=2.0,
                                                 in1=dt_relu[:], op0=ALU.mult, op1=ALU.add))
                turn.need(s_dt, 1)
                s_dt.by(dve.tensor_tensor(a_s[:], dt[:], neg_a[:].unsqueeze(1).to_broadcast([P, TILES, HEADS]),
                                          ALU.mult))
                for t in range(TILES):
                    turn.need(t_x, t + 1)
                    turn.need(s_xs, t + 1)
                    s_xdt.by(dve.tensor_tensor(per_head(xdt[:, t, :]), per_head(xs[:, t, :]), heads(dt[:, t, :]),
                                               ALU.mult))
                turn.need(m_cum, 2)
                flat = "p t h -> p (t h)"
                s_ncum.by(dve.tensor_scalar(cum[:].rearrange(flat), C[1][:, 0:32], 1.0, None, ALU.mult))
                turn.need(s_ncum, 1)
                s_ncum.by(dve.tensor_tensor(to_end[:].rearrange(flat), C[1][:, 32:64], cum[:].rearrange(flat),
                                            ALU.subtract))
                turn.need(m_g)
                s_gm.by(dve.tensor_tensor(gm[:], C[0][:].rearrange("p (t l) -> p t l", t=TILES),
                                          le.unsqueeze(1).to_broadcast([P, TILES, P]), ALU.mult))
                turn.need(s_gm)
                def gate(t):
                    turn.need(m_y, t + 1)
                    turn.need(s_skip, t + 1)
                    s_ysum.by(dve.tensor_tensor(yg[:, t, :], B[t % 2][:], y_off[:, t, :], ALU.add))
                    turn.need(s_ysum, t + 1)
                    turn.need(s_z, t + 1)
                    s_yg.by(dve.tensor_tensor(yg[:, t, :], yg[:, t, :], zs[:, t, :], ALU.mult))

                for t in range(TILES):
                    turn.need(s_decay, 2 * t + 2)
                    s_m.by(dve.tensor_tensor(m_s[:, t], m_s[:, t],
                                             gm[:, t, :].unsqueeze(1).to_broadcast([P, HEADS, P]), ALU.mult))
                    turn.need(m_state, t + 1)
                    turn.need(s_sdec, t + 1)
                    s_state.by(dve.tensor_tensor(state[:, t + 1, :], C[1][0:STATE, :], state[:, t + 1, :], ALU.add))
                    turn.need(m_off, t + 1)
                    turn.need(s_ecum)
                    s_yoff.by(dve.tensor_tensor(per_head(y_off[:, t, :]), per_head(A[t % 2][:]),
                                                heads(e_cum[:, t, :]), ALU.mult))
                    if t:
                        gate(t - 1)
                gate(TILES - 1)
                turn.need(s_rstd, 3)
                turn.need(s_res)
                for t in range(TILES):
                    turn.need(m_out, t + 1)
                    s_x1.by(dve.scalar_tensor_tensor(out=x1[:, t, :], in0=A[t % 2][:, 0:D],
                                                     scalar=rstd[:, 2, t:t + 1], in1=res[:, t, :],
                                                     op0=ALU.mult, op1=ALU.add))
                norm(2, x1, xl, s_xl, lambda t: turn.need(s_x1, t + 1))
                for t in range(TILES):
                    turn.need(m_sc, t + 1)
                    s_max.by(dve.tensor_reduce(neg_max[:, 0, t:t + 1], C[t % 2][:, 0:CTX], AX.X, ALU.max, negate=True))
                for t in range(TILES):
                    turn.need(s_probs, t + 1)
                    s_inv.by(dve.reciprocal(inv_sum[:, 0, t:t + 1], exp_sum[:, 0, t:t + 1]))
                for t in range(TILES):
                    turn.need(s_inv, t + 1)
                    turn.need(m_att, t + 1)
                    s_x2.by(dve.scalar_tensor_tensor(out=x2[:, t, :], in0=A[t % 2][:, 0:D],
                                                     scalar=inv_sum[:, 0, t:t + 1], in1=x1[:, t, :],
                                                     op0=ALU.mult, op1=ALU.add))
                norm(3, x2, xf, s_xf, lambda t: turn.need(s_x2, t + 1))
                for t in range(TILES):
                    turn.need(m_lg, t + 1)
                    s_max.by(dve.tensor_reduce(neg_max[:, 1, t:t + 1], C[t % 2][:, 0:EXPERTS], AX.X, ALU.max,
                                               negate=True))
                for t in range(TILES):
                    turn.need(s_elg, t + 1)
                    s_inv.by(dve.reciprocal(inv_sum[:, 1, t:t + 1], exp_sum[:, 1, t:t + 1]))
                for t in range(TILES):
                    turn.need(s_inv, TILES + t + 1)
                    s_scores.by(dve.tensor_scalar(scores[:, t, :], scores[:, t, :], inv_sum[:, 1, t:t + 1], None,
                                                  ALU.mult))
                for t in range(TILES):
                    turn.need(s_scores, t + 1)
                    s_biased.by(dve.tensor_tensor(biased[:, t, :], scores[:, t, :], gate_b_s[:], ALU.add))
                for t in range(TILES):
                    turn.need(s_biased, t + 1)
                    s_top.by(dve.max(top8[:, t, :], biased[:, t, :]))
                for t in range(TILES):
                    turn.need(s_top, t + 1)
                    s_top.by(dve.max_index(top_i[:, t, :], top8[:, t, :], biased[:, t, :]))
                for t in range(TILES):
                    turn.need(s_top, TILES + t + 1)
                    s_top.by(dve.tensor_copy(top_f[:, t, :], top_i[:, t, 0:TOP]))
                for t in range(TILES):
                    turn.need(s_top, 2 * TILES + t + 1)
                    s_hot.by(dve.tensor_tensor(hot[:, t], iota.unsqueeze(1).to_broadcast([P, TOP, EXPERTS]),
                                               top_f[:, t, :].unsqueeze(2).to_broadcast([P, TOP, EXPERTS]),
                                               ALU.is_equal))
                for t in range(TILES):
                    turn.need(s_hot, t + 1)
                    s_chosen.by(dve.tensor_reduce(chosen[:, t, :], hot[:, t].rearrange("p k e -> p e k"), AX.X, ALU.add))
                for t in range(TILES):
                    turn.need(s_chosen, t + 1)
                    turn.need(s_counts, t + 1)
                    s_counts.by(dve.tensor_tensor(counts[:, t + 1, :], counts[:, t, :], chosen[:, t, :], ALU.add))
                for t in range(TILES):
                    if t >= 2:
                        turn.need(s_pay, t - 1)
                    s_picked.by(dve.tensor_tensor(picked[:, t % 2], hot[:, t],
                                                  scores[:, t, :].unsqueeze(1).to_broadcast([P, TOP, EXPERTS]),
                                                  ALU.mult))
                    turn.need(s_picked, t + 1)
                    s_pay.by(dve.tensor_reduce(pay[:, t, :, 1].bitcast(F32), picked[:, t % 2], AX.X, ALU.add))
                for t in range(TILES):
                    s_pay.by(dve.tensor_copy(pay[:, t, :, 0],
                                             cs[:, bass.ds(g * TILES + (C_TOK + t), 1)].to_broadcast([P, TOP])))
                for n, (lo, hi) in enumerate(SB):
                    turn.need(m_s3, n + 1)
                    turn.need(s_hs, n + 1)
                    s_hm.by(dve.tensor_tensor(hm[0:hi - lo, n, :], B[n % 2][0:hi - lo, :], hs[0:hi - lo, n, :],
                                              ALU.mult))
                for t in range(TILES):
                    turn.need(m_rank, t + 1)
                    if t >= 2:
                        turn.need(s_place, t - 1)
                    s_placed.by(dve.tensor_tensor(placed[:, t % 2], hot[:, t],
                                                  C[t % 2][:, 256:256 + EXPERTS].unsqueeze(1)
                                                  .to_broadcast([P, TOP, EXPERTS]), ALU.mult))
                    turn.need(s_placed, t + 1)
                    s_place.by(dve.tensor_reduce(place[:, t, :], placed[:, t % 2], AX.X, ALU.add))
                for t in range(TILES):
                    turn.need(s_place, t + 1)
                    s_over.by(dve.tensor_scalar(over[:, t, :], place[:, t, :], float(CAP), float(NOWHERE),
                                                ALU.is_ge, ALU.mult))
                    s_over.by(dve.scalar_tensor_tensor(out=base[:, t, :], in0=top_f[:, t, :], scalar=float(CAP),
                                                       in1=place[:, t, :], op0=ALU.mult, op1=ALU.add))
                for t in range(TILES):
                    turn.need(s_over, 2 * t + 2)
                    s_over.by(dve.tensor_tensor(slot_f[:, t, :], base[:, t, :], over[:, t, :], ALU.add))
                for t in range(TILES):
                    turn.need(s_over, 2 * TILES + t + 1)
                    s_slot.by(dve.tensor_copy(slot_i[:, t, :], slot_f[:, t, :]))
                for t in range(TILES):
                    turn.need(m_sh, t + 1)
                    s_o.by(dve.tensor_tensor(o_s[:, t, :], DD[t % 2][:, 0:D], x2[:, t, :], ALU.add))
                group_end(turn)

            n_tok, active, e_rank = e_num[:, 0:1], e_num[:, 1:2], e_num[:, 2:3]
            dve.wait_ge(m_cnt.sem, 1)
            s_elist.by(dve.tensor_scalar(active, A[0][0:EXPERTS, 0:1], 1.0, None, ALU.min))
            dve.wait_ge(m_cnt.sem, 2)
            s_elist.by(dve.tensor_copy(e_rank, A[1][0:EXPERTS, 0:1]))
            dve.wait_ge(s_elist.sem, 2)
            s_elist.by(dve.tensor_scalar(e_hot[:], cs[0:EXPERTS, C_IOTA:C_IOTA + EXPERTS], e_rank, active,
                                         ALU.is_equal, ALU.mult))
            dve.wait_ge(m_cnt.sem, 3)
            s_elist.by(dve.tensor_copy(e_list[:, 0:EXPERTS], B[0][0:1, 0:EXPERTS]))
            s_elist.by(dve.tensor_scalar(e_list[:, EXPERTS:2 * EXPERTS], iota[0:1, :], B[0][0:1, 64 + 64:64 + 65],
                                         float(EXPERTS), ALU.is_ge, ALU.mult))
            dve.wait_ge(s_elist.sem, 5)
            s_elist.by(dve.tensor_tensor(e_list[:, EXPERTS:2 * EXPERTS], e_list[:, EXPERTS:2 * EXPERTS],
                                         e_list[:, 0:EXPERTS], ALU.add))
            dve.wait_ge(s_elist.sem, 6)
            dve.tensor_copy(e_list_i[:, 2 * EXPERTS:2 * EXPERTS + 1], B[0][0:1, 64 + 64:64 + 65])
            s_elist.by(dve.tensor_copy(e_list_i[:, 0:2 * EXPERTS], e_list[:, 0:2 * EXPERTS]))

            dve.wait_ge(s_elist.sem, 7)
            n_active = dve.value_load(e_list_i[0:1, 2 * EXPERTS:2 * EXPERTS + 1], min_val=0, max_val=EXPERTS)
            with dve.Fori(0, PAIRS) as i:
                with dve.If(i * 2 < n_active):
                    turn = Turn(dve, i)
                    for q in range(2):
                        turn.need(s_h1, q + 1)
                        s_hx.by(dve.tensor_tensor(hx[:, q].rearrange("p c t -> p (c t)"), h1[:, q, :],
                                                  B[q][0:FH, 2 * P:], ALU.mult))
                    for q in range(2):
                        turn.need(m_yo, q + 1)
                        turn.need(tab_in[q])
                        s_yo.by(dve.tensor_scalar(yo[:, q, :], C[q][:, 0:D], tab[:, q, 1:2].bitcast(F32), None,
                                                  ALU.mult))
                    turn.need(added)
                    dve.sem_inc(wait_done.sem, 1)
                with dve.Else():
                    dve.nop()

        @block.tensor
        def _(pe):
            pe.wait_ge(s_const.sem, 16)
            pe.wait_ge(s_weights.sem, s_weights.per * 16)
            pe.wait_ge(s_shared.sem, 5 * 16)
            pe.wait_ge(s_wout.sem, s_wout.per)
            for g in range(GROUPS):
                turn = Turn(pe, g)

                def blocks(src, dst, n):
                    for k in range(n):
                        ins = pe.transpose(dst[:, k * P:(k + 1) * P], src[:, k * P:(k + 1) * P], ident)
                    return ins

                for t in range(TILES):
                    turn.need(s_xh, t + 1)
                    if t >= 2:
                        turn.need(s_xnt, t - 1)
                    t_xh.by(blocks(xh[:, t, :], A[t % 2], KD))
                for t in range(TILES):
                    turn.need(s_xnt, t + 1)
                    if t >= 2:
                        turn.need(s_z, t - 1)
                    for k in range(KD):
                        ins = pe.matmul(B[t % 2][:], xnt[:, k, t * P:(t + 1) * P], w_in_s[:, k, 0:INNER],
                                        start=(k == 0), stop=(k == KD - 1))
                    m_z.by(ins)
                for t in range(TILES):
                    for k in range(KD):
                        ins = pe.matmul(C[0][:, t * HEADS:(t + 1) * HEADS], xnt[:, k, t * P:(t + 1) * P],
                                        w_in_s[:, k, PROJ - HEADS:], start=(k == 0), stop=(k == KD - 1))
                m_dt.by(ins)
                for c in range(CB):
                    if c >= 2:
                        turn.need(s_raw, c - 1)
                    for k in range(KD):
                        ins = pe.matmul(DD[c % 2][:], w_in_s[:, k, INNER + c * P:INNER + (c + 1) * P],
                                        xnt[:, k, :], start=(k == 0), stop=(k == KD - 1))
                    m_x.by(ins)
                for t in range(TILES):
                    turn.need(s_conv, CB - 1)
                    if t >= 2:
                        turn.need(s_xs, t - 1)
                    for c in range(INNER // P):
                        ins = pe.transpose(A[t % 2][:, c * P:(c + 1) * P], act_c[:, c, t * P:(t + 1) * P], ident)
                    t_x.by(ins)
                turn.need(s_conv)
                turn.need(s_dtv, 1)
                for t in range(TILES):
                    ins = pe.transpose(C[0][:, t * STATE:(t + 1) * STATE], act_c[0:STATE, CB - 1, t * P:(t + 1) * P],
                                       ident[0:STATE, 0:STATE])
                t_b.by(ins)
                turn.need(s_dt)
                a_all = a_s[:].rearrange("p t h -> p (t h)")
                m_cum.by(pe.matmul(C[1][:, 0:32], le, a_all, start=True, stop=True))
                m_cum.by(pe.matmul(C[1][:, 32:64], ones, a_all, start=True, stop=True))
                turn.need(c_moved)
                turn.need(s_btok)
                for t in range(TILES):
                    ins = pe.matmul(C[0][:, t * P:(t + 1) * P], act_c[0:STATE, CB - 1, t * P:(t + 1) * P],
                                    c_t[:, t * P:(t + 1) * P], start=True, stop=True)
                m_g.by(ins)

                def rows(t):
                    for half in range(2):
                        if t == 0:
                            turn.need(s_raw, CB)
                        else:
                            turn.need(s_drop, 2 * t - 1 + half)
                        for j in range(HEADS // 2):
                            h = half * (HEADS // 2) + j
                            ins = pe.matmul(DD[half][:, j * P:(j + 1) * P],
                                            a_s[:, t, h:h + 1].to_broadcast([P, P]), le, start=True, stop=True)
                        m_rows.by(ins)

                rows(0)
                for t in range(TILES):
                    turn.need(s_state, t + 1)
                    turn.need(s_xs)
                    if t >= 2:
                        turn.need(s_yoff, t - 1)
                    m_off.by(pe.matmul(A[t % 2][:], c_t[:, t * P:(t + 1) * P], state[:, t, :], start=True, stop=True))
                    turn.need(s_xdec, t + 1)
                    if t == 0:
                        turn.need(s_ecum)
                        turn.need(s_ncum, 2)
                    m_state.by(pe.matmul(C[1][0:STATE, :], b_tok[:, t, :], xdec[:, t, :], start=True, stop=True))
                    if t + 1 < TILES:
                        rows(t + 1)
                    turn.need(s_m, t + 1)
                    turn.need(s_xdt, t + 1)
                    turn.need(s_z)
                    if t >= 2:
                        turn.need(s_ysum, t - 1)
                    for h in range(HEADS):
                        ins = pe.matmul(B[t % 2][:, h * HEAD:(h + 1) * HEAD], m_s[:, t, h, :],
                                        xdt[:, t, h * HEAD:(h + 1) * HEAD], start=True, stop=True)
                    m_y.by(ins)

                for t in range(TILES):
                    turn.need(s_yg, t + 1)
                    turn.need(s_decay)
                    if t >= 2:
                        turn.need(s_ygt, t - 1)
                    t_yg.by(blocks(yg[:, t, :], DD[t % 2], INNER // P))
                    turn.need(s_ygt, t + 1)
                    turn.need(s_yoff)
                    if t >= 2:
                        turn.need(s_x1, t - 1)
                    for k in range(INNER // P):
                        ins = pe.matmul(A[t % 2][:, 0:D], yg_t[:, t % 2, k, :], w_out_s[:, k, :],
                                        start=(k == 0), stop=(k == INNER // P - 1))
                    m_out.by(ins)
                turn.need(ctx_loaded)
                for t in range(TILES):
                    turn.need(s_xl, t + 1)
                    turn.need(s_ysum)
                    if t >= 2:
                        turn.need(s_xlt, t - 1)
                    t_xl.by(blocks(xl[:, t, :], B[t % 2], KD))
                    turn.need(s_xlt, t + 1)
                    turn.need(s_gm)
                    turn.need(s_state)
                    if t >= 2:
                        turn.need(s_probs, t - 1)
                    for k in range(KD):
                        ins = pe.matmul(C[t % 2][:, 0:CTX], xl_t[:, t % 2, k, :], ctx_t_s[:, k, :],
                                        start=(k == 0), stop=(k == KD - 1))
                    m_sc.by(ins)
                for t in range(TILES):
                    turn.need(s_probs, t + 1)
                    turn.need(s_ygt)
                    if t >= 2:
                        turn.need(s_prt, t - 1)
                    t_pr.by(pe.transpose(DD[t % 2][0:CTX, 0:P], probs[:, t, :], ident))
                for t in range(TILES):
                    turn.need(s_prt, t + 1)
                    turn.need(s_x1)
                    if t >= 2:
                        turn.need(s_x2, t - 1)
                    m_att.by(pe.matmul(A[t % 2][:, 0:D], probs_t[:, t, :], ctx_s[:], start=True, stop=True))
                for t in range(TILES):
                    turn.need(s_xf, t + 1)
                    turn.need(s_xlt)
                    if t >= 2:
                        turn.need(s_xft, t - 1)
                    t_xf.by(blocks(xf[:, t, :], B[t % 2], KD))
                for t in range(TILES):
                    turn.need(s_xft, t + 1)
                    turn.need(s_probs)
                    if t >= 2:
                        turn.need(s_elg, t - 1)
                    for k in range(KD):
                        ins = pe.matmul(C[t % 2][:, 0:EXPERTS], xf_t[:, k, t * P:(t + 1) * P], gate_s[:, k, :],
                                        start=(k == 0), stop=(k == KD - 1))
                    m_lg.by(ins)
                for n, (lo, hi) in enumerate(SB):
                    turn.need(s_x2)
                    if n >= 2:
                        turn.need(s_hs, n - 1)
                    for k in range(KD):
                        ins = pe.matmul(A[n % 2][0:hi - lo, :], ws1_s[:, k, lo:hi], xf_t[:, k, :],
                                        start=(k == 0), stop=(k == KD - 1))
                    m_s1.by(ins)
                    if n >= 2:
                        turn.need(s_hm, n - 1)
                    for k in range(KD):
                        ins = pe.matmul(B[n % 2][0:hi - lo, :], ws3_s[:, k, lo:hi], xf_t[:, k, :],
                                        start=(k == 0), stop=(k == KD - 1))
                    m_s3.by(ins)
                for t in range(TILES):
                    turn.need(s_chosen, t + 1)
                    turn.need(s_counts, t + 1)
                    turn.need(s_elg)
                    if t >= 2:
                        turn.need(s_placed, t - 1)
                    pe.matmul(C[t % 2][:, 256:256 + EXPERTS], lt, chosen[:, t, :], start=True, stop=False)
                    m_rank.by(pe.matmul(C[t % 2][:, 256:256 + EXPERTS], ones, counts[:, t, :], start=False, stop=True))
                for t in range(TILES):
                    turn.need(s_hm)
                    turn.need(s_prt)
                    if t >= 2:
                        turn.need(s_o, t - 1)
                    for n, (lo, hi) in enumerate(SB):
                        ins = pe.matmul(DD[t % 2][:, 0:D], hm[0:hi - lo, n, t * P:(t + 1) * P],
                                        ws2_s[0:hi - lo, n, :], start=(n == 0), stop=(n == len(SB) - 1))
                    m_sh.by(ins)
                group_end(turn)

            m_cnt.by(pe.matmul(A[0][0:EXPERTS, 0:1], counts[:, TILES, :], ones[:, 0:1], start=True, stop=True))
            pe.wait_ge(s_elist.sem, 1)
            m_cnt.by(pe.matmul(A[1][0:EXPERTS, 0:1], lt[0:EXPERTS, 0:EXPERTS], e_num[:, 1:2], start=True, stop=True))
            pe.wait_ge(s_elist.sem, 3)
            pe.matmul(B[0][0:1, 0:EXPERTS], cs[0:EXPERTS, C_PART:C_PART + 1], e_hot[:], start=True, stop=True)
            m_cnt.by(pe.matmul(B[0][0:1, 128:129], ones[0:EXPERTS, 0:1], e_num[:, 1:2], start=True, stop=True))

            pe.wait_ge(s_elist.sem, 7)
            n_active = pe.value_load(e_list_i[0:1, 2 * EXPERTS:2 * EXPERTS + 1], min_val=0, max_val=EXPERTS)
            with pe.Fori(0, PAIRS) as i:
                with pe.If(i * 2 < n_active):
                    turn = Turn(pe, i)
                    for q in range(2):
                        turn.need(xb_in[q])
                        for k in range(KD):
                            ins = pe.transpose(A[q][:, k * P:(k + 1) * P], xb[:, q, k * P:(k + 1) * P], ident)
                        t_xb.by(ins)
                    for q in range(2):
                        turn.need(s_xbt, q + 1)
                        turn.need(w13_in[q])
                        for m in range(2):
                            for c in range(2):
                                lo = m * FF + c * FH
                                for k in range(KD):
                                    ins = pe.matmul(B[q][0:FH, (2 * m + c) * P:(2 * m + c + 1) * P],
                                                    w13_s[:, q, k, lo:lo + FH], xb_t[:, q, k, :],
                                                    start=(k == 0), stop=(k == KD - 1))
                        m_h.by(ins)
                    for q in range(2):
                        turn.need(s_hx, q + 1)
                        turn.need(w2_in[q])
                        for c in range(2):
                            ins = pe.matmul(C[q][:, 0:D], hx[:, q, c, :], w2_s[:, q, c, :],
                                            start=(c == 0), stop=(c == 1))
                        m_yo.by(ins)
                    turn.need(added)
                    pe.sem_inc(wait_done.sem, 1)
                with pe.Else():
                    pe.nop()


ACC_OOB = False


def kernel(x, ctx_1024, L0_attn_ln_w, L0_attn_ln_b, L0_attn_in_proj_w, L0_attn_conv_w, L0_attn_conv_b,
           L0_attn_dt_bias, L0_attn_A_log, L0_attn_D_skip, L0_attn_norm_w, L0_attn_out_proj_w, L0_ffn_gate_w,
           L0_ffn_gate_b, L0_ffn_w1, L0_ffn_w2, L0_ffn_w3, L0_ffn_ws1, L0_ffn_ws2, L0_ffn_ws3):
    import concourse.bacc as _bacc
    from concourse.bass_utils import run_bass_kernel_spmd as _run

    def lay(a):
        return np.ascontiguousarray(np.asarray(a))

    def on_partitions(a):
        a = np.asarray(a)
        return lay(np.swapaxes(a.reshape((a.shape[0] // P, P) + a.shape[1:]), 0, 1))

    ctx_rows = np.asarray(ctx_1024)
    of_group = np.arange(GROUPS) * GROUP // SEQ
    w13 = np.concatenate([np.asarray(L0_ffn_w1), np.asarray(L0_ffn_w3)], axis=1)
    arrays = {
        "x": lay(np.asarray(x).reshape(TOKENS, D)),
        "cst": constants(),
        "lnwb": lay(np.stack([on_partitions(L0_attn_ln_w), on_partitions(L0_attn_ln_b)], axis=1)),
        "w_in": on_partitions(np.asarray(L0_attn_in_proj_w).T),
        "conv_w": on_partitions(np.asarray(L0_attn_conv_w)[:, 0, :]),
        "conv_b": on_partitions(L0_attn_conv_b),
        "rows8": lay(np.broadcast_to(np.stack([np.asarray(L0_attn_dt_bias), np.asarray(L0_attn_A_log)])[None],
                                     (P, 2, HEADS))),
        "rows_d": lay(np.broadcast_to(np.repeat(np.asarray(L0_attn_D_skip), HEAD)[None], (P, INNER))),
        "norm_w": on_partitions(L0_attn_norm_w),
        "w_out": on_partitions(np.asarray(L0_attn_out_proj_w).T),
        "ctx_in": lay(ctx_rows[of_group]),
        "ctx_t": lay(ctx_rows.transpose(0, 2, 1).reshape(2, KD, P, CTX).transpose(0, 2, 1, 3)[of_group]),
        "gate_t": on_partitions(np.asarray(L0_ffn_gate_w).T),
        "gate_b": lay(np.broadcast_to(np.asarray(L0_ffn_gate_b)[None], (P, EXPERTS))),
        "w13": lay(w13.transpose(0, 2, 1).reshape(EXPERTS, KD, P, 2 * FF).transpose(0, 2, 1, 3)),
        "w2": lay(np.asarray(L0_ffn_w2).transpose(0, 2, 1)),
        "ws1": on_partitions(np.asarray(L0_ffn_ws1).T),
        "ws3": on_partitions(np.asarray(L0_ffn_ws3).T),
        "ws2": lay(np.asarray(L0_ffn_ws2).T),
    }
    nc = _bacc.Bacc("TRN2", target_bir_lowering=False, num_devices=1)
    args = [nc.dram_tensor(name, a.shape, mybir.dt.from_np(a.dtype), kind="ExternalInput").ap()
            for name, a in arrays.items()]
    out = nc.dram_tensor("out", (TOKENS, D), F32, kind="ExternalOutput").ap()
    decoder_layer(nc, *args, out)
    r = _run(nc, [arrays], core_ids=[0])
    return r.results[0]["out"].reshape(2, SEQ, D)
```

```python
from contextlib import ExitStack

import numpy as np

import concourse.bass as bass
from concourse import mybir

F32 = mybir.dt.float32
I32 = mybir.dt.int32
U32 = mybir.dt.uint32
BF16 = mybir.dt.bfloat16
ALU = mybir.AluOpType
ACT = mybir.ActivationFunctionType
AX = mybir.AxisListType

P = 128
TOKENS, D = 2048, 256
SEQ = 1024
KD = D // P
TILES = 4
GROUP = TILES * P
GROUPS = TOKENS // GROUP
INNER, STATE, HEADS, HEAD = 512, 64, 8, 64
CONV_DIM, TAPS = INNER + 2 * STATE, 4
CB = CONV_DIM // P
PROJ = 2 * INNER + 2 * STATE + HEADS
CTX = 77
EXPERTS, TOP, CAP, FF = 64, 6, 128, 176
FH = FF // 2
SHARED = 2 * FF
SB = [(0, 128), (128, 256), (256, SHARED)]
EPS = 1e-5
BATCH = 4
FAR = -3.0e38
NOWHERE = 1 << 20
ATANH = [1.0 / 17, 1.0 / 15, 1.0 / 13, 1.0 / 11, 1.0 / 9, 1.0 / 7, 1.0 / 5, 1.0 / 3]

C_ID, C_LE, C_LT, C_ONE, C_IOTA, C_TOK, C_CARRY, C_PART, C_KEY = 0, 128, 256, 384, 512, 576, 592, 596, 600
C_ALL = C_KEY + EXPERTS
KEY = 2 * EXPERTS * CAP


def constants():
    c = np.zeros((P, C_ALL), np.float32)
    i = np.arange(P)
    c[:, C_ID:C_ID + P] = i[:, None] == i[None, :]
    c[:, C_LE:C_LE + P] = i[:, None] <= i[None, :]
    c[:, C_LT:C_LT + P] = i[:, None] < i[None, :]
    c[:, C_ONE:C_ONE + P] = 1.0
    c[:, C_IOTA:C_IOTA + EXPERTS] = np.arange(EXPERTS)[None, :]
    c[:, C_TOK:C_TOK + TOKENS // P] = i[:, None] + P * np.arange(TOKENS // P)[None, :]
    c[:, C_CARRY:C_CARRY + GROUPS] = (np.arange(GROUPS) * GROUP % SEQ != 0)[None, :]
    c[:, C_PART] = i
    c[:, C_KEY:C_KEY + EXPERTS] = KEY - CAP * np.arange(EXPERTS)[None, :]
    return c


def row_pickers():
    r = np.arange(3 * TILES * HEADS) % (TILES * HEADS)
    pick = r[:, None] == np.arange(TILES * HEADS)[None, :]
    return np.ascontiguousarray(np.broadcast_to(pick[:, :, None], (len(r), TILES * HEADS, P)))


class Signal:

    def __init__(self, nc, ctx, name, per, unit=1, ahead=0):
        self.sem, self.per, self.unit, self.ahead = ctx.enter_context(nc.semaphore(name)), per, unit, ahead

    def of(self, g, k=None):
        return (g * self.per + (self.per if k is None else k)) * self.unit

    def turn(self, i, k=None):
        k = self.per if k is None else k
        return i * (self.per * self.unit) + (k + self.ahead) * self.unit


def decoder_layer(nc, x, cst, picks, lnwb, w_in, conv_w, conv_b, rows8, rows_d, norm_w, w_out, ctx_in, ctx_t,
                  gate_t, gate_b, w13, w2, ws1, ws3, ws2, out):
    ROW = D + EXPERTS
    xf_dram = nc.dram_tensor("xf_scratch", (TOKENS, ROW), F32, kind="Internal").ap()
    slots = nc.dram_tensor("slot_table", ((EXPERTS + 1) * CAP, 1), I32, kind="Internal").ap()
    x_v = x.rearrange("(g t p) d -> g p t d", p=P, t=TILES)
    xf_v = xf_dram.rearrange("(g t p) d -> g p t d", p=P, t=TILES)
    out_v = out.rearrange("(g t p) d -> g p t d", p=P, t=TILES)
    TH = TILES * HEADS
    LIST = EXPERTS + BATCH

    with ExitStack() as ctx:
        def sb(name, shape, dt=F32):
            return ctx.enter_context(nc.sbuf_tensor(name, shape, dt))

        def signal(name, per, unit=1, ahead=0):
            return Signal(nc, ctx, name, per, unit, ahead)

        bank = [ctx.enter_context(nc.psum_tensor(f"bank{i}", [P, 512], F32)) for i in range(8)]
        A, B, C, DD = bank[0:2], bank[2:4], bank[4:6], bank[6:8]

        cs = sb("cs", [P, C_ALL])
        ident, le, lt, ones = (cs[:, c:c + P] for c in (C_ID, C_LE, C_LT, C_ONE))
        iota = cs[:, C_IOTA:C_IOTA + EXPERTS]
        lt_b = sb("lt_b", [P, P], BF16)
        ones_b = sb("ones_b", [P, P], BF16)
        pick_s = sb("pick_s", [3 * TH, TH, P], BF16)
        tok_i = sb("tok_i", [P, TOKENS // P], I32)
        lnwb_s = sb("lnwb_s", [P, 2, KD])
        w_in_s = sb("w_in_s", [P, KD, PROJ])
        conv_w_s = sb("conv_w_s", [P, CB, TAPS])
        conv_b_s = sb("conv_b_s", [P, CB])
        rows8_s = sb("rows8_s", [P, 2, HEADS])
        neg_a = sb("neg_a", [P, HEADS])
        rows_d_s = sb("rows_d_s", [P, INNER])
        norm_w_s = sb("norm_w_s", [P, INNER // P])
        w_out_s = sb("w_out_s", [P, INNER // P, D])
        gate_s = sb("gate_s", [P, KD, EXPERTS])
        gate_b_s = sb("gate_b_s", [P, EXPERTS])
        ws1_s = sb("ws1_s", [P, KD, SHARED])
        ws3_s = sb("ws3_s", [P, KD, SHARED])
        ws2_s = sb("ws2_s", [P, len(SB), D])
        minus_half = sb("minus_half", [P, TILES])
        blank = sb("blank", [P, EXPERTS + 1], I32)

        x_s = sb("x_s", [P, TILES, D])
        y1 = sb("y1", [P, TILES, D])
        res = sb("res", [P, TILES, D])
        xh = sb("xh", [P, TILES, D])
        stats = sb("stats", [P, 4, TILES, 6])
        mv = sb("mv", [P, 4, TILES, 2])
        var_eps = sb("var_eps", [P, 5, TILES])
        rstd = sb("rstd", [P, 5, TILES])
        shift = sb("shift", [P, 4, TILES])
        xnt = sb("xnt", [P, KD, GROUP])
        zs = sb("zs", [P, TILES, INNER])
        raw = sb("raw", [P, CB, GROUP + TAPS - 1])
        conv = sb("conv", [P, CB, GROUP])
        c_t = sb("c_t", [STATE, GROUP])
        dt_v, dt_abs, dt_u, dt_den, dt_s, dt_q, dt_p, dt_relu = (
            sb(f"dt_{n}", [P, TH]) for n in ("v", "abs", "u", "den", "s", "q", "p", "relu"))
        dt = sb("dt", [P, TILES, HEADS])
        a_s = sb("a_s", [P, TILES, HEADS])
        xs = sb("xs", [P, TILES, INNER])
        b_tok = sb("b_tok", [P, TILES, STATE])
        xdt = sb("xdt", [P, TILES, INNER])
        cum = sb("cum", [P, TILES, HEADS])
        to_end = sb("to_end", [P, TILES, HEADS])
        e_cum = sb("e_cum", [P, TILES, HEADS])
        e_end = sb("e_end", [P, TILES, HEADS])
        e_tot = sb("e_tot", [P, TILES, HEADS])
        cum_parts = sb("cum_parts", [3 * TH, P], BF16)
        cum_mid = sb("cum_mid", [TH, P], BF16)
        cum_rest = sb("cum_rest", [TH, 2, P])
        xdec = sb("xdec", [P, TILES, INNER])
        gm = sb("gm", [P, TILES, P])
        m_s = sb("m_s", [P, TILES, HEADS, P])
        state = sb("state", [STATE, TILES + 1, INNER])
        y_off = sb("y_off", [P, TILES, INNER])
        yg = y_off
        square = sb("square", [P, INNER])
        sumsq = sb("sumsq", [P, TILES])
        yg_t = sb("yg_t", [P, 2, INNER // P, P])
        x1 = sb("x1", [P, TILES, D])
        xl = sb("xl", [P, TILES, D])
        xl_t = sb("xl_t", [P, 2, KD, P])
        ctx_s = sb("ctx_s", [CTX, D])
        ctx_t_s = sb("ctx_t_s", [P, KD, CTX])
        neg_max = sb("neg_max", [P, 2, TILES])
        exp_sum = sb("exp_sum", [P, 2, TILES])
        inv_sum = sb("inv_sum", [P, 2, TILES])
        probs = sb("probs", [P, TILES, CTX])
        probs_t = sb("probs_t", [CTX, TILES, P])
        x2 = sb("x2", [P, TILES, D])
        xf = sb("xf", [P, TILES, ROW])
        xf_t = sb("xf_t", [P, KD, GROUP])
        biased = sb("biased", [P, TILES, EXPERTS + 2])
        top8 = sb("top8", [P, TILES, 8])
        taken = sb("taken", [P, TILES, EXPERTS + 2])
        chosen = sb("chosen", [P, TILES, EXPERTS], BF16)
        counts = sb("counts", [P, TILES + 1, EXPERTS], BF16)
        fits = sb("fits", [P, TILES, EXPERTS])
        key = sb("key", [P, TILES, EXPERTS])
        top_key = sb("top_key", [P, TILES, 8])
        slot_i = sb("slot_i", [P, TILES, 8], I32)
        hs = sb("hs", [P, len(SB), GROUP])
        o_s = sb("o_s", [P, TILES, D])

        e_num = sb("e_num", [EXPERTS, 4])
        e_hot = sb("e_hot", [EXPERTS, EXPERTS])
        e_list = sb("e_list", [1, 2 * LIST + 1])
        e_list_i = sb("e_list_i", [1, 2 * LIST + 1], I32)
        slots_i = sb("slots_i", [EXPERTS + 1, CAP], I32)
        slots_f = sb("slots_f", [EXPERTS + 1, CAP])
        slots_t = sb("slots_t", [P, EXPERTS + 1], I32)
        tab_g = sb("tab_g", [P, BATCH, 1], I32)
        tab_s = sb("tab_s", [P, BATCH, 1], I32)

        def over(tensor, name, shape):
            axes = " ".join("abc"[:len(tensor.shape) - 1])
            flat = tensor[:].rearrange(f"p {axes} -> p ({axes})")
            size = int(np.prod(shape[1:]))
            names = " ".join("abcd"[:len(shape) - 1])
            return flat[0:shape[0], 0:size].rearrange(f"p ({names}) -> p {names}",
                                                      **dict(zip("abcd", shape[1:])))

        xb = over(y_off, "xb", [P, BATCH, ROW])
        xb_t = over(xdec, "xb_t", [P, BATCH, KD, P])
        w13_s = over(m_s, "w13_s", [P, BATCH, KD, 2 * FF])
        w2_s = over(raw, "w2_s", [FH, BATCH, 2, D])
        h1 = over(xdt, "h1", [FH, BATCH, 2 * P])
        hx = over(xs, "hx", [FH, BATCH, 2, P])
        yo = over(zs, "yo", [P, BATCH, D])

        s_const = signal("s_const", 1, 16)
        s_weights = signal("s_weights", 11, 16)
        s_shared = signal("s_shared", 5, 16)
        s_blank = signal("s_blank", 1)
        s_table = signal("s_table", 1, 16)
        s_zero = signal("s_zero", 5)
        s_small = signal("s_small", 3)
        s_exp_a = signal("s_exp_a", 1)
        s_wout = signal("s_wout", INNER // P + 1)
        s_half = signal("s_half", 1)

        x_in = signal("x_in", 1, 16)
        f_stats = signal("f_stats", 2 * TILES)
        f_mv = signal("f_mv", 2 * TILES)
        f_var = signal("f_var", 2)
        f_rstd = signal("f_rstd", 2)
        s_y1 = signal("s_y1", TILES)
        f_shift = signal("f_shift", 1)
        s_res = signal("s_res", 1)
        s_xh = signal("s_xh", TILES)
        t_xh = signal("t_xh", TILES)
        s_xnt = signal("s_xnt", TILES)
        m_z = signal("m_z", TILES)
        s_z = signal("s_z", TILES)
        m_dt = signal("m_dt", 1)
        m_x = signal("m_x", CB)
        s_halo = signal("s_halo", 1)
        s_raw = signal("s_raw", CB)
        s_tap = signal("s_tap", CB * TAPS)
        s_conv = signal("s_conv", CB)
        c_moved = signal("c_moved", 1, 16)
        s_dtv = signal("s_dtv", 3)
        s_u = signal("s_u", 1)
        s_sq = signal("s_sq", 4)
        s_poly = signal("s_poly", len(ATANH) + 1)
        s_dt = signal("s_dt", 2)
        t_x = signal("t_x", TILES)
        t_b = signal("t_b", 1)
        s_xs = signal("s_xs", TILES)
        s_btok = signal("s_btok", 1)
        s_xdt = signal("s_xdt", TILES)
        m_cum = signal("m_cum", 3)
        s_cum = signal("s_cum", 2)
        s_parts = signal("s_parts", 6)
        s_ecum = signal("s_ecum", 3)
        s_xd = signal("s_xd", TILES)
        s_xdec = signal("s_xdec", TILES)
        m_g = signal("m_g", 1)
        s_gm = signal("s_gm", 1)
        m_rows = signal("m_rows", 2 * TILES)
        s_drop = signal("s_drop", 2 * TILES)
        s_decay = signal("s_decay", 2 * TILES)
        s_m = signal("s_m", TILES)
        m_y = signal("m_y", TILES)
        m_off = signal("m_off", TILES)
        m_state = signal("m_state", TILES)
        s_sdec = signal("s_sdec", TILES)
        s_state = signal("s_state", TILES + 1)
        s_yoff = signal("s_yoff", TILES)
        s_skip = signal("s_skip", TILES)
        s_ysum = signal("s_ysum", TILES)
        s_yg = signal("s_yg", TILES)
        ctx_loaded = signal("ctx_loaded", 2, 16)
        s_sumsq = signal("s_sumsq", TILES)
        t_yg = signal("t_yg", TILES)
        s_ygt = signal("s_ygt", TILES)
        m_out = signal("m_out", TILES)
        t_stats = signal("t_stats", 2 * TILES)
        t_mv = signal("t_mv", 2 * TILES)
        t_var = signal("t_var", 3)
        t_rstd = signal("t_rstd", 3)
        t_shift = signal("t_shift", 2)
        s_x1 = signal("s_x1", TILES)
        s_xl = signal("s_xl", TILES)
        t_xl = signal("t_xl", TILES)
        s_xlt = signal("s_xlt", TILES)
        m_sc = signal("m_sc", TILES)
        s_max = signal("s_max", 2 * TILES)
        s_probs = signal("s_probs", TILES)
        s_inv = signal("s_inv", 2 * TILES)
        t_pr = signal("t_pr", TILES)
        s_prt = signal("s_prt", TILES)
        m_att = signal("m_att", TILES)
        s_x2 = signal("s_x2", TILES)
        s_xf = signal("s_xf", TILES)
        xf_out = signal("xf_out", 1, 16)
        t_xf = signal("t_xf", TILES)
        s_xft = signal("s_xft", TILES)
        m_lg = signal("m_lg", TILES)
        s_elg = signal("s_elg", TILES)
        s_scores = signal("s_scores", TILES)
        s_biased = signal("s_biased", TILES)
        s_top = signal("s_top", TILES)
        s_six = signal("s_six", TILES)
        s_taken = signal("s_taken", TILES)
        s_chosen = signal("s_chosen", TILES)
        s_counts = signal("s_counts", TILES + 1)
        m_rank = signal("m_rank", TILES)
        s_fits = signal("s_fits", 2 * TILES)
        s_key = signal("s_key", TILES)
        s_order = signal("s_order", TILES)
        s_slot = signal("s_slot", TILES)
        sent = signal("sent", TOP * TILES, 16)
        m_s1 = signal("m_s1", len(SB))
        m_s3 = signal("m_s3", len(SB))
        s_hs = signal("s_hs", len(SB))
        s_hm = signal("s_hm", len(SB))
        m_sh = signal("m_sh", TILES)
        s_o = signal("s_o", TILES)
        o_out = signal("o_out", 1, 16)

        slots_in = signal("slots_in", 1, 16)
        m_cnt = signal("m_cnt", 3)
        s_elist = signal("s_elist", 9)
        s_slots = signal("s_slots", 2)
        m_slots = signal("m_slots", 1)
        w_in_e = [signal(f"w_in_e{q}", 2, 16) for q in range(BATCH)]
        s_tabg = signal("s_tabg", BATCH)
        s_tabs = signal("s_tabs", BATCH)
        xb_in = [signal(f"xb_in{q}", 1, 16) for q in range(BATCH)]
        t_xb = signal("t_xb", BATCH)
        s_xbt = signal("s_xbt", BATCH, ahead=BATCH)
        m_h = signal("m_h", BATCH)
        s_h1 = signal("s_h1", BATCH)
        s_hx = signal("s_hx", BATCH, ahead=BATCH)
        m_yo = signal("m_yo", BATCH, ahead=BATCH)
        s_yo = signal("s_yo", BATCH, ahead=BATCH)
        added = signal("added", BATCH, 16)
        landed = signal("landed", BATCH, ahead=BATCH)
        waited = signal("waited", 1)

        block = ctx.enter_context(nc.Block())
        flat = "p t h -> p (t h)"
        TURNS = EXPERTS // BATCH

        def heads(ap):
            return ap.unsqueeze(2).to_broadcast([ap.shape[0], HEADS, HEAD])

        def per_head(ap):
            return ap.rearrange("p (h c) -> p h c", h=HEADS)

        def half_bank(banks, t):
            return banks[t // 2][:, t % 2 * D:(t % 2 + 1) * D]

        def logit(t):
            return C[t // 2][:, t % 2 * EXPERTS:(t % 2 + 1) * EXPERTS]

        def rank(t):
            return C[t // 2][:, D + t % 2 * EXPERTS:D + (t % 2 + 1) * EXPERTS]

        def rounds(front, scan, tail_and_front):
            front(0)
            for g in range(GROUPS):
                scan(g)
                tail_and_front(g, g + 1 if g + 1 < GROUPS else None)

        def turns_of(n_active):
            return (n_active + (BATCH - 1)) // BATCH

        def number_of(engine, at, top, least=0):
            return engine.value_load(e_list_i[0:1, at], min_val=least, max_val=top)

        @block.sync
        def _(sp):

            def load_x(g):
                if g:
                    sp.wait_ge(s_y1.sem, s_y1.of(g - 1))
                if g:
                    sp.wait_ge(s_res.sem, s_res.of(g - 1))
                sp.dma_start(x_s[:], x_v[g]).then_inc(x_in.sem, 16)

            load_x(0)
            sp.dma_start(cs[:], cst).then_inc(s_const.sem, 16)
            sp.dma_start(lnwb_s[:], lnwb).then_inc(s_weights.sem, 16)
            sp.dma_start(w_in_s[:], w_in).then_inc(s_weights.sem, 16)
            for dst, src in ((pick_s, picks), (conv_w_s, conv_w), (conv_b_s, conv_b), (rows8_s, rows8),
                             (rows_d_s, rows_d), (norm_w_s, norm_w), (w_out_s, w_out), (gate_s, gate_t),
                             (gate_b_s, gate_b)):
                sp.dma_start(dst[:], src).then_inc(s_weights.sem, 16)
            sp.dma_start(ws1_s[:], ws1).then_inc(s_shared.sem, 16)
            sp.dma_start(ws3_s[:], ws3).then_inc(s_shared.sem, 16)
            for n, (lo, hi) in enumerate(SB):
                sp.dma_start(ws2_s[0:hi - lo, n, :], ws2[lo:hi, :]).then_inc(s_shared.sem, 16)
            sp.wait_ge(s_blank.sem, s_blank.of(0))
            sp.dma_start(slots.rearrange("(p n) w -> p (n w)", p=P), blank[:]).then_inc(s_table.sem, 16)

            def move_c(g):
                sp.wait_ge(s_conv.sem, s_conv.of(g))
                if g:
                    sp.wait_ge(m_g.sem, m_g.of(g - 1))
                if g:
                    sp.wait_ge(m_off.sem, m_off.of(g - 1))
                sp.dma_start(c_t[:], conv[STATE:P, CB - 1, :]).then_inc(c_moved.sem, 16)

            def tail_and_front(g, f):
                if g:
                    sp.wait_ge(m_sc.sem, m_sc.of(g - 1))
                if g:
                    sp.wait_ge(m_att.sem, m_att.of(g - 1))
                sp.dma_start(ctx_s[:], ctx_in[g]).then_inc(ctx_loaded.sem, 16)
                sp.dma_start(ctx_t_s[:], ctx_t[g]).then_inc(ctx_loaded.sem, 16)
                if f is not None:
                    move_c(f)
                sp.wait_ge(s_xf.sem, s_xf.of(g))
                sp.wait_ge(s_scores.sem, s_scores.of(g))
                sp.dma_start(xf_v[g], xf[:]).then_inc(xf_out.sem, 16)
                sp.wait_ge(s_o.sem, s_o.of(g))
                sp.dma_start(out_v[g], o_s[:]).then_inc(o_out.sem, 16)

            def scan(g):
                if g + 1 < GROUPS:
                    load_x(g + 1)

            rounds(move_c, scan, tail_and_front)
            sp.wait_ge(o_out.sem, o_out.of(GROUPS - 1))
            sp.wait_ge(sent.sem, sent.of(GROUPS - 1))
            sp.dma_start(slots_i[:], slots.rearrange("(e c) w -> e (c w)", c=CAP)).then_inc(slots_in.sem, 16)

            sp.wait_ge(s_elist.sem, s_elist.of(0))
            n_active = number_of(sp, slice(2 * LIST, 2 * LIST + 1), EXPERTS, 1)

            def load_expert(q, at):
                e = number_of(sp, at, EXPERTS - 1)
                sp.dma_start(w13_s[:, q], w13[bass.ds(e, 1)].rearrange("o p k f -> (o p) k f")).then_inc(w_in_e[q].sem, 16)
                sp.dma_start(w2_s[:, q], w2[bass.ds(e, 1)].rearrange("o (c f) d -> (o f) c d", f=FH)).then_inc(w_in_e[q].sem, 16)

            for q in range(BATCH):
                load_expert(q, slice(q, q + 1))
            with sp.Fori(0, TURNS) as i:
                with sp.If(i * BATCH < n_active):
                    for q in range(BATCH):
                        sp.wait_ge(m_yo.sem, m_yo.turn(i, q + 1))
                        sp.sem_inc(waited.sem, 1)
                        load_expert(q, bass.ds(i * BATCH + (BATCH + q), 1))
                with sp.Else():
                    sp.nop()
            for q in range(BATCH):
                sp.wait_ge(w_in_e[q].sem, w_in_e[q].turn(turns_of(n_active)))
            sp.sem_inc(waited.sem, 1)

        @block.gpsimd
        def _(pool):
            pool.memset(blank[:], NOWHERE).then_inc(s_blank.sem, 1)
            pool.memset(minus_half[:], -0.5).then_inc(s_half.sem, 1)
            pool.wait_ge(s_half.sem, s_half.of(0))

            def inverse_root(slot, src, scale, g, var, done, k):
                pool.tensor_scalar(var_eps[:, slot, :], src, scale, EPS, ALU.mult, ALU.add).then_inc(var.sem, 1)
                pool.wait_ge(var.sem, var.of(g, k))
                pool.tensor_tensor(rstd[:, slot, :], var_eps[:, slot, :], minus_half[:], ALU.pow).then_inc(done.sem, 1)

            def front_root(g, n):
                pool.wait_ge(f_mv.sem, f_mv.of(g, (n + 1) * TILES))
                if n:
                    if g:
                        pool.wait_ge(s_xh.sem, s_xh.of(g - 1))
                inverse_root(n, mv[:, n, :, 1], 1.0, g, f_var, f_rstd, n + 1)

            def residual(g):
                pool.wait_ge(s_y1.sem, s_y1.of(g))
                if g:
                    pool.wait_ge(s_x1.sem, s_x1.of(g - 1))
                pool.tensor_tensor(res[:], x_s[:], y1[:], ALU.add).then_inc(s_res.sem, 1)

            def front(g):
                front_root(g, 0)
                front_root(g, 1)
                residual(g)

            def scan(g):
                def skip(t):
                    pool.wait_ge(s_xd.sem, s_xd.of(g, t + 1))
                    pool.wait_ge(s_yoff.sem, s_yoff.of(g, t + 1))
                    pool.tensor_tensor(y_off[:, t, :], y_off[:, t, :], xs[:, t, :], ALU.add).then_inc(s_skip.sem, 1)

                if g == 0:
                    pool.wait_ge(s_weights.sem, s_weights.of(0))
                pool.wait_ge(s_ecum.sem, s_ecum.of(g))
                for t in range(TILES):
                    pool.wait_ge(s_xdt.sem, s_xdt.of(g, t + 1))
                    if g and t == 0:
                        pool.wait_ge(m_state.sem, m_state.of(g - 1))
                    pool.tensor_tensor(per_head(xdec[:, t, :]), per_head(xdt[:, t, :]),
                                       heads(e_end[:, t, :]), ALU.mult).then_inc(s_xdec.sem, 1)
                    pool.wait_ge(s_state.sem, s_state.of(g, t + 1))
                    pool.tensor_tensor(per_head(state[:, t + 1, :]), per_head(state[:, t, :]),
                                       heads(e_tot[0:STATE, t, :]), ALU.mult).then_inc(s_sdec.sem, 1)
                    pool.tensor_tensor(xs[:, t, :], xs[:, t, :], rows_d_s[:], ALU.mult).then_inc(s_xd.sem, 1)
                    if t:
                        skip(t - 1)
                skip(TILES - 1)

            def scatter(g, t):
                if g < 0:
                    return
                pool.wait_ge(s_slot.sem, s_slot.of(g, t + 1))
                if g == 0 and t == 0:
                    pool.wait_ge(s_table.sem, s_table.of(0))
                for k in range(TOP):
                    n = g * TILES + t
                    pool.indirect_dma_start(
                out=slots, out_offset=bass.IndirectOffsetOnAxis(ap=slot_i[:, t, k:k + 1], axis=0),
                in_=tok_i[:, n:n + 1], in_offset=None, bounds_check=EXPERTS * CAP - 1, oob_is_err=False).then_inc(sent.sem, 16)

            def tail_and_front(g, f):
                if f is not None:
                    front_root(f, 0)
                pool.wait_ge(s_sumsq.sem, s_sumsq.of(g))
                inverse_root(2, sumsq[:], 1.0 / INNER, g, t_var, t_rstd, 1)
                if f is not None:
                    front_root(f, 1)
                pool.wait_ge(t_mv.sem, t_mv.of(g, TILES))
                inverse_root(3, mv[:, 2, :, 1], 1.0, g, t_var, t_rstd, 2)
                if f is not None:
                    residual(f)
                scatter(g - 1, 0)
                scatter(g - 1, 1)
                pool.wait_ge(t_mv.sem, t_mv.of(g, 2 * TILES))
                inverse_root(4, mv[:, 3, :, 1], 1.0, g, t_var, t_rstd, 3)
                scatter(g - 1, 2)
                scatter(g - 1, 3)

            rounds(front, scan, tail_and_front)
            for t in range(TILES):
                scatter(GROUPS - 1, t)

            pool.wait_ge(s_elist.sem, s_elist.of(0))
            pool.wait_ge(s_slots.sem, s_slots.of(0))
            pool.wait_ge(xf_out.sem, xf_out.of(GROUPS - 1))
            pool.wait_ge(o_out.sem, o_out.of(GROUPS - 1))
            n_active = number_of(pool, slice(2 * LIST, 2 * LIST + 1), EXPERTS, 1)

            def copy_slots(q, e):
                pool.tensor_copy(tab_g[:, q, :], slots_t[:, bass.ds(e, 1)]).then_inc(s_tabg.sem, 1)

            def gather(q):
                pool.indirect_dma_start(
        out=xb[:, q, :], out_offset=None, in_=xf_dram,
        in_offset=bass.IndirectOffsetOnAxis(ap=tab_g[:, q, :], axis=0),
        bounds_check=TOKENS - 1, oob_is_err=False).then_inc(xb_in[q].sem, 16)

            for q in range(BATCH):
                e = number_of(pool, slice(LIST + q, LIST + q + 1), EXPERTS)
                copy_slots(q, e)
                pool.wait_ge(s_tabg.sem, s_tabg.of(0, q + 1))
                gather(q)
            pool.sem_inc(landed.sem, BATCH)
            with pool.Fori(0, TURNS) as i:
                with pool.If(i * BATCH < n_active):
                    for q in range(BATCH):
                        e = number_of(pool, bass.ds(i * BATCH + (LIST + q), 1), EXPERTS)
                        pool.tensor_copy(tab_s[:, q, :], slots_t[:, bass.ds(e, 1)]).then_inc(s_tabs.sem, 1)
                        pool.wait_ge(s_tabs.sem, s_tabs.turn(i, q + 1))
                        pool.wait_ge(s_yo.sem, s_yo.turn(i, q + 1))
                        if q:
                            pool.wait_ge(added.sem, added.turn(i, q))
                            pool.sem_inc(landed.sem, 1)
                        else:
                            pool.sem_inc(waited.sem, 1)
                        pool.indirect_dma_start(
                   out=out, out_offset=bass.IndirectOffsetOnAxis(ap=tab_s[:, q, :], axis=0),
                   in_=yo[:, q, :], in_offset=None, bounds_check=TOKENS - 1, oob_is_err=False,
                   compute_op=ALU.add).then_inc(added.sem, 16)
                        e = number_of(pool, bass.ds(i * BATCH + (LIST + BATCH + q), 1), EXPERTS)
                        copy_slots(q, e)
                        pool.wait_ge(s_tabg.sem, s_tabg.turn(i, BATCH + q + 1))
                        pool.sem_inc(waited.sem, 1)
                        gather(q)
                    pool.wait_ge(added.sem, added.turn(i))
                    pool.sem_inc(landed.sem, 1)
                with pool.Else():
                    pool.nop()
            for q in range(BATCH):
                pool.wait_ge(xb_in[q].sem, xb_in[q].turn(turns_of(n_active)))
            pool.wait_ge(added.sem, added.turn(turns_of(n_active), 0))
            pool.sem_inc(waited.sem, 1)

        @block.scalar
        def _(act):
            act.wait_ge(s_weights.sem, s_weights.of(0))
            act.activation(neg_a[:], rows8_s[:, 1, :], ACT.Exp).then_inc(s_exp_a.sem, 1)

            def normed_front(g):
                for t in range(TILES):
                    if t == 0:
                        act.wait_ge(f_shift.sem, f_shift.of(g))
                    act.activation(xh[:, t, :], y1[:, t, :], ACT.Identity, scale=rstd[:, 1, t:t + 1],
                                   bias=shift[:, 1, t:t + 1]).then_inc(s_xh.sem, 1)

            def channels(g):
                for t in range(TILES):
                    act.wait_ge(t_xh.sem, t_xh.of(g, t + 1))
                    if g and t == 0:
                        act.wait_ge(m_dt.sem, m_dt.of(g - 1))
                    for k in range(KD):
                        ins = act.activation(xnt[:, k, t * P:(t + 1) * P], DD[t % 2][:, k * P:(k + 1) * P],
                                             ACT.Identity, scale=lnwb_s[:, 0, k:k + 1], bias=lnwb_s[:, 1, k:k + 1])
                    ins.then_inc(s_xnt.sem, 1)

            def gate_z(g):
                for t in range(TILES):
                    act.wait_ge(m_z.sem, m_z.of(g, t + 1))
                    act.activation(zs[:, t, :], DD[t % 2][:], ACT.Silu).then_inc(s_z.sem, 1)

            def raw_x(g, c):
                if c == 0:
                    act.wait_ge(s_halo.sem, s_halo.of(g))
                act.wait_ge(m_x.sem, m_x.of(g, c + 1))
                act.activation(raw[:, c, TAPS - 1:], DD[c % 2][:], ACT.Copy).then_inc(s_raw.sem, 1)

            def conv_act(g, c):
                act.wait_ge(s_tap.sem, s_tap.of(g, TAPS * (c + 1)))
                act.activation(conv[:, c, :], conv[:, c, :], ACT.Silu, bias=conv_b_s[:, c:c + 1]).then_inc(s_conv.sem, 1)

            def small_exp(g):
                act.wait_ge(s_dtv.sem, s_dtv.of(g, 2))
                act.activation(dt_u[:], dt_abs[:], ACT.Exp, scale=-1.0).then_inc(s_u.sem, 1)

            def token_major(g):
                for t in range(TILES):
                    act.wait_ge(t_x.sem, t_x.of(g, t + 1))
                    if g and t == 0:
                        act.wait_ge(s_skip.sem, s_skip.of(g - 1))
                    act.activation(xs[:, t, :], DD[t % 2][:], ACT.Copy).then_inc(s_xs.sem, 1)
                act.wait_ge(t_b.sem, t_b.of(g))
                if g:
                    act.wait_ge(m_state.sem, m_state.of(g - 1))
                act.activation(b_tok[:].rearrange("p t n -> p (t n)"), C[0][:, 0:TILES * STATE], ACT.Copy).then_inc(s_btok.sem, 1)

            def front(g):
                normed_front(g)
                channels(g)
                gate_z(g)
                for c in range(CB):
                    raw_x(g, c)
                for c in range(CB):
                    conv_act(g, c)
                token_major(g)
                small_exp(g)

            def scan(g):
                act.wait_ge(s_cum.sem, s_cum.of(g))
                act.wait_ge(m_cum.sem, m_cum.of(g))
                act.activation(e_cum[:].rearrange(flat), cum[:].rearrange(flat), ACT.Exp).then_inc(s_ecum.sem, 1)
                act.activation(e_end[:].rearrange(flat), to_end[:].rearrange(flat), ACT.Exp).then_inc(s_ecum.sem, 1)
                act.activation(e_tot[:].rearrange(flat), C[1][:, TH:2 * TH], ACT.Exp).then_inc(s_ecum.sem, 1)
                for t in range(TILES):
                    for half in range(2):
                        act.wait_ge(m_rows.sem, m_rows.of(g, 2 * t + half + 1))
                        if g and t == 0 and half == 0:
                            act.wait_ge(m_y.sem, m_y.of(g - 1))
                        for j in range(HEADS // 2):
                            h = half * (HEADS // 2) + j
                            ins = act.activation(m_s[:, t, h, :], DD[half][:, j * P:(j + 1) * P], ACT.Relu,
                                                 scale=-1.0, bias=cum[:, t, h:h + 1])
                        ins.then_inc(s_drop.sem, 1)
                    for half in range(2):
                        act.wait_ge(s_drop.sem, s_drop.of(g, 2 * t + half + 1))
                        pair = m_s[:, t, half * (HEADS // 2):(half + 1) * (HEADS // 2), :]
                        act.activation(pair, pair, ACT.Exp, scale=-1.0).then_inc(s_decay.sem, 1)

            def out_side(g):
                for t in range(TILES):
                    act.wait_ge(t_yg.sem, t_yg.of(g, t + 1))
                    if t >= 2:
                        act.wait_ge(m_out.sem, m_out.of(g, t - 1))
                    act.activation(yg_t[:, t % 2].rearrange("p k c -> p (k c)"), B[t % 2][:], ACT.Copy).then_inc(s_ygt.sem, 1)
                    act.wait_ge(s_yg.sem, s_yg.of(g, t + 1))
                    if g or t:
                        act.wait_ge(s_sumsq.sem, s_sumsq.of(g, t))
                    act.activation(square[:], yg[:, t, :], ACT.Square, accum_out=sumsq[:, t:t + 1]).then_inc(s_sumsq.sem, 1)

            def attention(g):
                for t in range(TILES):
                    if t == 0:
                        act.wait_ge(t_shift.sem, t_shift.of(g, 1))
                    if g and t == 0:
                        act.wait_ge(o_out.sem, o_out.of(g - 1))
                    act.activation(xl[:, t, :], x1[:, t, :], ACT.Identity, scale=rstd[:, 3, t:t + 1],
                                   bias=shift[:, 2, t:t + 1]).then_inc(s_xl.sem, 1)

                def softmax(t):
                    act.wait_ge(s_max.sem, s_max.of(g, t + 1))
                    act.activation(probs[:, t, :], C[t % 2][:, 0:CTX], ACT.Exp,
                                   bias=neg_max[:, 0, t:t + 1], accum_out=exp_sum[:, 0, t:t + 1]).then_inc(s_probs.sem, 1)

                for t in range(TILES):
                    act.wait_ge(t_xl.sem, t_xl.of(g, t + 1))
                    if t >= 2:
                        act.wait_ge(m_sc.sem, m_sc.of(g, t - 1))
                    act.activation(xl_t[:, t % 2].rearrange("p k c -> p (k c)"), B[t % 2][:, 0:D], ACT.Copy).then_inc(s_xlt.sem, 1)
                    if t:
                        softmax(t - 1)
                softmax(TILES - 1)
                for t in range(TILES):
                    act.wait_ge(t_pr.sem, t_pr.of(g, t + 1))
                    if g and t == 0:
                        act.wait_ge(m_att.sem, m_att.of(g - 1))
                    act.activation(probs_t[:, t, :], B[t % 2][0:CTX, 0:P], ACT.Copy).then_inc(s_prt.sem, 1)

            def route_in(g):
                for t in range(TILES):
                    if t == 0:
                        act.wait_ge(t_shift.sem, t_shift.of(g, 2))
                    if g and t == 0:
                        act.wait_ge(xf_out.sem, xf_out.of(g - 1))
                    act.activation(xf[:, t, 0:D], x2[:, t, :], ACT.Identity, scale=rstd[:, 4, t:t + 1],
                                   bias=shift[:, 3, t:t + 1]).then_inc(s_xf.sem, 1)
                for t in range(TILES):
                    act.wait_ge(t_xf.sem, t_xf.of(g, t + 1))
                    if g and t == 0:
                        act.wait_ge(m_s3.sem, m_s3.of(g - 1))
                    act.activation(xf_t[:, :, t * P:(t + 1) * P],
                                   B[t % 2][:, 0:D].rearrange("p (k c) -> p k c", k=KD), ACT.Copy).then_inc(s_xft.sem, 1)

            def route_exp(g):
                for t in range(TILES):
                    if t % 2 == 0:
                        act.wait_ge(s_max.sem, s_max.of(g, TILES + t // 2 * 2 + 2))
                    act.activation(xf[:, t, D:], logit(t), ACT.Exp,
                                   bias=neg_max[:, 1, t:t + 1], accum_out=exp_sum[:, 1, t:t + 1]).then_inc(s_elg.sem, 1)

            def shared_act(g):
                for n, (lo, hi) in enumerate(SB):
                    act.wait_ge(m_s1.sem, m_s1.of(g, n + 1))
                    if g and n == 0:
                        act.wait_ge(m_sh.sem, m_sh.of(g - 1))
                    act.activation(hs[0:hi - lo, n, :], A[n % 2][0:hi - lo, :], ACT.Silu).then_inc(s_hs.sem, 1)

            def tail_and_front(g, f):
                out_side(g)
                if f is not None:
                    normed_front(f)
                    channels(f)
                attention(g)
                if f is not None:
                    gate_z(f)
                    raw_x(f, 0)
                    raw_x(f, 1)
                    conv_act(f, 0)
                    raw_x(f, 2)
                    conv_act(f, 1)
                route_in(g)
                if f is not None:
                    raw_x(f, 3)
                    conv_act(f, 2)
                    raw_x(f, 4)
                route_exp(g)
                if f is not None:
                    conv_act(f, 3)
                shared_act(g)
                if f is not None:
                    conv_act(f, 4)
                    token_major(f)
                    small_exp(f)

            rounds(front, scan, tail_and_front)

            act.wait_ge(s_elist.sem, s_elist.of(0))
            n_active = number_of(act, slice(2 * LIST, 2 * LIST + 1), EXPERTS, 1)
            act.sem_inc(s_xbt.sem, BATCH)
            with act.Fori(0, TURNS) as i:
                with act.If(i * BATCH < n_active):
                    def rows_out(q):
                        act.wait_ge(t_xb.sem, t_xb.turn(i, q + 1))
                        act.activation(xb_t[:, q].rearrange("p k c -> p (k c)"), A[q % 2][:, 0:D], ACT.Copy).then_inc(s_xbt.sem, 1)

                    rows_out(0)
                    for q in range(BATCH):
                        if q + 1 < BATCH:
                            rows_out(q + 1)
                        act.wait_ge(m_h.sem, m_h.turn(i, q + 1))
                        act.activation(h1[:, q, :], B[q % 2][0:FH, 0:2 * P], ACT.Silu).then_inc(s_h1.sem, 1)
                with act.Else():
                    act.nop()

        @block.vector
        def _(dve):
            dve.memset(state[:], 0.0).then_inc(s_zero.sem, 1)
            dve.memset(counts[:], 0.0).then_inc(s_zero.sem, 1)
            dve.memset(raw[:], 0.0).then_inc(s_zero.sem, 1)
            dve.memset(e_list[:], 0.0).then_inc(s_zero.sem, 1)
            dve.memset(biased[:], FAR).then_inc(s_zero.sem, 1)
            dve.wait_ge(s_zero.sem, s_zero.of(0))

            def norm_stats(n, src, g, src_ready, stat, done, base):
                for t in range(TILES):
                    dve.wait_ge(src_ready.sem, src_ready.of(g, min(t + 1, src_ready.per)))
                    dve.bn_stats(stats[:, n, t, :], src[:, t, :]).then_inc(stat.sem, 1)
                for t in range(TILES):
                    dve.wait_ge(stat.sem, stat.of(g, base + t + 1))
                    dve.bn_aggr(mv[:, n, t, :], stats[:, n, t, :]).then_inc(done.sem, 1)

            def norm_shift(n, slot, g, rooted, k, done):
                dve.wait_ge(rooted.sem, rooted.of(g, k))
                dve.scalar_tensor_tensor(out=shift[:, n, :], in0=mv[:, n, :, 0], scalar=-1.0,
                                         in1=rstd[:, slot, :], op0=ALU.mult, op1=ALU.mult).then_inc(done.sem, 1)

            def first_norm(g):
                if g:
                    dve.wait_ge(s_xh.sem, s_xh.of(g - 1))
                if g:
                    dve.wait_ge(s_tap.sem, s_tap.of(g - 1))
                dve.tensor_scalar(raw[:, :, 0:TAPS - 1], raw[:, :, GROUP:],
                                  0.0 if g * GROUP % SEQ == 0 else 1.0, None, ALU.mult).then_inc(s_halo.sem, 1)
                norm_stats(0, x_s, g, x_in, f_stats, f_mv, 0)

            def first_apply(g):
                dve.wait_ge(f_rstd.sem, f_rstd.of(g, 1))
                for t in range(TILES):
                    dve.tensor_scalar(y1[:, t, :], x_s[:, t, :], mv[:, 0, t, 0:1], rstd[:, 0, t:t + 1],
                                      ALU.subtract, ALU.mult).then_inc(s_y1.sem, 1)
                norm_stats(1, y1, g, s_y1, f_stats, f_mv, TILES)

            def conv_taps(g, c):
                if c == 0:
                    dve.wait_ge(s_halo.sem, s_halo.of(g))
                dve.wait_ge(s_raw.sem, s_raw.of(g, c + 1))
                if g and c == 0:
                    dve.wait_ge(t_b.sem, t_b.of(g - 1))
                if g and c == 0:
                    dve.wait_ge(c_moved.sem, c_moved.of(g - 1))
                dve.tensor_scalar(conv[:, c, :], raw[:, c, TAPS - 1:], conv_w_s[:, c, TAPS - 1:TAPS],
                                  None, ALU.mult).then_inc(s_tap.sem, 1)
                for j in range(TAPS - 1):
                    dve.wait_ge(s_tap.sem, s_tap.of(g, TAPS * c + j + 1))
                    dve.scalar_tensor_tensor(out=conv[:, c, :], in0=raw[:, c, j:j + GROUP],
                                             scalar=conv_w_s[:, c, j:j + 1], in1=conv[:, c, :],
                                             op0=ALU.mult, op1=ALU.add).then_inc(s_tap.sem, 1)

            def dt_before(g):
                dve.wait_ge(m_dt.sem, m_dt.of(g))
                if g:
                    dve.wait_ge(s_dt.sem, s_dt.of(g - 1))
                dve.tensor_tensor(dt_v[:].rearrange("p (t h) -> p t h", h=HEADS),
                                  C[0][:, 0:TH].rearrange("p (t h) -> p t h", h=HEADS),
                                  rows8_s[:, 0, :].unsqueeze(1).to_broadcast([P, TILES, HEADS]), ALU.add).then_inc(s_dtv.sem, 1)
                dve.wait_ge(s_dtv.sem, s_dtv.of(g, 1))
                dve.scalar_tensor_tensor(out=dt_abs[:], in0=dt_v[:], scalar=-1.0, in1=dt_v[:],
                                         op0=ALU.mult, op1=ALU.max).then_inc(s_dtv.sem, 1)
                dve.tensor_scalar(dt_relu[:], dt_v[:], 0.0, None, ALU.max).then_inc(s_dtv.sem, 1)

            def dt_after(g):
                dve.wait_ge(s_u.sem, s_u.of(g))
                dve.tensor_scalar(dt_den[:], dt_u[:], 2.0, None, ALU.add).then_inc(s_sq.sem, 1)
                dve.wait_ge(s_sq.sem, s_sq.of(g, 1))
                dve.reciprocal(dt_den[:], dt_den[:]).then_inc(s_sq.sem, 1)
                dve.wait_ge(s_sq.sem, s_sq.of(g, 2))
                dve.tensor_tensor(dt_s[:], dt_u[:], dt_den[:], ALU.mult).then_inc(s_sq.sem, 1)
                dve.wait_ge(s_sq.sem, s_sq.of(g, 3))
                dve.tensor_tensor(dt_q[:], dt_s[:], dt_s[:], ALU.mult).then_inc(s_sq.sem, 1)
                dve.wait_ge(s_sq.sem, s_sq.of(g))
                dve.tensor_scalar(dt_p[:], dt_q[:], ATANH[0], None, ALU.mult).then_inc(s_poly.sem, 1)
                for n, c in enumerate(ATANH[1:]):
                    dve.wait_ge(s_poly.sem, s_poly.of(g, n + 1))
                    dve.scalar_tensor_tensor(out=dt_p[:], in0=dt_p[:], scalar=c, in1=dt_q[:],
                                             op0=ALU.add, op1=ALU.mult).then_inc(s_poly.sem, 1)
                dve.wait_ge(s_poly.sem, s_poly.of(g, len(ATANH)))
                dve.scalar_tensor_tensor(out=dt_p[:], in0=dt_p[:], scalar=1.0, in1=dt_s[:],
                                         op0=ALU.add, op1=ALU.mult).then_inc(s_poly.sem, 1)
                dve.wait_ge(s_poly.sem, s_poly.of(g))
                dve.wait_ge(s_dtv.sem, s_dtv.of(g))
                dve.scalar_tensor_tensor(out=dt[:].rearrange(flat), in0=dt_p[:], scalar=2.0,
                                         in1=dt_relu[:], op0=ALU.mult, op1=ALU.add).then_inc(s_dt.sem, 1)
                dve.wait_ge(s_dt.sem, s_dt.of(g, 1))
                if g == 0:
                    dve.wait_ge(s_wout.sem, s_wout.of(0))
                dve.tensor_tensor(a_s[:], dt[:], neg_a[:].unsqueeze(1).to_broadcast([P, TILES, HEADS]),
                                  ALU.mult).then_inc(s_dt.sem, 1)

            def inputs(g):
                for t in range(TILES):
                    dve.wait_ge(s_xs.sem, s_xs.of(g, t + 1))
                    if g and t == 0:
                        dve.wait_ge(s_xdec.sem, s_xdec.of(g - 1))
                    dve.tensor_tensor(per_head(xdt[:, t, :]), per_head(xs[:, t, :]), heads(dt[:, t, :]),
                                      ALU.mult).then_inc(s_xdt.sem, 1)

            def front(g):
                first_norm(g)
                first_apply(g)
                norm_shift(1, 1, g, f_rstd, 2, f_shift)
                dve.wait_ge(s_const.sem, s_const.of(0))
                dve.wait_ge(s_weights.sem, s_weights.of(0))
                dve.wait_ge(s_exp_a.sem, s_exp_a.of(0))
                dve.tensor_scalar(neg_a[:], neg_a[:], -1.0, None, ALU.mult).then_inc(s_wout.sem, 1)
                for k in range(INNER // P):
                    dve.tensor_scalar(w_out_s[:, k, :], w_out_s[:, k, :], norm_w_s[:, k:k + 1], None,
                                      ALU.mult).then_inc(s_wout.sem, 1)
                dve.tensor_copy(lt_b[:], lt).then_inc(s_small.sem, 1)
                dve.tensor_copy(ones_b[:], ones).then_inc(s_small.sem, 1)
                dve.tensor_copy(tok_i[:], cs[:, C_TOK:C_TOK + TOKENS // P]).then_inc(s_small.sem, 1)
                for c in range(CB):
                    conv_taps(g, c)
                dt_before(g)
                dt_after(g)
                inputs(g)

            def scan(g):
                if g:
                    dve.wait_ge(s_state.sem, s_state.of(g - 1))
                dve.tensor_scalar(state[:, 0, :], state[:, TILES, :],
                                  0.0 if g * GROUP % SEQ == 0 else 1.0, None, ALU.mult).then_inc(s_state.sem, 1)
                dve.wait_ge(m_cum.sem, m_cum.of(g))
                if g:
                    dve.wait_ge(m_rows.sem, m_rows.of(g - 1))
                rows = C[1][0:TH, 2 * TH:2 * TH + P]
                dve.tensor_copy(cum_parts[0:TH, :], rows).then_inc(s_parts.sem, 1)
                dve.tensor_copy(cum[:].rearrange(flat), C[1][:, 0:TH]).then_inc(s_cum.sem, 1)
                dve.wait_ge(s_parts.sem, s_parts.of(g, 1))
                dve.tensor_tensor(cum_rest[:, 0, :], rows, cum_parts[0:TH, :], ALU.subtract).then_inc(s_parts.sem, 1)
                dve.wait_ge(s_cum.sem, s_cum.of(g, 1))
                dve.tensor_tensor(to_end[:].rearrange(flat), C[1][:, TH:2 * TH], cum[:].rearrange(flat),
                                  ALU.subtract).then_inc(s_cum.sem, 1)
                dve.wait_ge(s_parts.sem, s_parts.of(g, 2))
                dve.tensor_copy(cum_mid[:], cum_rest[:, 0, :]).then_inc(s_parts.sem, 1)
                dve.wait_ge(s_parts.sem, s_parts.of(g, 3))
                dve.tensor_tensor(cum_rest[:, 1, :], cum_rest[:, 0, :], cum_mid[:], ALU.subtract).then_inc(s_parts.sem, 1)
                dve.tensor_copy(cum_parts[TH:2 * TH, :], cum_mid[:]).then_inc(s_parts.sem, 1)
                dve.wait_ge(s_parts.sem, s_parts.of(g, 4))
                dve.tensor_copy(cum_parts[2 * TH:3 * TH, :], cum_rest[:, 1, :]).then_inc(s_parts.sem, 1)
                dve.wait_ge(m_g.sem, m_g.of(g))
                dve.tensor_tensor(gm[:], C[0][:].rearrange("p (t l) -> p t l", t=TILES),
                                  le.unsqueeze(1).to_broadcast([P, TILES, P]), ALU.mult).then_inc(s_gm.sem, 1)
                dve.wait_ge(s_gm.sem, s_gm.of(g))

                def gate(t):
                    dve.wait_ge(m_y.sem, m_y.of(g, t + 1))
                    dve.wait_ge(s_skip.sem, s_skip.of(g, t + 1))
                    dve.tensor_tensor(yg[:, t, :], B[t % 2][:], y_off[:, t, :], ALU.add).then_inc(s_ysum.sem, 1)
                    dve.wait_ge(s_ysum.sem, s_ysum.of(g, t + 1))
                    dve.wait_ge(s_z.sem, s_z.of(g, t + 1))
                    dve.tensor_tensor(yg[:, t, :], yg[:, t, :], zs[:, t, :], ALU.mult).then_inc(s_yg.sem, 1)

                for t in range(TILES):
                    dve.wait_ge(s_decay.sem, s_decay.of(g, 2 * t + 2))
                    dve.tensor_tensor(m_s[:, t], m_s[:, t],
                                      gm[:, t, :].unsqueeze(1).to_broadcast([P, HEADS, P]), ALU.mult).then_inc(s_m.sem, 1)
                    dve.wait_ge(m_state.sem, m_state.of(g, t + 1))
                    dve.wait_ge(s_sdec.sem, s_sdec.of(g, t + 1))
                    dve.tensor_tensor(state[:, t + 1, :], C[1][0:STATE, :], state[:, t + 1, :], ALU.add).then_inc(s_state.sem, 1)
                    dve.wait_ge(m_off.sem, m_off.of(g, t + 1))
                    if t == 0:
                        dve.wait_ge(s_ecum.sem, s_ecum.of(g))
                    if g and t == 0:
                        dve.wait_ge(t_yg.sem, t_yg.of(g - 1))
                    if g and t == 0:
                        dve.wait_ge(s_sumsq.sem, s_sumsq.of(g - 1))
                    dve.tensor_tensor(per_head(y_off[:, t, :]), per_head(A[t % 2][:]),
                                      heads(e_cum[:, t, :]), ALU.mult).then_inc(s_yoff.sem, 1)
                    if t:
                        gate(t - 1)
                gate(TILES - 1)

            def block_out(g):
                dve.wait_ge(t_rstd.sem, t_rstd.of(g, 1))
                dve.wait_ge(s_res.sem, s_res.of(g))
                for t in range(TILES):
                    if t % 2 == 0:
                        dve.wait_ge(m_out.sem, m_out.of(g, t // 2 * 2 + 2))
                    if g and t == 0:
                        dve.wait_ge(s_xl.sem, s_xl.of(g - 1))
                    dve.scalar_tensor_tensor(out=x1[:, t, :], in0=half_bank(A, t),
                                             scalar=rstd[:, 2, t:t + 1], in1=res[:, t, :],
                                             op0=ALU.mult, op1=ALU.add).then_inc(s_x1.sem, 1)

            def attention_max(g):
                for t in range(TILES):
                    dve.wait_ge(m_sc.sem, m_sc.of(g, t + 1))
                    dve.tensor_reduce(neg_max[:, 0, t:t + 1], C[t % 2][:, 0:CTX], AX.X, ALU.max, negate=True).then_inc(s_max.sem, 1)

            def attention_out(g):
                for t in range(TILES):
                    dve.wait_ge(s_probs.sem, s_probs.of(g, t + 1))
                    dve.reciprocal(inv_sum[:, 0, t:t + 1], exp_sum[:, 0, t:t + 1]).then_inc(s_inv.sem, 1)
                for t in range(TILES):
                    dve.wait_ge(s_inv.sem, s_inv.of(g, t + 1))
                    if t % 2 == 0:
                        dve.wait_ge(m_att.sem, m_att.of(g, t // 2 * 2 + 2))
                    if g and t == 0:
                        dve.wait_ge(s_xf.sem, s_xf.of(g - 1))
                    dve.scalar_tensor_tensor(out=x2[:, t, :], in0=half_bank(A, t),
                                             scalar=inv_sum[:, 0, t:t + 1], in1=x1[:, t, :],
                                             op0=ALU.mult, op1=ALU.add).then_inc(s_x2.sem, 1)
                norm_stats(3, x2, g, s_x2, t_stats, t_mv, TILES)

            def choose(g):
                for t in range(TILES):
                    if t % 2 == 0:
                        dve.wait_ge(m_lg.sem, m_lg.of(g, t // 2 * 2 + 2))
                    dve.tensor_reduce(neg_max[:, 1, t:t + 1], logit(t), AX.X, ALU.max, negate=True).then_inc(s_max.sem, 1)
                for t in range(TILES):
                    dve.wait_ge(s_elg.sem, s_elg.of(g, t + 1))
                    dve.reciprocal(inv_sum[:, 1, t:t + 1], exp_sum[:, 1, t:t + 1]).then_inc(s_inv.sem, 1)
                for t in range(TILES):
                    dve.wait_ge(s_inv.sem, s_inv.of(g, TILES + t + 1))
                    dve.tensor_scalar(xf[:, t, D:], xf[:, t, D:], inv_sum[:, 1, t:t + 1], None, ALU.mult).then_inc(s_scores.sem, 1)
                for t in range(TILES):
                    dve.wait_ge(s_scores.sem, s_scores.of(g, t + 1))
                    dve.tensor_tensor(biased[:, t, 0:EXPERTS], xf[:, t, D:], gate_b_s[:], ALU.add).then_inc(s_biased.sem, 1)
                for t in range(TILES):
                    dve.wait_ge(s_biased.sem, s_biased.of(g, t + 1))
                    dve.max(top8[:, t, :], biased[:, t, 0:EXPERTS]).then_inc(s_top.sem, 1)
                for t in range(TILES):
                    dve.wait_ge(s_top.sem, s_top.of(g, t + 1))
                    dve.memset(top8[:, t, TOP:], FAR).then_inc(s_six.sem, 1)
                for t in range(TILES):
                    dve.wait_ge(s_six.sem, s_six.of(g, t + 1))
                    dve.match_replace(out=taken[:, t, :], in_to_replace=top8[:, t, :],
                                      in_values=biased[:, t, :], imm_value=-FAR).then_inc(s_taken.sem, 1)
                for t in range(TILES):
                    dve.wait_ge(s_taken.sem, s_taken.of(g, t + 1))
                    dve.tensor_tensor(chosen[:, t, :], taken[:, t, 0:EXPERTS], biased[:, t, 0:EXPERTS],
                                      ALU.not_equal).then_inc(s_chosen.sem, 1)
                if g:
                    dve.wait_ge(s_counts.sem, s_counts.of(g - 1))
                dve.tensor_copy(counts[:, 0, :], counts[:, TILES, :]).then_inc(s_counts.sem, 1)
                for t in range(TILES):
                    dve.wait_ge(s_chosen.sem, s_chosen.of(g, t + 1))
                    dve.wait_ge(s_counts.sem, s_counts.of(g, t + 1))
                    dve.tensor_tensor(counts[:, t + 1, :], counts[:, t, :], chosen[:, t, :], ALU.add).then_inc(s_counts.sem, 1)

            def shared_mult(g):
                for n, (lo, hi) in enumerate(SB):
                    dve.wait_ge(m_s3.sem, m_s3.of(g, n + 1))
                    dve.wait_ge(s_hs.sem, s_hs.of(g, n + 1))
                    dve.tensor_tensor(hs[0:hi - lo, n, :], B[n % 2][0:hi - lo, :], hs[0:hi - lo, n, :],
                                      ALU.mult).then_inc(s_hm.sem, 1)

            def place(g):
                for t in range(TILES):
                    if t % 2 == 0:
                        dve.wait_ge(m_rank.sem, m_rank.of(g, t // 2 * 2 + 2))
                    dve.scalar_tensor_tensor(out=fits[:, t, :], in0=rank(t), scalar=float(CAP),
                                             in1=chosen[:, t, :], op0=ALU.is_lt, op1=ALU.mult).then_inc(s_fits.sem, 1)
                    dve.scalar_tensor_tensor(out=key[:, t, :], in0=rank(t), scalar=-1.0,
                                             in1=cs[:, C_KEY:C_KEY + EXPERTS], op0=ALU.mult, op1=ALU.add).then_inc(s_fits.sem, 1)
                for t in range(TILES):
                    dve.wait_ge(s_fits.sem, s_fits.of(g, 2 * t + 2))
                    dve.tensor_tensor(key[:, t, :], key[:, t, :], fits[:, t, :], ALU.mult).then_inc(s_key.sem, 1)
                for t in range(TILES):
                    dve.wait_ge(s_key.sem, s_key.of(g, t + 1))
                    dve.max(top_key[:, t, :], key[:, t, :]).then_inc(s_order.sem, 1)
                if g:
                    dve.wait_ge(sent.sem, sent.of(g - 1))
                for t in range(TILES):
                    dve.wait_ge(s_order.sem, s_order.of(g, t + 1))
                    dve.tensor_scalar(slot_i[:, t, :], top_key[:, t, :], -1.0, float(KEY), ALU.mult, ALU.add).then_inc(s_slot.sem, 1)

            def layer_out(g):
                for t in range(TILES):
                    if t % 2 == 0:
                        dve.wait_ge(m_sh.sem, m_sh.of(g, t // 2 * 2 + 2))
                    if g and t == 0:
                        dve.wait_ge(o_out.sem, o_out.of(g - 1))
                    dve.tensor_tensor(o_s[:, t, :], half_bank(DD, t), x2[:, t, :], ALU.add).then_inc(s_o.sem, 1)

            def tail_and_front(g, f):
                if f is not None:
                    first_norm(f)
                block_out(g)
                if f is not None:
                    first_apply(f)
                norm_stats(2, x1, g, s_x1, t_stats, t_mv, 0)
                if f is not None:
                    norm_shift(1, 1, f, f_rstd, 2, f_shift)
                norm_shift(2, 3, g, t_rstd, 2, t_shift)
                attention_max(g)
                attention_out(g)
                if f is not None:
                    conv_taps(f, 0)
                norm_shift(3, 4, g, t_rstd, 3, t_shift)
                if f is not None:
                    conv_taps(f, 1)
                    conv_taps(f, 2)
                choose(g)
                if f is not None:
                    conv_taps(f, 3)
                shared_mult(g)
                if f is not None:
                    conv_taps(f, 4)
                place(g)
                layer_out(g)
                if f is not None:
                    dt_before(f)
                    dt_after(f)
                    inputs(f)

            rounds(front, scan, tail_and_front)

            active, e_rank = e_num[:, 1:2], e_num[:, 2:3]
            dve.wait_ge(m_cnt.sem, m_cnt.of(0, 1))
            dve.tensor_scalar(active, A[0][0:EXPERTS, 0:1], 1.0, None, ALU.min).then_inc(s_elist.sem, 1)
            dve.wait_ge(m_cnt.sem, m_cnt.of(0, 2))
            dve.tensor_copy(e_rank, A[1][0:EXPERTS, 0:1]).then_inc(s_elist.sem, 1)
            dve.wait_ge(s_elist.sem, s_elist.of(0, 2))
            dve.tensor_scalar(e_hot[:], cs[0:EXPERTS, C_IOTA:C_IOTA + EXPERTS], e_rank, active,
                              ALU.is_equal, ALU.mult).then_inc(s_elist.sem, 1)
            dve.wait_ge(m_cnt.sem, m_cnt.of(0, 3))
            n_act = B[0][0:1, 128:129]
            dve.memset(e_list[:, LIST:2 * LIST], float(EXPERTS)).then_inc(s_elist.sem, 1)
            dve.tensor_copy(e_list[:, 0:EXPERTS], B[0][0:1, 0:EXPERTS]).then_inc(s_elist.sem, 1)
            dve.wait_ge(s_elist.sem, s_elist.of(0, 5))
            dve.tensor_copy(e_list[:, 2 * LIST:], n_act).then_inc(s_elist.sem, 1)
            dve.wait_ge(s_elist.sem, s_elist.of(0, 6))
            dve.tensor_scalar(e_list[:, LIST:LIST + EXPERTS], iota[0:1, :],
                              e_list[:, 2 * LIST:], float(EXPERTS), ALU.is_ge, ALU.mult).then_inc(s_elist.sem, 1)
            dve.wait_ge(s_elist.sem, s_elist.of(0, 7))
            dve.tensor_tensor(e_list[:, LIST:LIST + EXPERTS], e_list[:, LIST:LIST + EXPERTS],
                              e_list[:, 0:EXPERTS], ALU.add).then_inc(s_elist.sem, 1)
            dve.wait_ge(s_elist.sem, s_elist.of(0, 8))
            dve.tensor_copy(e_list_i[:], e_list[:]).then_inc(s_elist.sem, 1)
            dve.wait_ge(slots_in.sem, slots_in.of(0))
            dve.tensor_copy(slots_f[:], slots_i[:]).then_inc(s_slots.sem, 1)
            dve.wait_ge(m_slots.sem, m_slots.of(0))
            dve.tensor_copy(slots_t[:], C[0][:, 0:EXPERTS + 1]).then_inc(s_slots.sem, 1)
            dve.wait_ge(s_elist.sem, s_elist.of(0))
            n_active = number_of(dve, slice(2 * LIST, 2 * LIST + 1), EXPERTS, 1)
            dve.sem_inc(s_hx.sem, BATCH)
            dve.sem_inc(s_yo.sem, BATCH)
            with dve.Fori(0, TURNS) as i:
                with dve.If(i * BATCH < n_active):
                    def product(q):
                        dve.wait_ge(s_h1.sem, s_h1.turn(i, q + 1))
                        dve.tensor_tensor(hx[:, q].rearrange("p c t -> p (c t)"), h1[:, q, :],
                                          B[q % 2][0:FH, 2 * P:], ALU.mult).then_inc(s_hx.sem, 1)

                    product(0)
                    for q in range(BATCH):
                        if q + 1 < BATCH:
                            product(q + 1)
                        e = number_of(dve, bass.ds(i * BATCH + q, 1), EXPERTS - 1)
                        dve.wait_ge(m_yo.sem, m_yo.turn(i, q + 1))
                        dve.wait_ge(landed.sem, landed.turn(i, q + 1 - BATCH))
                        dve.tensor_scalar(yo[:, q, :], C[q % 2][:, 0:D], xb[:, q, bass.ds(e + D, 1)], None,
                                          ALU.mult).then_inc(s_yo.sem, 1)
                with dve.Else():
                    dve.nop()

        @block.tensor
        def _(pe):

            def blocks(src, dst, n):
                for k in range(n):
                    ins = pe.transpose(dst[:, k * P:(k + 1) * P], src[:, k * P:(k + 1) * P], ident)
                return ins

            def turn_in(g):
                if g == 0:
                    pe.wait_ge(s_const.sem, s_const.of(0))
                for t in range(TILES):
                    pe.wait_ge(s_xh.sem, s_xh.of(g, t + 1))
                    if g and t == 0:
                        pe.wait_ge(s_drop.sem, s_drop.of(g - 1))
                    if t >= 2:
                        pe.wait_ge(s_xnt.sem, s_xnt.of(g, t - 1))
                    blocks(xh[:, t, :], DD[t % 2], KD).then_inc(t_xh.sem, 1)

            def project_z(g, tiles=range(TILES)):
                if g == 0:
                    pe.wait_ge(s_weights.sem, s_weights.of(0))
                for t in tiles:
                    if t < 2:
                        pe.wait_ge(s_xnt.sem, s_xnt.of(g, min(t + 3, TILES)))
                    if t >= 2:
                        pe.wait_ge(s_z.sem, s_z.of(g, t - 1))
                    for k in range(KD):
                        ins = pe.matmul(DD[t % 2][:], xnt[:, k, t * P:(t + 1) * P], w_in_s[:, k, 0:INNER],
                                        start=(k == 0), stop=(k == KD - 1))
                    ins.then_inc(m_z.sem, 1)

            def project_x(g, c):
                if c < 2:
                    pe.wait_ge(s_z.sem, s_z.of(g, min(c + 3, TILES)))
                if c >= 2:
                    pe.wait_ge(s_raw.sem, s_raw.of(g, c - 1))
                for k in range(KD):
                    ins = pe.matmul(DD[c % 2][:], w_in_s[:, k, INNER + c * P:INNER + (c + 1) * P],
                                    xnt[:, k, :], start=(k == 0), stop=(k == KD - 1))
                ins.then_inc(m_x.sem, 1)

            def project_dt(g):
                if g:
                    pe.wait_ge(s_fits.sem, s_fits.of(g - 1))
                for t in range(TILES):
                    for k in range(KD):
                        ins = pe.matmul(C[0][:, t * HEADS:(t + 1) * HEADS], xnt[:, k, t * P:(t + 1) * P],
                                        w_in_s[:, k, PROJ - HEADS:], start=(k == 0), stop=(k == KD - 1))
                ins.then_inc(m_dt.sem, 1)

            def token_major(g):
                if g == 0:
                    pe.wait_ge(s_raw.sem, s_raw.of(g))
                for t in range(TILES):
                    if t == 0:
                        pe.wait_ge(s_conv.sem, s_conv.of(g, CB - 1))
                    if t >= 2:
                        pe.wait_ge(s_xs.sem, s_xs.of(g, t - 1))
                    for c in range(INNER // P):
                        ins = pe.transpose(DD[t % 2][:, c * P:(c + 1) * P], conv[:, c, t * P:(t + 1) * P], ident)
                    ins.then_inc(t_x.sem, 1)
                pe.wait_ge(s_conv.sem, s_conv.of(g))
                pe.wait_ge(s_dtv.sem, s_dtv.of(g, 1))
                for t in range(TILES):
                    ins = pe.transpose(C[0][:, t * STATE:(t + 1) * STATE], conv[0:STATE, CB - 1, t * P:(t + 1) * P],
                                       ident[0:STATE, 0:STATE])
                ins.then_inc(t_b.sem, 1)

            def front(g):
                turn_in(g)
                project_z(g)
                for c in range(CB):
                    project_x(g, c)
                project_dt(g)
                token_major(g)

            def scan(g):
                pe.wait_ge(s_dt.sem, s_dt.of(g))
                a_all = a_s[:].rearrange(flat)
                pe.matmul(C[1][:, 0:TH], le, a_all, start=True, stop=True).then_inc(m_cum.sem, 1)
                pe.matmul(C[1][:, TH:2 * TH], ones, a_all, start=True, stop=True).then_inc(m_cum.sem, 1)
                pe.matmul(C[1][0:TH, 2 * TH:2 * TH + P], a_all, le, start=True, stop=True).then_inc(m_cum.sem, 1)
                pe.wait_ge(c_moved.sem, c_moved.of(g))
                pe.wait_ge(s_btok.sem, s_btok.of(g))
                for t in range(TILES):
                    ins = pe.matmul(C[0][:, t * P:(t + 1) * P], conv[0:STATE, CB - 1, t * P:(t + 1) * P],
                                    c_t[:, t * P:(t + 1) * P], start=True, stop=True)
                ins.then_inc(m_g.sem, 1)

                def rows(t):
                    for half in range(2):
                        if t == 0:
                            if t == 0 and half == 0:
                                pe.wait_ge(s_xs.sem, s_xs.of(g))
                        else:
                            pe.wait_ge(s_drop.sem, s_drop.of(g, 2 * t - 1 + half))
                        for j in range(HEADS // 2):
                            h = t * HEADS + half * (HEADS // 2) + j
                            ins = pe.matmul(DD[half][:, j * P:(j + 1) * P], pick_s[:, h, :], cum_parts[:],
                                            start=True, stop=True)
                        ins.then_inc(m_rows.sem, 1)

                pe.wait_ge(s_parts.sem, s_parts.of(g))
                rows(0)
                for t in range(TILES):
                    pe.wait_ge(s_state.sem, s_state.of(g, t + 1))
                    if g and t == 0:
                        pe.wait_ge(s_hs.sem, s_hs.of(g - 1))
                    if t >= 2:
                        pe.wait_ge(s_yoff.sem, s_yoff.of(g, t - 1))
                    pe.matmul(A[t % 2][:], c_t[:, t * P:(t + 1) * P], state[:, t, :], start=True, stop=True).then_inc(m_off.sem, 1)
                    pe.wait_ge(s_xdec.sem, s_xdec.of(g, t + 1))
                    if t == 0:
                        pe.wait_ge(s_ecum.sem, s_ecum.of(g))
                    if t == 0:
                        pe.wait_ge(s_cum.sem, s_cum.of(g))
                    pe.matmul(C[1][0:STATE, :], b_tok[:, t, :], xdec[:, t, :], start=True, stop=True).then_inc(m_state.sem, 1)
                    if t + 1 < TILES:
                        rows(t + 1)
                    pe.wait_ge(s_m.sem, s_m.of(g, t + 1))
                    pe.wait_ge(s_xdt.sem, s_xdt.of(g, t + 1))
                    if t >= 2:
                        pe.wait_ge(s_ysum.sem, s_ysum.of(g, t - 1))
                    for h in range(HEADS):
                        ins = pe.matmul(B[t % 2][:, h * HEAD:(h + 1) * HEAD], m_s[:, t, h, :],
                                        xdt[:, t, h * HEAD:(h + 1) * HEAD], start=True, stop=True)
                    ins.then_inc(m_y.sem, 1)

            def block_out(g):
                if g == 0:
                    pe.wait_ge(s_wout.sem, s_wout.of(0))
                for t in range(TILES):
                    pe.wait_ge(s_yg.sem, s_yg.of(g, t + 1))
                    if t < 2:
                        pe.wait_ge(s_ysum.sem, s_ysum.of(g, min(t + 3, TILES)))
                    blocks(yg[:, t, :], B[t % 2], INNER // P).then_inc(t_yg.sem, 1)
                    pe.wait_ge(s_ygt.sem, s_ygt.of(g, t + 1))
                    if t == 0:
                        pe.wait_ge(s_yoff.sem, s_yoff.of(g))
                    for k in range(INNER // P):
                        ins = pe.matmul(half_bank(A, t), yg_t[:, t % 2, k, :], w_out_s[:, k, :],
                                        start=(k == 0), stop=(k == INNER // P - 1))
                    ins.then_inc(m_out.sem, 1)

            def scores(g):
                pe.wait_ge(ctx_loaded.sem, ctx_loaded.of(g))
                for t in range(TILES):
                    pe.wait_ge(s_xl.sem, s_xl.of(g, t + 1))
                    blocks(xl[:, t, :], B[t % 2], KD).then_inc(t_xl.sem, 1)
                    pe.wait_ge(s_xlt.sem, s_xlt.of(g, t + 1))
                    if t == 0:
                        pe.wait_ge(s_gm.sem, s_gm.of(g))
                    if t == 0:
                        pe.wait_ge(s_state.sem, s_state.of(g))
                    if t >= 2:
                        pe.wait_ge(s_probs.sem, s_probs.of(g, t - 1))
                    for k in range(KD):
                        ins = pe.matmul(C[t % 2][:, 0:CTX], xl_t[:, t % 2, k, :], ctx_t_s[:, k, :],
                                        start=(k == 0), stop=(k == KD - 1))
                    ins.then_inc(m_sc.sem, 1)

            def turn_probs(g):
                for t in range(TILES):
                    if t >= 2:
                        pe.wait_ge(s_probs.sem, s_probs.of(g, t + 1))
                    if t >= 2:
                        pe.wait_ge(s_prt.sem, s_prt.of(g, t - 1))
                    pe.transpose(B[t % 2][0:CTX, 0:P], probs[:, t, :], ident).then_inc(t_pr.sem, 1)

            def attend(g):
                for t in range(TILES):
                    if t >= 2:
                        pe.wait_ge(s_prt.sem, s_prt.of(g, t + 1))
                    if t == 0:
                        pe.wait_ge(s_x1.sem, s_x1.of(g))
                    pe.matmul(half_bank(A, t), probs_t[:, t, :], ctx_s[:], start=True, stop=True).then_inc(m_att.sem, 1)

            def turn_xf(g):
                for t in range(TILES):
                    pe.wait_ge(s_xf.sem, s_xf.of(g, t + 1))
                    if t >= 2:
                        pe.wait_ge(s_xft.sem, s_xft.of(g, t - 1))
                    blocks(xf[:, t, :], B[t % 2], KD).then_inc(t_xf.sem, 1)

            def logits(g):
                for t in range(TILES):
                    if t >= 2:
                        pe.wait_ge(s_xft.sem, s_xft.of(g, t + 1))
                    for k in range(KD):
                        ins = pe.matmul(logit(t), xf_t[:, k, t * P:(t + 1) * P], gate_s[:, k, :],
                                        start=(k == 0), stop=(k == KD - 1))
                    ins.then_inc(m_lg.sem, 1)

            def shared_in(g):
                if g == 0:
                    pe.wait_ge(s_shared.sem, s_shared.of(0))
                for n, (lo, hi) in enumerate(SB):
                    if n == 0:
                        pe.wait_ge(s_x2.sem, s_x2.of(g))
                    if n >= 2:
                        pe.wait_ge(s_hs.sem, s_hs.of(g, n - 1))
                    for k in range(KD):
                        ins = pe.matmul(A[n % 2][0:hi - lo, :], ws1_s[:, k, lo:hi], xf_t[:, k, :],
                                        start=(k == 0), stop=(k == KD - 1))
                    ins.then_inc(m_s1.sem, 1)
                    if n >= 2:
                        pe.wait_ge(s_hm.sem, s_hm.of(g, n - 1))
                    for k in range(KD):
                        ins = pe.matmul(B[n % 2][0:hi - lo, :], ws3_s[:, k, lo:hi], xf_t[:, k, :],
                                        start=(k == 0), stop=(k == KD - 1))
                    ins.then_inc(m_s3.sem, 1)

            def ranks(g):
                if g == 0:
                    pe.wait_ge(s_small.sem, s_small.of(0))
                for t in range(TILES):
                    pe.wait_ge(s_chosen.sem, s_chosen.of(g, t + 1))
                    pe.wait_ge(s_counts.sem, s_counts.of(g, t + 1))
                    if t == 0:
                        pe.wait_ge(s_elg.sem, s_elg.of(g))
                    pe.matmul(rank(t), lt_b[:], chosen[:, t, :], start=True, stop=False)
                    pe.matmul(rank(t), ones_b[:], counts[:, t, :],
                              start=False, stop=True).then_inc(m_rank.sem, 1)

            def shared_out(g):
                for t in range(TILES):
                    if t == 0:
                        pe.wait_ge(s_hm.sem, s_hm.of(g))
                    if g and t == 0:
                        pe.wait_ge(s_drop.sem, s_drop.of(g))
                    if g + 1 < GROUPS:
                        if t == 0:
                            pe.wait_ge(s_raw.sem, s_raw.of(g + 1))
                    for n, (lo, hi) in enumerate(SB):
                        ins = pe.matmul(half_bank(DD, t), hs[0:hi - lo, n, t * P:(t + 1) * P],
                                        ws2_s[0:hi - lo, n, :], start=(n == 0), stop=(n == len(SB) - 1))
                    ins.then_inc(m_sh.sem, 1)

            def tail_and_front(g, f):
                block_out(g)
                if f is not None:
                    turn_in(f)
                scores(g)
                if f is not None:
                    project_z(f, (0, 1))
                turn_probs(g)
                if f is not None:
                    project_z(f, (2, 3))
                attend(g)
                if f is not None:
                    project_x(f, 0)
                if f is not None:
                    project_x(f, 1)
                    project_x(f, 2)
                turn_xf(g)
                if f is not None:
                    project_x(f, 3)
                logits(g)
                if f is not None:
                    project_x(f, 4)
                shared_in(g)
                ranks(g)
                shared_out(g)
                if f is not None:
                    pe.wait_ge(s_o.sem, s_o.of(g))
                    project_dt(f)
                    token_major(f)

            rounds(front, scan, tail_and_front)

            pe.wait_ge(s_hs.sem, s_hs.of(GROUPS - 1))
            pe.matmul(A[0][0:EXPERTS, 0:1], counts[:, TILES, :], ones_b[:, 0:1], start=True, stop=True).then_inc(m_cnt.sem, 1)
            pe.wait_ge(s_elist.sem, s_elist.of(0, 1))
            pe.matmul(A[1][0:EXPERTS, 0:1], lt[0:EXPERTS, 0:EXPERTS], e_num[:, 1:2], start=True, stop=True).then_inc(m_cnt.sem, 1)
            pe.wait_ge(s_elist.sem, s_elist.of(0, 3))
            pe.matmul(B[0][0:1, 0:EXPERTS], cs[0:EXPERTS, C_PART:C_PART + 1], e_hot[:], start=True, stop=True)
            pe.matmul(B[0][0:1, 128:129], ones[0:EXPERTS, 0:1], e_num[:, 1:2], start=True, stop=True).then_inc(m_cnt.sem, 1)
            pe.wait_ge(s_slots.sem, s_slots.of(0, 1))
            pe.wait_ge(s_fits.sem, s_fits.of(GROUPS - 1))
            pe.transpose(C[0][:, 0:EXPERTS + 1], slots_f[:], ident[0:EXPERTS + 1, 0:EXPERTS + 1]).then_inc(m_slots.sem, 1)

            pe.wait_ge(s_elist.sem, s_elist.of(0))
            n_active = number_of(pe, slice(2 * LIST, 2 * LIST + 1), EXPERTS, 1)
            pe.sem_inc(m_yo.sem, BATCH)
            with pe.Fori(0, TURNS) as i:
                with pe.If(i * BATCH < n_active):
                    def rows_in(q):
                        pe.wait_ge(xb_in[q].sem, xb_in[q].turn(i))
                        pe.wait_ge(s_xbt.sem, s_xbt.turn(i, q - 1))
                        for k in range(KD):
                            ins = pe.transpose(A[q % 2][:, k * P:(k + 1) * P], xb[:, q, k * P:(k + 1) * P], ident)
                        ins.then_inc(t_xb.sem, 1)

                    def down(q):
                        pe.wait_ge(s_hx.sem, s_hx.turn(i, q + 1))
                        pe.wait_ge(s_yo.sem, s_yo.turn(i, q - 1))
                        for c in range(2):
                            ins = pe.matmul(C[q % 2][:, 0:D], hx[:, q, c, :], w2_s[:, q, c, :],
                                            start=(c == 0), stop=(c == 1))
                        ins.then_inc(m_yo.sem, 1)

                    rows_in(0)
                    for q in range(BATCH):
                        if q + 1 < BATCH:
                            rows_in(q + 1)
                        pe.wait_ge(s_xbt.sem, s_xbt.turn(i, q + 1))
                        pe.wait_ge(w_in_e[q].sem, w_in_e[q].turn(i))
                        pe.wait_ge(s_hx.sem, s_hx.turn(i, q - 1))
                        for m in range(2):
                            for c in range(2):
                                lo = m * FF + c * FH
                                for k in range(KD):
                                    ins = pe.matmul(B[q % 2][0:FH, (2 * m + c) * P:(2 * m + c + 1) * P],
                                                    w13_s[:, q, k, lo:lo + FH], xb_t[:, q, k, :],
                                                    start=(k == 0), stop=(k == KD - 1))
                        ins.then_inc(m_h.sem, 1)
                        if q:
                            down(q - 1)
                    down(BATCH - 1)
                with pe.Else():
                    pe.nop()


def kernel(x, ctx_1024, L0_attn_ln_w, L0_attn_ln_b, L0_attn_in_proj_w, L0_attn_conv_w, L0_attn_conv_b,
           L0_attn_dt_bias, L0_attn_A_log, L0_attn_D_skip, L0_attn_norm_w, L0_attn_out_proj_w, L0_ffn_gate_w,
           L0_ffn_gate_b, L0_ffn_w1, L0_ffn_w2, L0_ffn_w3, L0_ffn_ws1, L0_ffn_ws2, L0_ffn_ws3):
    import ml_dtypes

    import concourse.bacc as _bacc
    from concourse.bass_utils import run_bass_kernel_spmd as _run

    def lay(a):
        return np.ascontiguousarray(np.asarray(a))

    def on_partitions(a):
        a = np.asarray(a)
        return lay(np.swapaxes(a.reshape((a.shape[0] // P, P) + a.shape[1:]), 0, 1))

    ctx_rows = np.asarray(ctx_1024)
    of_group = np.arange(GROUPS) * GROUP // SEQ
    w13 = np.concatenate([np.asarray(L0_ffn_w1), np.asarray(L0_ffn_w3)], axis=1)
    arrays = {
        "x": lay(np.asarray(x).reshape(TOKENS, D)),
        "cst": constants(),
        "picks": row_pickers().astype(ml_dtypes.bfloat16),
        "lnwb": lay(np.stack([on_partitions(L0_attn_ln_w), on_partitions(L0_attn_ln_b)], axis=1)),
        "w_in": on_partitions(np.asarray(L0_attn_in_proj_w).T),
        "conv_w": on_partitions(np.asarray(L0_attn_conv_w)[:, 0, :]),
        "conv_b": on_partitions(L0_attn_conv_b),
        "rows8": lay(np.broadcast_to(np.stack([np.asarray(L0_attn_dt_bias), np.asarray(L0_attn_A_log)])[None],
                                     (P, 2, HEADS))),
        "rows_d": lay(np.broadcast_to(np.repeat(np.asarray(L0_attn_D_skip), HEAD)[None], (P, INNER))),
        "norm_w": on_partitions(L0_attn_norm_w),
        "w_out": on_partitions(np.asarray(L0_attn_out_proj_w).T),
        "ctx_in": lay(ctx_rows[of_group]),
        "ctx_t": lay(ctx_rows.transpose(0, 2, 1).reshape(2, KD, P, CTX).transpose(0, 2, 1, 3)[of_group]),
        "gate_t": on_partitions(np.asarray(L0_ffn_gate_w).T),
        "gate_b": lay(np.broadcast_to(np.asarray(L0_ffn_gate_b)[None], (P, EXPERTS))),
        "w13": lay(w13.transpose(0, 2, 1).reshape(EXPERTS, KD, P, 2 * FF).transpose(0, 2, 1, 3)),
        "w2": lay(np.asarray(L0_ffn_w2).transpose(0, 2, 1)),
        "ws1": on_partitions(np.asarray(L0_ffn_ws1).T),
        "ws3": on_partitions(np.asarray(L0_ffn_ws3).T),
        "ws2": lay(np.asarray(L0_ffn_ws2).T),
    }
    nc = _bacc.Bacc("TRN2", target_bir_lowering=False, num_devices=1)
    args = [nc.dram_tensor(name, a.shape, mybir.dt.from_np(a.dtype), kind="ExternalInput").ap()
            for name, a in arrays.items()]
    out = nc.dram_tensor("out", (TOKENS, D), F32, kind="ExternalOutput").ap()
    decoder_layer(nc, *args, out)
    r = _run(nc, [arrays], core_ids=[0])
    return r.results[0]["out"].reshape(2, SEQ, D)
```

```python
from contextlib import ExitStack

import numpy as np

import concourse.bass as bass
from concourse import mybir

F32 = mybir.dt.float32
I32 = mybir.dt.int32
U32 = mybir.dt.uint32
BF16 = mybir.dt.bfloat16
ALU = mybir.AluOpType
ACT = mybir.ActivationFunctionType
AX = mybir.AxisListType

P = 128
TOKENS, D = 2048, 256
SEQ = 1024
KD = D // P
TILES = 4
GROUP = TILES * P
GROUPS = TOKENS // GROUP
INNER, STATE, HEADS, HEAD = 512, 64, 8, 64
CONV_DIM, TAPS = INNER + 2 * STATE, 4
CB = CONV_DIM // P
PROJ = 2 * INNER + 2 * STATE + HEADS
CTX = 77
EXPERTS, TOP, CAP, FF = 64, 6, 128, 176
FH = FF // 2
SHARED = 2 * FF
SB = [(0, 128), (128, 256), (256, SHARED)]
EPS = 1e-5
BATCH = 4
FAR = -3.0e38
NOWHERE = 1 << 20
ATANH = [1.0 / 17, 1.0 / 15, 1.0 / 13, 1.0 / 11, 1.0 / 9, 1.0 / 7, 1.0 / 5, 1.0 / 3]

C_ID, C_LE, C_LT, C_ONE, C_IOTA, C_TOK, C_CARRY, C_PART, C_KEY = 0, 128, 256, 384, 512, 576, 592, 596, 600
C_ALL = C_KEY + EXPERTS
KEY = 2 * EXPERTS * CAP


def constants():
    c = np.zeros((P, C_ALL), np.float32)
    i = np.arange(P)
    c[:, C_ID:C_ID + P] = i[:, None] == i[None, :]
    c[:, C_LE:C_LE + P] = i[:, None] <= i[None, :]
    c[:, C_LT:C_LT + P] = i[:, None] < i[None, :]
    c[:, C_ONE:C_ONE + P] = 1.0
    c[:, C_IOTA:C_IOTA + EXPERTS] = np.arange(EXPERTS)[None, :]
    c[:, C_TOK:C_TOK + TOKENS // P] = i[:, None] + P * np.arange(TOKENS // P)[None, :]
    c[:, C_CARRY:C_CARRY + GROUPS] = (np.arange(GROUPS) * GROUP % SEQ != 0)[None, :]
    c[:, C_PART] = i
    c[:, C_KEY:C_KEY + EXPERTS] = KEY - CAP * np.arange(EXPERTS)[None, :]
    return c


def row_pickers():
    r = np.arange(3 * TILES * HEADS) % (TILES * HEADS)
    pick = r[:, None] == np.arange(TILES * HEADS)[None, :]
    return np.ascontiguousarray(np.broadcast_to(pick[:, :, None], (len(r), TILES * HEADS, P)))


class Signal:

    def __init__(self, nc, ctx, name, per, unit=1, ahead=0):
        self.sem, self.per, self.unit, self.ahead = ctx.enter_context(nc.semaphore(name)), per, unit, ahead

    def of(self, g, k=None):
        return (g * self.per + (self.per if k is None else k)) * self.unit

    def turn(self, i, k=None):
        k = self.per if k is None else k
        return i * (self.per * self.unit) + (k + self.ahead) * self.unit


def decoder_layer(nc, x, cst, picks, lnwb, w_in, conv_w, conv_b, rows8, skip_w, norm_w, w_out, ctx_in, ctx_t,
                  gate_t, gate_b, w13, w2, ws1, ws3, ws2, out):
    ROW = D + EXPERTS
    xf_dram = nc.dram_tensor("xf_scratch", (TOKENS, ROW), F32, kind="Internal").ap()
    slots = nc.dram_tensor("slot_table", ((EXPERTS + 1) * CAP, 1), I32, kind="Internal").ap()
    x_v = x.rearrange("(g t p) d -> g p t d", p=P, t=TILES)
    xf_v = xf_dram.rearrange("(g t p) d -> g p t d", p=P, t=TILES)
    out_v = out.rearrange("(g t p) d -> g p t d", p=P, t=TILES)
    TH = TILES * HEADS
    LIST = EXPERTS + BATCH

    with ExitStack() as ctx:
        def sb(name, shape, dt=F32):
            return ctx.enter_context(nc.sbuf_tensor(name, shape, dt))

        def signal(name, per, unit=1, ahead=0):
            return Signal(nc, ctx, name, per, unit, ahead)

        bank = [ctx.enter_context(nc.psum_tensor(f"bank{i}", [P, 512], F32)) for i in range(8)]
        A, B, C, DD = bank[0:2], bank[2:4], bank[4:6], bank[6:8]

        cs = sb("cs", [P, C_ALL])
        ident, le, lt, ones = (cs[:, c:c + P] for c in (C_ID, C_LE, C_LT, C_ONE))
        iota = cs[:, C_IOTA:C_IOTA + EXPERTS]
        lt_b = sb("lt_b", [P, P], BF16)
        ones_b = sb("ones_b", [P, P], BF16)
        pick_s = sb("pick_s", [3 * TH, TH, P], BF16)
        tok_i = sb("tok_i", [P, TOKENS // P], I32)
        lnwb_s = sb("lnwb_s", [P, 2, KD])
        w_in_s = sb("w_in_s", [P, KD, PROJ])
        conv_w_s = sb("conv_w_s", [P, CB, TAPS])
        conv_b_s = sb("conv_b_s", [P, CB])
        rows8_s = sb("rows8_s", [P, 2, HEADS])
        neg_a = sb("neg_a", [P, HEADS])
        skip_w_s = sb("skip_w_s", [P, INNER // P])
        skip_diag = sb("skip_diag", [P, INNER // P, P])
        norm_w_s = sb("norm_w_s", [P, INNER // P])
        w_out_s = sb("w_out_s", [P, INNER // P, D])
        gate_s = sb("gate_s", [P, KD, EXPERTS])
        gate_b_s = sb("gate_b_s", [P, EXPERTS])
        ws1_s = sb("ws1_s", [P, KD, SHARED])
        ws3_s = sb("ws3_s", [P, KD, SHARED])
        ws2_s = sb("ws2_s", [P, len(SB), D])
        minus_half = sb("minus_half", [P, TILES])
        blank = sb("blank", [P, EXPERTS + 1], I32)

        x_s = sb("x_s", [P, TILES, D])
        y1 = sb("y1", [P, TILES, D])
        res = sb("res", [P, TILES, D])
        xh = sb("xh", [P, TILES, D])
        stats = sb("stats", [P, 4, TILES, 6])
        mv = sb("mv", [P, 4, TILES, 2])
        var_eps = sb("var_eps", [P, 5, TILES])
        rstd = sb("rstd", [P, 5, TILES])
        xnt = sb("xnt", [P, KD, GROUP])
        zs = sb("zs", [P, TILES, INNER])
        raw = sb("raw", [P, CB, GROUP + TAPS - 1])
        conv = sb("conv", [P, CB, GROUP])
        c_t = sb("c_t", [STATE, GROUP])
        dt_v, dt_abs, dt_u, dt_den, dt_s, dt_q, dt_p, dt_relu = (
            sb(f"dt_{n}", [P, TH]) for n in ("v", "abs", "u", "den", "s", "q", "p", "relu"))
        dt = sb("dt", [P, TILES, HEADS])
        a_s = sb("a_s", [P, TILES, HEADS])
        xs = sb("xs", [P, TILES, INNER])
        b_tok = sb("b_tok", [P, TILES, STATE])
        xdt = sb("xdt", [P, TILES, INNER])
        cum = sb("cum", [P, TILES, HEADS])
        to_end = sb("to_end", [P, TILES, HEADS])
        e_cum = sb("e_cum", [P, TILES, HEADS])
        e_end = sb("e_end", [P, TILES, HEADS])
        e_tot = sb("e_tot", [P, TILES, HEADS])
        cum_parts = sb("cum_parts", [3 * TH, P], BF16)
        cum_mid = sb("cum_mid", [TH, P], BF16)
        cum_rest = sb("cum_rest", [TH, 2, P])
        xdec = sb("xdec", [P, TILES, INNER])
        gm = sb("gm", [P, TILES, P])
        m_s = sb("m_s", [P, TILES, HEADS, P])
        state = sb("state", [STATE, TILES + 1, INNER])
        y_off = sb("y_off", [P, TILES, INNER])
        yg = y_off
        square = sb("square", [P, INNER])
        sumsq = sb("sumsq", [P, TILES])
        yg_t = sb("yg_t", [P, 2, INNER // P, P])
        x1 = sb("x1", [P, TILES, D])
        xl = sb("xl", [P, TILES, D])
        xl_t = sb("xl_t", [P, 2, KD, P])
        ctx_s = sb("ctx_s", [CTX, D])
        ctx_t_s = sb("ctx_t_s", [P, KD, CTX])
        neg_max = sb("neg_max", [P, 2, TILES])
        exp_sum = sb("exp_sum", [P, 2, TILES])
        inv_sum = sb("inv_sum", [P, 2, TILES])
        probs = sb("probs", [P, TILES, CTX])
        probs_t = sb("probs_t", [CTX, TILES, P])
        x2 = sb("x2", [P, TILES, D])
        xf = sb("xf", [P, TILES, ROW])
        xf_t = sb("xf_t", [P, KD, GROUP])
        biased = sb("biased", [P, TILES, EXPERTS + 2])
        top8 = sb("top8", [P, TILES, 8])
        taken = sb("taken", [P, TILES, EXPERTS + 2])
        chosen = sb("chosen", [P, TILES, EXPERTS], BF16)
        counts = sb("counts", [P, TILES + 1, EXPERTS], BF16)
        fits = sb("fits", [P, TILES, EXPERTS])
        key = sb("key", [P, TILES, EXPERTS])
        top_key = sb("top_key", [P, TILES, 8])
        slot_i = sb("slot_i", [P, TILES, 8], I32)
        hs = sb("hs", [P, len(SB), GROUP])
        o_s = sb("o_s", [P, TILES, D])

        e_num = sb("e_num", [EXPERTS, 4])
        e_hot = sb("e_hot", [EXPERTS, EXPERTS])
        e_list = sb("e_list", [1, 2 * LIST + 1])
        e_list_i = sb("e_list_i", [1, 2 * LIST + 1], I32)
        slots_i = sb("slots_i", [EXPERTS + 1, CAP], I32)
        slots_f = sb("slots_f", [EXPERTS + 1, CAP])
        slots_t = sb("slots_t", [P, EXPERTS + 1], I32)
        weight = sb("weight", [P, BATCH])
        tab_g = sb("tab_g", [P, BATCH, 1], I32)
        tab_s = sb("tab_s", [P, BATCH, 1], I32)

        def over(tensor, name, shape):
            axes = " ".join("abc"[:len(tensor.shape) - 1])
            flat = tensor[:].rearrange(f"p {axes} -> p ({axes})")
            size = int(np.prod(shape[1:]))
            names = " ".join("abcd"[:len(shape) - 1])
            return flat[0:shape[0], 0:size].rearrange(f"p ({names}) -> p {names}",
                                                      **dict(zip("abcd", shape[1:])))

        xb = over(y_off, "xb", [P, BATCH, ROW])
        xb_t = over(xdec, "xb_t", [P, BATCH, KD, P])
        w13_s = over(m_s, "w13_s", [P, BATCH, KD, 2 * FF])
        w2_s = over(raw, "w2_s", [FH, BATCH, 2, D])
        h1 = over(xdt, "h1", [FH, BATCH, 2 * P])
        hx = over(xs, "hx", [FH, BATCH, 2, P])
        yo = over(zs, "yo", [P, BATCH, D])

        s_const = signal("s_const", 1, 16)
        s_weights = signal("s_weights", 11, 16)
        s_shared = signal("s_shared", 5, 16)
        s_blank = signal("s_blank", 1)
        s_table = signal("s_table", 1, 16)
        s_zero = signal("s_zero", 3)
        s_small = signal("s_small", 3)
        s_exp_a = signal("s_exp_a", 1)
        s_wt = signal("s_wt", BATCH)
        s_wout = signal("s_wout", INNER // P + 1)
        s_half = signal("s_half", 1)

        x_in = signal("x_in", 1, 16)
        f_stats = signal("f_stats", 2 * TILES)
        f_mv = signal("f_mv", 2 * TILES)
        f_var = signal("f_var", 2)
        f_rstd = signal("f_rstd", 2)
        s_y1 = signal("s_y1", TILES)
        s_res = signal("s_res", 1)
        s_xh = signal("s_xh", TILES)
        t_xh = signal("t_xh", TILES)
        s_xnt = signal("s_xnt", TILES)
        m_z = signal("m_z", TILES)
        s_z = signal("s_z", TILES)
        m_dt = signal("m_dt", 1)
        m_x = signal("m_x", CB)
        s_halo = signal("s_halo", 1)
        s_raw = signal("s_raw", CB)
        s_tap = signal("s_tap", CB * (TAPS - 1))
        s_conv = signal("s_conv", CB)
        c_moved = signal("c_moved", 1, 16)
        s_dtv = signal("s_dtv", 3)
        s_u = signal("s_u", 1)
        s_sq = signal("s_sq", 4)
        s_poly = signal("s_poly", len(ATANH) + 1)
        s_dt = signal("s_dt", 2)
        t_x = signal("t_x", TILES)
        t_b = signal("t_b", 1)
        s_xs = signal("s_xs", TILES)
        s_btok = signal("s_btok", 1)
        s_xdt = signal("s_xdt", TILES)
        m_cum = signal("m_cum", 3)
        s_cum = signal("s_cum", 2)
        s_parts = signal("s_parts", 6)
        s_ecum = signal("s_ecum", 3)
        s_diag = signal("s_diag", INNER // P)
        s_xdec = signal("s_xdec", TILES)
        m_g = signal("m_g", 1)
        s_gm = signal("s_gm", 1)
        m_rows = signal("m_rows", 2 * TILES)
        s_drop = signal("s_drop", 2 * TILES)
        s_decay = signal("s_decay", 2 * TILES)
        s_m = signal("s_m", TILES)
        m_y = signal("m_y", TILES)
        m_off = signal("m_off", TILES)
        m_state = signal("m_state", TILES)
        s_sdec = signal("s_sdec", TILES)
        s_state = signal("s_state", TILES + 1)
        s_yoff = signal("s_yoff", TILES)
        s_ysum = signal("s_ysum", TILES)
        s_yg = signal("s_yg", TILES)
        ctx_loaded = signal("ctx_loaded", 2, 16)
        s_sumsq = signal("s_sumsq", TILES)
        t_yg = signal("t_yg", TILES)
        s_ygt = signal("s_ygt", TILES)
        m_out = signal("m_out", TILES)
        t_stats = signal("t_stats", 2 * TILES)
        t_mv = signal("t_mv", 2 * TILES)
        t_var = signal("t_var", 3)
        t_rstd = signal("t_rstd", 3)
        s_x1 = signal("s_x1", TILES)
        s_xl = signal("s_xl", TILES)
        t_xl = signal("t_xl", TILES)
        s_xlt = signal("s_xlt", TILES)
        m_sc = signal("m_sc", TILES)
        s_max = signal("s_max", 2 * TILES)
        s_probs = signal("s_probs", TILES)
        s_inv = signal("s_inv", 2 * TILES)
        t_pr = signal("t_pr", TILES)
        s_prt = signal("s_prt", TILES)
        m_att = signal("m_att", TILES)
        s_x2 = signal("s_x2", TILES)
        s_xf = signal("s_xf", TILES)
        xf_out = signal("xf_out", 1, 16)
        t_xf = signal("t_xf", TILES)
        s_xft = signal("s_xft", TILES)
        m_lg = signal("m_lg", TILES)
        s_elg = signal("s_elg", TILES)
        s_scores = signal("s_scores", TILES)
        s_biased = signal("s_biased", TILES)
        s_top = signal("s_top", TILES)
        s_six = signal("s_six", TILES)
        s_taken = signal("s_taken", TILES)
        s_chosen = signal("s_chosen", TILES)
        s_counts = signal("s_counts", TILES + 1)
        m_rank = signal("m_rank", TILES)
        s_fits = signal("s_fits", 2 * TILES)
        s_key = signal("s_key", TILES)
        s_order = signal("s_order", TILES)
        s_slot = signal("s_slot", TILES)
        sent = signal("sent", TOP * TILES, 16)
        m_s1 = signal("m_s1", len(SB))
        m_s3 = signal("m_s3", len(SB))
        s_hs = signal("s_hs", len(SB))
        s_hm = signal("s_hm", len(SB))
        m_sh = signal("m_sh", TILES)
        s_o = signal("s_o", TILES)
        o_out = signal("o_out", 1, 16)

        slots_in = signal("slots_in", 1, 16)
        m_cnt = signal("m_cnt", 3)
        s_elist = signal("s_elist", 9)
        s_slots = signal("s_slots", 2)
        m_slots = signal("m_slots", 1)
        w_in_e = [signal(f"w_in_e{q}", 2, 16) for q in range(BATCH)]
        s_tabg = signal("s_tabg", BATCH)
        s_tabs = signal("s_tabs", BATCH)
        xb_in = [signal(f"xb_in{q}", 1, 16) for q in range(BATCH)]
        t_xb = signal("t_xb", BATCH)
        s_xbt = signal("s_xbt", BATCH, ahead=BATCH)
        m_h = signal("m_h", BATCH)
        s_h1 = signal("s_h1", BATCH)
        s_hx = signal("s_hx", BATCH, ahead=BATCH)
        m_yo = signal("m_yo", BATCH, ahead=BATCH)
        s_yo = signal("s_yo", BATCH, ahead=BATCH)
        added = signal("added", BATCH, 16, ahead=1)
        landed = signal("landed", BATCH, ahead=BATCH)
        waited = signal("waited", 1)

        block = ctx.enter_context(nc.Block())
        flat = "p t h -> p (t h)"
        TURNS = EXPERTS // BATCH

        def heads(ap):
            return ap.unsqueeze(2).to_broadcast([ap.shape[0], HEADS, HEAD])

        def per_head(ap):
            return ap.rearrange("p (h c) -> p h c", h=HEADS)

        def half_bank(banks, t):
            return banks[t // 2][:, t % 2 * D:(t % 2 + 1) * D]

        def score(t):
            return C[t // 2][:, t % 2 * P:t % 2 * P + CTX]

        def logit(t):
            return C[t // 2][:, t % 2 * EXPERTS:(t % 2 + 1) * EXPERTS]

        def rank(t):
            return C[t // 2][:, D + t % 2 * EXPERTS:D + (t % 2 + 1) * EXPERTS]

        def rounds(front, scan, tail_and_front):
            front(0)
            for g in range(GROUPS):
                scan(g)
                tail_and_front(g, g + 1 if g + 1 < GROUPS else None)

        def turns_of(n_active):
            return (n_active + (BATCH - 1)) // BATCH

        def number_of(engine, at, top, least=0):
            return engine.value_load(e_list_i[0:1, at], min_val=least, max_val=top)

        @block.sync
        def _(sp):

            def load_x(g):
                if g:
                    sp.wait_ge(s_y1.sem, s_y1.of(g - 1))
                if g:
                    sp.wait_ge(s_res.sem, s_res.of(g - 1))
                sp.dma_start(x_s[:], x_v[g]).then_inc(x_in.sem, 16)

            load_x(0)
            sp.dma_start(cs[:], cst).then_inc(s_const.sem, 16)
            sp.dma_start(lnwb_s[:], lnwb).then_inc(s_weights.sem, 16)
            sp.dma_start(w_in_s[:], w_in).then_inc(s_weights.sem, 16)
            for dst, src in ((pick_s, picks), (conv_w_s, conv_w), (conv_b_s, conv_b), (rows8_s, rows8),
                             (skip_w_s, skip_w), (norm_w_s, norm_w), (w_out_s, w_out), (gate_s, gate_t),
                             (gate_b_s, gate_b)):
                sp.dma_start(dst[:], src).then_inc(s_weights.sem, 16)
            sp.dma_start(ws1_s[:], ws1).then_inc(s_shared.sem, 16)
            sp.dma_start(ws3_s[:], ws3).then_inc(s_shared.sem, 16)
            for n, (lo, hi) in enumerate(SB):
                sp.dma_start(ws2_s[0:hi - lo, n, :], ws2[lo:hi, :]).then_inc(s_shared.sem, 16)
            sp.wait_ge(s_blank.sem, s_blank.of(0))
            sp.dma_start(slots.rearrange("(p n) w -> p (n w)", p=P), blank[:]).then_inc(s_table.sem, 16)

            def move_c(g):
                sp.wait_ge(s_conv.sem, s_conv.of(g))
                if g:
                    sp.wait_ge(m_g.sem, m_g.of(g - 1))
                if g:
                    sp.wait_ge(m_off.sem, m_off.of(g - 1))
                sp.dma_start(c_t[:], conv[STATE:P, CB - 1, :]).then_inc(c_moved.sem, 16)

            def store_out(g):
                sp.wait_ge(s_o.sem, s_o.of(g))
                sp.dma_start(out_v[g], o_s[:]).then_inc(o_out.sem, 16)

            def scan(g):
                if g:
                    sp.wait_ge(m_sc.sem, m_sc.of(g - 1))
                if g:
                    sp.wait_ge(m_att.sem, m_att.of(g - 1))
                sp.dma_start(ctx_s[:], ctx_in[g]).then_inc(ctx_loaded.sem, 16)
                sp.dma_start(ctx_t_s[:], ctx_t[g]).then_inc(ctx_loaded.sem, 16)
                if g:
                    store_out(g - 1)

            def front(g):
                load_x(1)
                move_c(g)

            def tail_and_front(g, f):
                if g + 2 < GROUPS:
                    load_x(g + 2)
                sp.wait_ge(s_xf.sem, s_xf.of(g))
                sp.wait_ge(s_scores.sem, s_scores.of(g))
                sp.dma_start(xf_v[g], xf[:]).then_inc(xf_out.sem, 16)
                if f is not None:
                    move_c(f)
                else:
                    store_out(g)

            rounds(front, scan, tail_and_front)

            sp.wait_ge(s_elist.sem, s_elist.of(0))
            n_active = number_of(sp, slice(2 * LIST, 2 * LIST + 1), EXPERTS, 1)

            def load_expert(q, at):
                e = number_of(sp, at, EXPERTS - 1)
                sp.dma_start(w13_s[:, q], w13[bass.ds(e, 1)].rearrange("o p k f -> (o p) k f")).then_inc(w_in_e[q].sem, 16)
                sp.dma_start(w2_s[:, q], w2[bass.ds(e, 1)].rearrange("o (c f) d -> (o f) c d", f=FH)).then_inc(w_in_e[q].sem, 16)

            for q in range(BATCH):
                load_expert(q, slice(q, q + 1))
            sp.wait_ge(sent.sem, sent.of(GROUPS - 1))
            sp.dma_start(slots_i[:], slots.rearrange("(e c) w -> e (c w)", c=CAP)).then_inc(slots_in.sem, 16)
            with sp.Fori(0, TURNS) as i:
                with sp.If(i * BATCH < n_active):
                    for q in range(BATCH):
                        sp.wait_ge(m_yo.sem, m_yo.turn(i, q + 1))
                        sp.sem_inc(waited.sem, 1)
                        load_expert(q, bass.ds(i * BATCH + (BATCH + q), 1))
                with sp.Else():
                    sp.nop()
            for q in range(BATCH):
                sp.wait_ge(w_in_e[q].sem, w_in_e[q].turn(turns_of(n_active)))
            sp.sem_inc(waited.sem, 1)

        @block.gpsimd
        def _(pool):
            pool.memset(blank[:], NOWHERE).then_inc(s_blank.sem, 1)
            pool.memset(minus_half[:], -0.5).then_inc(s_half.sem, 1)
            pool.wait_ge(s_half.sem, s_half.of(0))

            def inverse_root(slot, src, scale, g, var, done, k):
                pool.tensor_scalar(var_eps[:, slot, :], src, scale, EPS, ALU.mult, ALU.add).then_inc(var.sem, 1)
                pool.wait_ge(var.sem, var.of(g, k))
                pool.tensor_tensor(rstd[:, slot, :], var_eps[:, slot, :], minus_half[:], ALU.pow).then_inc(done.sem, 1)

            def front_root(g, n):
                pool.wait_ge(f_mv.sem, f_mv.of(g, (n + 1) * TILES))
                inverse_root(n, mv[:, n, :, 1], 1.0, g, f_var, f_rstd, n + 1)

            def prepare(g):
                front_root(g, 0)
                front_root(g, 1)

            def residual(g):
                pool.wait_ge(s_y1.sem, s_y1.of(g))
                if g:
                    pool.wait_ge(s_x1.sem, s_x1.of(g - 1))
                pool.tensor_tensor(res[:], x_s[:], y1[:], ALU.add).then_inc(s_res.sem, 1)

            def front(g):
                prepare(g)
                residual(g)

            def scatter(g, pieces):
                if g < 0:
                    return
                for piece in pieces:
                    t, k = divmod(piece, TOP)
                    if k == 0:
                        pool.wait_ge(s_slot.sem, s_slot.of(g, t + 1))
                    if g == 0 and t == 0:
                        pool.wait_ge(s_table.sem, s_table.of(0))
                    n = g * TILES + t
                    pool.indirect_dma_start(
                        out=slots, out_offset=bass.IndirectOffsetOnAxis(ap=slot_i[:, t, k:k + 1], axis=0),
                        in_=tok_i[:, n:n + 1], in_offset=None,
                        bounds_check=EXPERTS * CAP - 1, oob_is_err=False).then_inc(sent.sem, 16)

            def scan(g):
                def decayed_input(t):
                    if t == 0:
                        pool.wait_ge(s_ecum.sem, s_ecum.of(g))
                    pool.wait_ge(s_xdt.sem, s_xdt.of(g, t + 1))
                    if g and t == 0:
                        pool.wait_ge(m_state.sem, m_state.of(g - 1))
                    pool.tensor_tensor(per_head(xdec[:, t, :]), per_head(xdt[:, t, :]),
                                       heads(e_end[:, t, :]), ALU.mult).then_inc(s_xdec.sem, 1)

                def gate(t):
                    pool.wait_ge(s_ysum.sem, s_ysum.of(g, t + 1))
                    pool.wait_ge(s_z.sem, s_z.of(g, t + 1))
                    pool.tensor_tensor(yg[:, t, :], yg[:, t, :], zs[:, t, :], ALU.mult).then_inc(s_yg.sem, 1)

                decayed_input(0)
                for t in range(TILES):
                    pool.wait_ge(s_state.sem, s_state.of(g, t + 1))
                    pool.tensor_tensor(per_head(state[:, t + 1, :]), per_head(state[:, t, :]),
                                       heads(e_tot[0:STATE, t, :]), ALU.mult).then_inc(s_sdec.sem, 1)
                    if t + 1 < TILES:
                        decayed_input(t + 1)
                    if t:
                        gate(t - 1)
                    if g == 0 and t < 2:
                        front_root(1, t)
                    if g + 1 == GROUPS and t + 1 < TILES:
                        scatter(g - 1, range(2 * t, 2 * t + 2))
                gate(TILES - 1)

            def tail_and_front(g, f):
                done = 0 if f is not None else 2 * (TILES - 1)
                scatter(g - 1, range(done, done + TOP))
                pool.wait_ge(s_sumsq.sem, s_sumsq.of(g))
                inverse_root(2, sumsq[:], 1.0 / INNER, g, t_var, t_rstd, 1)
                pool.wait_ge(t_mv.sem, t_mv.of(g, TILES))
                inverse_root(3, mv[:, 2, :, 1], 1.0, g, t_var, t_rstd, 2)
                if f is not None:
                    residual(f)
                if g + 2 < GROUPS:
                    front_root(g + 2, 0)
                    front_root(g + 2, 1)
                pool.wait_ge(t_mv.sem, t_mv.of(g, 2 * TILES))
                inverse_root(4, mv[:, 3, :, 1], 1.0, g, t_var, t_rstd, 3)
                scatter(g - 1, range(done + TOP, TOP * TILES))

            rounds(front, scan, tail_and_front)
            scatter(GROUPS - 1, range(TOP * TILES))

            pool.wait_ge(s_elist.sem, s_elist.of(0))
            n_active = number_of(pool, slice(2 * LIST, 2 * LIST + 1), EXPERTS, 1)
            first = [number_of(pool, slice(LIST + q, LIST + q + 1), EXPERTS) for q in range(BATCH)]
            pool.wait_ge(xf_out.sem, xf_out.of(GROUPS - 1))
            pool.wait_ge(o_out.sem, o_out.of(GROUPS - 1))
            pool.indirect_dma_start(
                out=out, out_offset=bass.IndirectOffsetOnAxis(ap=blank[:, 0:1], axis=0),
                in_=yo[:, 0, :], in_offset=None, bounds_check=TOKENS - 1, oob_is_err=False,
                compute_op=ALU.add).then_inc(added.sem, 16)
            pool.wait_ge(s_slots.sem, s_slots.of(0))

            def copy_slots(q, e):
                pool.tensor_copy(tab_g[:, q, :], slots_t[:, bass.ds(e, 1)]).then_inc(s_tabg.sem, 1)

            def gather(q):
                pool.indirect_dma_start(
                    out=xb[:, q, :], out_offset=None, in_=xf_dram,
                    in_offset=bass.IndirectOffsetOnAxis(ap=tab_g[:, q, :], axis=0),
                    bounds_check=TOKENS - 1, oob_is_err=False).then_inc(xb_in[q].sem, 16)

            for q in range(BATCH):
                copy_slots(q, first[q])
                pool.wait_ge(s_tabg.sem, s_tabg.of(0, q + 1))
                gather(q)
            pool.sem_inc(landed.sem, BATCH)
            with pool.Fori(0, TURNS) as i:
                with pool.If(i * BATCH < n_active):
                    for q in range(BATCH):
                        pool.wait_ge(t_xb.sem, t_xb.turn(i, q + 1))
                        pool.wait_ge(s_wt.sem, s_wt.turn(i, q + 1))
                        pool.sem_inc(waited.sem, 1)
                        pool.tensor_copy(tab_s[:, q, :], tab_g[:, q, :]).then_inc(s_tabs.sem, 1)
                        e = number_of(pool, bass.ds(i * BATCH + (LIST + BATCH + q), 1), EXPERTS)
                        pool.wait_ge(s_tabs.sem, s_tabs.turn(i, q + 1))
                        pool.sem_inc(waited.sem, 1)
                        copy_slots(q, e)
                        pool.wait_ge(s_tabg.sem, s_tabg.turn(i, BATCH + q + 1))
                        pool.sem_inc(waited.sem, 1)
                        gather(q)
                        pool.wait_ge(s_yo.sem, s_yo.turn(i, q + 1))
                        pool.wait_ge(added.sem, added.turn(i, q))
                        pool.sem_inc(landed.sem, 1)
                        pool.indirect_dma_start(
                            out=out, out_offset=bass.IndirectOffsetOnAxis(ap=tab_s[:, q, :], axis=0),
                            in_=yo[:, q, :], in_offset=None, bounds_check=TOKENS - 1, oob_is_err=False,
                            compute_op=ALU.add).then_inc(added.sem, 16)
                with pool.Else():
                    pool.nop()
            for q in range(BATCH):
                pool.wait_ge(xb_in[q].sem, xb_in[q].turn(turns_of(n_active)))
            pool.wait_ge(added.sem, added.turn(turns_of(n_active), 0))
            pool.sem_inc(waited.sem, 1)

        @block.scalar
        def _(act):
            act.wait_ge(s_weights.sem, s_weights.of(0))
            act.activation(neg_a[:], rows8_s[:, 1, :], ACT.Exp).then_inc(s_exp_a.sem, 1)

            def channels(g):
                for t in range(TILES):
                    act.wait_ge(t_xh.sem, t_xh.of(g, t + 1))
                    if g and t == 0:
                        act.wait_ge(m_dt.sem, m_dt.of(g - 1))
                    for k in range(KD):
                        ins = act.activation(xnt[:, k, t * P:(t + 1) * P], DD[t % 2][:, k * P:(k + 1) * P],
                                             ACT.Identity, scale=lnwb_s[:, 0, k:k + 1], bias=lnwb_s[:, 1, k:k + 1])
                    ins.then_inc(s_xnt.sem, 1)

            def gate_z(g):
                for t in range(TILES):
                    act.wait_ge(m_z.sem, m_z.of(g, t + 1))
                    act.activation(zs[:, t, :], DD[t % 2][:], ACT.Silu).then_inc(s_z.sem, 1)

            def raw_x(g, c):
                if c == 0:
                    act.wait_ge(s_halo.sem, s_halo.of(g))
                act.wait_ge(m_x.sem, m_x.of(g, c + 1))
                if g and c == 0:
                    act.wait_ge(m_y.sem, m_y.of(g - 1))
                if g and c == 0:
                    act.wait_ge(c_moved.sem, c_moved.of(g - 1))
                act.activation(raw[:, c, TAPS - 1:], DD[c % 2][:], ACT.Copy)
                act.activation(conv[:, c, :], DD[c % 2][:], ACT.Identity,
                               scale=conv_w_s[:, c, TAPS - 1:TAPS], bias=conv_b_s[:, c:c + 1]).then_inc(s_raw.sem, 1)

            def conv_act(g, c):
                act.wait_ge(s_tap.sem, s_tap.of(g, (TAPS - 1) * (c + 1)))
                act.activation(conv[:, c, :], conv[:, c, :], ACT.Silu).then_inc(s_conv.sem, 1)

            def small_exp(g):
                act.wait_ge(s_dtv.sem, s_dtv.of(g, 2))
                act.activation(dt_u[:], dt_abs[:], ACT.Exp, scale=-1.0).then_inc(s_u.sem, 1)

            def token_major(g):
                for t in range(TILES):
                    act.wait_ge(t_x.sem, t_x.of(g, t + 1))
                    if g and t == 0:
                        act.wait_ge(s_xdt.sem, s_xdt.of(g - 1))
                    act.activation(xs[:, t, :], DD[t % 2][:], ACT.Copy).then_inc(s_xs.sem, 1)
                act.wait_ge(t_b.sem, t_b.of(g))
                if g:
                    act.wait_ge(m_state.sem, m_state.of(g - 1))
                act.activation(b_tok[:].rearrange("p t n -> p (t n)"), C[0][:, 0:TILES * STATE], ACT.Copy).then_inc(s_btok.sem, 1)

            def front(g):
                channels(g)
                for c in range(CB):
                    raw_x(g, c)
                small_exp(g)
                conv_act(g, 0)
                conv_act(g, 1)
                gate_z(g)
                for c in range(2, CB):
                    conv_act(g, c)
                token_major(g)

            def scan(g):
                act.wait_ge(s_cum.sem, s_cum.of(g))
                act.wait_ge(m_cum.sem, m_cum.of(g))
                act.activation(e_cum[:].rearrange(flat), cum[:].rearrange(flat), ACT.Exp).then_inc(s_ecum.sem, 1)
                act.activation(e_end[:].rearrange(flat), to_end[:].rearrange(flat), ACT.Exp).then_inc(s_ecum.sem, 1)
                act.activation(e_tot[:].rearrange(flat), C[1][:, TH:2 * TH], ACT.Exp).then_inc(s_ecum.sem, 1)
                for t in range(TILES):
                    for half in range(2):
                        act.wait_ge(m_rows.sem, m_rows.of(g, 2 * t + half + 1))
                        for j in range(HEADS // 2):
                            h = half * (HEADS // 2) + j
                            ins = act.activation(m_s[:, t, h, :], DD[half][:, j * P:(j + 1) * P], ACT.Relu,
                                                 scale=-1.0, bias=cum[:, t, h:h + 1])
                        ins.then_inc(s_drop.sem, 1)
                    for half in range(2):
                        act.wait_ge(s_drop.sem, s_drop.of(g, 2 * t + half + 1))
                        pair = m_s[:, t, half * (HEADS // 2):(half + 1) * (HEADS // 2), :]
                        act.activation(pair, pair, ACT.Exp, scale=-1.0).then_inc(s_decay.sem, 1)

            def out_side(g, f):
                for t in range(TILES):
                    act.wait_ge(t_yg.sem, t_yg.of(g, t + 1))
                    if t >= 2:
                        act.wait_ge(m_out.sem, m_out.of(g, t - 1))
                    act.activation(yg_t[:, t % 2].rearrange("p k c -> p (k c)"), B[t % 2][:], ACT.Copy).then_inc(s_ygt.sem, 1)
                    act.wait_ge(s_yg.sem, s_yg.of(g, t + 1))
                    if g or t:
                        act.wait_ge(s_sumsq.sem, s_sumsq.of(g, t))
                    act.activation(square[:], yg[:, t, :], ACT.Square, accum_out=sumsq[:, t:t + 1]).then_inc(s_sumsq.sem, 1)
                    if f is not None and t < 2:
                        raw_x(f, t)

            def attention(g):
                def softmax(t):
                    if t % 2 == 0:
                        act.wait_ge(s_max.sem, s_max.of(g, t // 2 * 2 + 2))
                    act.activation(probs[:, t, :], score(t), ACT.Exp,
                                   bias=neg_max[:, 0, t:t + 1], accum_out=exp_sum[:, 0, t:t + 1]).then_inc(s_probs.sem, 1)

                for t in range(TILES):
                    act.wait_ge(t_xl.sem, t_xl.of(g, t + 1))
                    if t >= 2:
                        act.wait_ge(m_sc.sem, m_sc.of(g, t - 1))
                    act.activation(xl_t[:, t % 2].rearrange("p k c -> p (k c)"), B[t % 2][:, 0:D], ACT.Copy).then_inc(s_xlt.sem, 1)
                for t in range(TILES):
                    softmax(t)
                for t in range(TILES):
                    act.wait_ge(t_pr.sem, t_pr.of(g, t + 1))
                    if g and t == 0:
                        act.wait_ge(m_att.sem, m_att.of(g - 1))
                    act.activation(probs_t[:, t, :], B[t % 2][0:CTX, 0:P], ACT.Copy).then_inc(s_prt.sem, 1)

            def route_in(g):
                for t in range(TILES):
                    act.wait_ge(t_xf.sem, t_xf.of(g, t + 1))
                    if g and t == 0:
                        act.wait_ge(m_s3.sem, m_s3.of(g - 1))
                    act.activation(xf_t[:, :, t * P:(t + 1) * P],
                                   B[t % 2][:, 0:D].rearrange("p (k c) -> p k c", k=KD), ACT.Copy).then_inc(s_xft.sem, 1)

            def route_exp(g):
                for t in range(TILES):
                    if t % 2 == 0:
                        act.wait_ge(s_max.sem, s_max.of(g, TILES + t // 2 * 2 + 2))
                    act.activation(xf[:, t, D:], logit(t), ACT.Exp,
                                   bias=neg_max[:, 1, t:t + 1], accum_out=exp_sum[:, 1, t:t + 1]).then_inc(s_elg.sem, 1)

            def shared_act(g, n):
                lo, hi = SB[n]
                act.wait_ge(m_s1.sem, m_s1.of(g, n + 1))
                if g and n == 0:
                    act.wait_ge(m_sh.sem, m_sh.of(g - 1))
                act.activation(hs[0:hi - lo, n, :], A[n % 2][0:hi - lo, :], ACT.Silu).then_inc(s_hs.sem, 1)

            def tail_and_front(g, f):
                if f is not None:
                    channels(f)
                out_side(g, f)
                if f is not None:
                    raw_x(f, 2)
                    raw_x(f, 3)
                attention(g)
                if f is not None:
                    small_exp(f)
                    raw_x(f, 4)
                    conv_act(f, 0)
                    conv_act(f, 1)
                    gate_z(f)
                route_in(g)
                route_exp(g)
                if f is not None:
                    conv_act(f, 2)
                shared_act(g, 0)
                if f is not None:
                    conv_act(f, 3)
                shared_act(g, 1)
                if f is not None:
                    conv_act(f, 4)
                shared_act(g, 2)
                if f is not None:
                    token_major(f)

            rounds(front, scan, tail_and_front)

            act.wait_ge(s_elist.sem, s_elist.of(0))
            n_active = number_of(act, slice(2 * LIST, 2 * LIST + 1), EXPERTS, 1)
            act.sem_inc(s_xbt.sem, BATCH)
            with act.Fori(0, TURNS) as i:
                with act.If(i * BATCH < n_active):
                    def rows_out(q):
                        act.wait_ge(t_xb.sem, t_xb.turn(i, q + 1))
                        act.activation(xb_t[:, q].rearrange("p k c -> p (k c)"), A[q % 2][:, 0:D], ACT.Copy).then_inc(s_xbt.sem, 1)

                    rows_out(0)
                    for q in range(BATCH):
                        if q + 1 < BATCH:
                            rows_out(q + 1)
                        act.wait_ge(m_h.sem, m_h.turn(i, q + 1))
                        act.activation(h1[:, q, :], B[q % 2][0:FH, 0:2 * P], ACT.Silu).then_inc(s_h1.sem, 1)
                with act.Else():
                    act.nop()

        @block.vector
        def _(dve):
            dve.memset(counts[:], 0.0).then_inc(s_zero.sem, 1)
            dve.memset(e_list[:], 0.0).then_inc(s_zero.sem, 1)
            dve.memset(biased[:], FAR).then_inc(s_zero.sem, 1)
            dve.wait_ge(s_zero.sem, s_zero.of(0))

            def norm_stats(n, src, g, src_ready, stat, done, base):
                for t in range(TILES):
                    dve.wait_ge(src_ready.sem, src_ready.of(g, min(t + 1, src_ready.per)))
                    dve.bn_stats(stats[:, n, t, :], src[:, t, :]).then_inc(stat.sem, 1)
                for t in range(TILES):
                    dve.wait_ge(stat.sem, stat.of(g, base + t + 1))
                    dve.bn_aggr(mv[:, n, t, :], stats[:, n, t, :]).then_inc(done.sem, 1)

            def normed(dst, src, n, slot, g, rooted, k, done):
                dve.wait_ge(rooted.sem, rooted.of(g, k))
                for t in range(TILES):
                    dve.tensor_scalar(dst[:, t, 0:D], src[:, t, :], mv[:, n, t, 0:1],
                                      rstd[:, slot, t:t + 1], ALU.subtract, ALU.mult).then_inc(done.sem, 1)

            def second_apply(g):
                if g:
                    dve.wait_ge(t_xh.sem, t_xh.of(g - 1))
                normed(xh, y1, 1, 1, g, f_rstd, 2, s_xh)

            def halo(g):
                if g:
                    dve.wait_ge(s_tap.sem, s_tap.of(g - 1))
                if g * GROUP % SEQ == 0:
                    dve.memset(raw[:, :, 0:TAPS - 1], 0.0).then_inc(s_halo.sem, 1)
                else:
                    dve.tensor_copy(raw[:, :, 0:TAPS - 1], raw[:, :, GROUP:]).then_inc(s_halo.sem, 1)

            def first_norm(g):
                if g:
                    dve.wait_ge(s_xh.sem, s_xh.of(g - 1))
                norm_stats(0, x_s, g, x_in, f_stats, f_mv, 0)

            def first_apply(g):
                dve.wait_ge(f_rstd.sem, f_rstd.of(g, 1))
                if g:
                    dve.wait_ge(s_res.sem, s_res.of(g - 1))
                for t in range(TILES):
                    dve.tensor_scalar(y1[:, t, :], x_s[:, t, :], mv[:, 0, t, 0:1], rstd[:, 0, t:t + 1],
                                      ALU.subtract, ALU.mult).then_inc(s_y1.sem, 1)
                norm_stats(1, y1, g, s_y1, f_stats, f_mv, TILES)

            def conv_taps(g, c):
                if c == 0:
                    dve.wait_ge(s_halo.sem, s_halo.of(g))
                dve.wait_ge(s_raw.sem, s_raw.of(g, c + 1))
                for j in range(TAPS - 1):
                    if j:
                        dve.wait_ge(s_tap.sem, s_tap.of(g, (TAPS - 1) * c + j))
                    dve.scalar_tensor_tensor(out=conv[:, c, :], in0=raw[:, c, j:j + GROUP],
                                             scalar=conv_w_s[:, c, j:j + 1], in1=conv[:, c, :],
                                             op0=ALU.mult, op1=ALU.add).then_inc(s_tap.sem, 1)

            def dt_before(g):
                dve.wait_ge(m_dt.sem, m_dt.of(g))
                if g:
                    dve.wait_ge(s_dt.sem, s_dt.of(g - 1))
                dve.tensor_tensor(dt_v[:].rearrange("p (t h) -> p t h", h=HEADS),
                                  DD[1][:, 0:TH].rearrange("p (t h) -> p t h", h=HEADS),
                                  rows8_s[:, 0, :].unsqueeze(1).to_broadcast([P, TILES, HEADS]), ALU.add).then_inc(s_dtv.sem, 1)
                dve.wait_ge(s_dtv.sem, s_dtv.of(g, 1))
                dve.scalar_tensor_tensor(out=dt_abs[:], in0=dt_v[:], scalar=-1.0, in1=dt_v[:],
                                         op0=ALU.mult, op1=ALU.max).then_inc(s_dtv.sem, 1)
                dve.tensor_scalar(dt_relu[:], dt_v[:], 0.0, None, ALU.max).then_inc(s_dtv.sem, 1)

            def dt_after(g):
                dve.wait_ge(s_u.sem, s_u.of(g))
                dve.tensor_scalar(dt_den[:], dt_u[:], 2.0, None, ALU.add).then_inc(s_sq.sem, 1)
                dve.wait_ge(s_sq.sem, s_sq.of(g, 1))
                dve.reciprocal(dt_den[:], dt_den[:]).then_inc(s_sq.sem, 1)
                dve.wait_ge(s_sq.sem, s_sq.of(g, 2))
                dve.tensor_tensor(dt_s[:], dt_u[:], dt_den[:], ALU.mult).then_inc(s_sq.sem, 1)
                dve.wait_ge(s_sq.sem, s_sq.of(g, 3))
                dve.tensor_tensor(dt_q[:], dt_s[:], dt_s[:], ALU.mult).then_inc(s_sq.sem, 1)
                dve.wait_ge(s_sq.sem, s_sq.of(g))
                dve.tensor_scalar(dt_p[:], dt_q[:], ATANH[0], None, ALU.mult).then_inc(s_poly.sem, 1)
                for n, c in enumerate(ATANH[1:]):
                    dve.wait_ge(s_poly.sem, s_poly.of(g, n + 1))
                    dve.scalar_tensor_tensor(out=dt_p[:], in0=dt_p[:], scalar=c, in1=dt_q[:],
                                             op0=ALU.add, op1=ALU.mult).then_inc(s_poly.sem, 1)
                dve.wait_ge(s_poly.sem, s_poly.of(g, len(ATANH)))
                dve.scalar_tensor_tensor(out=dt_p[:], in0=dt_p[:], scalar=1.0, in1=dt_s[:],
                                         op0=ALU.add, op1=ALU.mult).then_inc(s_poly.sem, 1)
                dve.wait_ge(s_poly.sem, s_poly.of(g))
                dve.wait_ge(s_dtv.sem, s_dtv.of(g))
                dve.scalar_tensor_tensor(out=dt[:].rearrange(flat), in0=dt_p[:], scalar=2.0,
                                         in1=dt_relu[:], op0=ALU.mult, op1=ALU.add).then_inc(s_dt.sem, 1)
                dve.wait_ge(s_dt.sem, s_dt.of(g, 1))
                if g == 0:
                    dve.wait_ge(s_wout.sem, s_wout.of(0))
                dve.tensor_tensor(a_s[:], dt[:], neg_a[:].unsqueeze(1).to_broadcast([P, TILES, HEADS]),
                                  ALU.mult).then_inc(s_dt.sem, 1)

            def inputs(g):
                for t in range(TILES):
                    dve.wait_ge(s_xs.sem, s_xs.of(g, t + 1))
                    if g and t == 0:
                        dve.wait_ge(s_xdec.sem, s_xdec.of(g - 1))
                    dve.tensor_tensor(per_head(xdt[:, t, :]), per_head(xs[:, t, :]), heads(dt[:, t, :]),
                                      ALU.mult).then_inc(s_xdt.sem, 1)

            def front(g):
                halo(g)
                first_norm(g)
                first_apply(g)
                second_apply(g)
                dve.wait_ge(s_const.sem, s_const.of(0))
                dve.wait_ge(s_weights.sem, s_weights.of(0))
                dve.wait_ge(s_exp_a.sem, s_exp_a.of(0))
                dve.tensor_scalar(neg_a[:], neg_a[:], -1.0, None, ALU.mult).then_inc(s_wout.sem, 1)
                for k in range(INNER // P):
                    dve.tensor_scalar(w_out_s[:, k, :], w_out_s[:, k, :], norm_w_s[:, k:k + 1], None,
                                      ALU.mult).then_inc(s_wout.sem, 1)
                for c in range(INNER // P):
                    dve.tensor_scalar(skip_diag[:, c, :], ident, skip_w_s[:, c:c + 1], None, ALU.mult).then_inc(s_diag.sem, 1)
                dve.tensor_copy(lt_b[:], lt).then_inc(s_small.sem, 1)
                dve.tensor_copy(ones_b[:], ones).then_inc(s_small.sem, 1)
                dve.tensor_copy(tok_i[:], cs[:, C_TOK:C_TOK + TOKENS // P]).then_inc(s_small.sem, 1)
                conv_taps(g, 0)
                conv_taps(g, 1)
                dt_before(g)
                conv_taps(g, 2)
                conv_taps(g, 3)
                conv_taps(g, 4)
                dt_after(g)
                scan_in(g)

            def scan_in(g):
                dve.wait_ge(m_cum.sem, m_cum.of(g))
                if g:
                    dve.wait_ge(m_rows.sem, m_rows.of(g - 1))
                rows = C[1][0:TH, 2 * TH:2 * TH + P]
                dve.tensor_copy(cum_parts[0:TH, :], rows).then_inc(s_parts.sem, 1)
                dve.tensor_copy(cum[:].rearrange(flat), C[1][:, 0:TH]).then_inc(s_cum.sem, 1)
                dve.wait_ge(s_parts.sem, s_parts.of(g, 1))
                dve.tensor_tensor(cum_rest[:, 0, :], rows, cum_parts[0:TH, :], ALU.subtract).then_inc(s_parts.sem, 1)
                dve.wait_ge(s_cum.sem, s_cum.of(g, 1))
                dve.tensor_tensor(to_end[:].rearrange(flat), C[1][:, TH:2 * TH], cum[:].rearrange(flat),
                                  ALU.subtract).then_inc(s_cum.sem, 1)
                dve.wait_ge(s_parts.sem, s_parts.of(g, 2))
                dve.tensor_copy(cum_mid[:], cum_rest[:, 0, :]).then_inc(s_parts.sem, 1)
                dve.wait_ge(s_parts.sem, s_parts.of(g, 3))
                dve.tensor_tensor(cum_rest[:, 1, :], cum_rest[:, 0, :], cum_mid[:], ALU.subtract).then_inc(s_parts.sem, 1)
                dve.tensor_copy(cum_parts[TH:2 * TH, :], cum_mid[:]).then_inc(s_parts.sem, 1)
                dve.wait_ge(s_parts.sem, s_parts.of(g, 4))
                dve.tensor_copy(cum_parts[2 * TH:3 * TH, :], cum_rest[:, 1, :]).then_inc(s_parts.sem, 1)

            def scan(g):
                if g:
                    dve.wait_ge(s_state.sem, s_state.of(g - 1))
                if g * GROUP % SEQ == 0:
                    dve.memset(state[:, 0, :], 0.0).then_inc(s_state.sem, 1)
                else:
                    dve.tensor_copy(state[:, 0, :], state[:, TILES, :]).then_inc(s_state.sem, 1)
                dve.wait_ge(m_g.sem, m_g.of(g))
                dve.tensor_tensor(gm[:], C[0][:].rearrange("p (t l) -> p t l", t=TILES),
                                  le.unsqueeze(1).to_broadcast([P, TILES, P]), ALU.mult).then_inc(s_gm.sem, 1)
                dve.wait_ge(s_gm.sem, s_gm.of(g))
                inputs(g)

                def add_inter(t):
                    dve.wait_ge(m_y.sem, m_y.of(g, t + 1))
                    dve.wait_ge(s_yoff.sem, s_yoff.of(g, t + 1))
                    dve.tensor_tensor(yg[:, t, :], B[t % 2][:], y_off[:, t, :], ALU.add).then_inc(s_ysum.sem, 1)

                for t in range(TILES):
                    dve.wait_ge(s_decay.sem, s_decay.of(g, 2 * t + 2))
                    dve.tensor_tensor(m_s[:, t], m_s[:, t],
                                      gm[:, t, :].unsqueeze(1).to_broadcast([P, HEADS, P]), ALU.mult).then_inc(s_m.sem, 1)
                    dve.wait_ge(m_state.sem, m_state.of(g, t + 1))
                    dve.wait_ge(s_sdec.sem, s_sdec.of(g, t + 1))
                    dve.tensor_tensor(state[:, t + 1, :], C[1][0:STATE, :], state[:, t + 1, :], ALU.add).then_inc(s_state.sem, 1)
                    dve.wait_ge(m_off.sem, m_off.of(g, t + 1))
                    if t == 0:
                        dve.wait_ge(s_ecum.sem, s_ecum.of(g))
                    if g and t == 0:
                        dve.wait_ge(t_yg.sem, t_yg.of(g - 1))
                    if g and t == 0:
                        dve.wait_ge(s_sumsq.sem, s_sumsq.of(g - 1))
                    dve.tensor_tensor(per_head(y_off[:, t, :]), per_head(A[t % 2][:]),
                                      heads(e_cum[:, t, :]), ALU.mult).then_inc(s_yoff.sem, 1)
                    if t:
                        add_inter(t - 1)
                    if t % 2 and g:
                        layer_out(g - 1, (t - 1, t))
                    if g == 0 and t < 3:
                        (first_norm, first_apply, second_apply)[t](1)
                add_inter(TILES - 1)

            def block_out(g):
                dve.wait_ge(t_rstd.sem, t_rstd.of(g, 1))
                if g:
                    dve.wait_ge(s_res.sem, s_res.of(g))
                for t in range(TILES):
                    if t % 2 == 0:
                        dve.wait_ge(m_out.sem, m_out.of(g, t // 2 * 2 + 2))
                    if g and t == 0:
                        dve.wait_ge(s_xl.sem, s_xl.of(g - 1))
                    dve.scalar_tensor_tensor(out=x1[:, t, :], in0=half_bank(A, t),
                                             scalar=rstd[:, 2, t:t + 1], in1=res[:, t, :],
                                             op0=ALU.mult, op1=ALU.add).then_inc(s_x1.sem, 1)

            def attention_max(g):
                for t in range(TILES):
                    if t % 2 == 0:
                        dve.wait_ge(m_sc.sem, m_sc.of(g, t // 2 * 2 + 2))
                    dve.tensor_reduce(neg_max[:, 0, t:t + 1], score(t), AX.X, ALU.max, negate=True).then_inc(s_max.sem, 1)

            def attention_out(g):
                for t in range(TILES):
                    dve.wait_ge(s_probs.sem, s_probs.of(g, t + 1))
                    dve.reciprocal(inv_sum[:, 0, t:t + 1], exp_sum[:, 0, t:t + 1]).then_inc(s_inv.sem, 1)
                for t in range(TILES):
                    dve.wait_ge(s_inv.sem, s_inv.of(g, t + 1))
                    if t % 2 == 0:
                        dve.wait_ge(m_att.sem, m_att.of(g, t // 2 * 2 + 2))
                    if g and t == 0:
                        dve.wait_ge(s_xf.sem, s_xf.of(g - 1))
                    dve.scalar_tensor_tensor(out=x2[:, t, :], in0=half_bank(A, t),
                                             scalar=inv_sum[:, 0, t:t + 1], in1=x1[:, t, :],
                                             op0=ALU.mult, op1=ALU.add).then_inc(s_x2.sem, 1)
                norm_stats(3, x2, g, s_x2, t_stats, t_mv, TILES)

            def choose_max(g):
                for t in range(TILES):
                    if t % 2 == 0:
                        dve.wait_ge(m_lg.sem, m_lg.of(g, t // 2 * 2 + 2))
                    dve.tensor_reduce(neg_max[:, 1, t:t + 1], logit(t), AX.X, ALU.max, negate=True).then_inc(s_max.sem, 1)

            def choose(g):
                for t in range(TILES):
                    dve.wait_ge(s_elg.sem, s_elg.of(g, t + 1))
                    dve.reciprocal(inv_sum[:, 1, t:t + 1], exp_sum[:, 1, t:t + 1]).then_inc(s_inv.sem, 1)
                for t in range(TILES):
                    dve.wait_ge(s_inv.sem, s_inv.of(g, TILES + t + 1))
                    dve.tensor_scalar(xf[:, t, D:], xf[:, t, D:], inv_sum[:, 1, t:t + 1], None, ALU.mult).then_inc(s_scores.sem, 1)
                for t in range(TILES):
                    dve.wait_ge(s_scores.sem, s_scores.of(g, t + 1))
                    dve.tensor_tensor(biased[:, t, 0:EXPERTS], xf[:, t, D:], gate_b_s[:], ALU.add).then_inc(s_biased.sem, 1)
                for t in range(TILES):
                    dve.wait_ge(s_biased.sem, s_biased.of(g, t + 1))
                    dve.max(top8[:, t, :], biased[:, t, 0:EXPERTS]).then_inc(s_top.sem, 1)
                for t in range(TILES):
                    dve.wait_ge(s_top.sem, s_top.of(g, t + 1))
                    dve.memset(top8[:, t, TOP:], FAR).then_inc(s_six.sem, 1)
                for t in range(TILES):
                    dve.wait_ge(s_six.sem, s_six.of(g, t + 1))
                    dve.match_replace(out=taken[:, t, :], in_to_replace=top8[:, t, :],
                                      in_values=biased[:, t, :], imm_value=-FAR).then_inc(s_taken.sem, 1)
                for t in range(TILES):
                    dve.wait_ge(s_taken.sem, s_taken.of(g, t + 1))
                    dve.tensor_tensor(chosen[:, t, :], taken[:, t, 0:EXPERTS], biased[:, t, 0:EXPERTS],
                                      ALU.not_equal).then_inc(s_chosen.sem, 1)
                if g:
                    dve.wait_ge(s_counts.sem, s_counts.of(g - 1))
                dve.tensor_copy(counts[:, 0, :], counts[:, TILES, :]).then_inc(s_counts.sem, 1)
                for t in range(TILES):
                    dve.wait_ge(s_chosen.sem, s_chosen.of(g, t + 1))
                    dve.wait_ge(s_counts.sem, s_counts.of(g, t + 1))
                    dve.tensor_tensor(counts[:, t + 1, :], counts[:, t, :], chosen[:, t, :], ALU.add).then_inc(s_counts.sem, 1)

            def shared_mult(g, n):
                lo, hi = SB[n]
                dve.wait_ge(m_s3.sem, m_s3.of(g, n + 1))
                dve.wait_ge(s_hs.sem, s_hs.of(g, n + 1))
                dve.tensor_tensor(hs[0:hi - lo, n, :], B[n % 2][0:hi - lo, :], hs[0:hi - lo, n, :],
                                  ALU.mult).then_inc(s_hm.sem, 1)

            def place(g):
                for t in range(TILES):
                    if t % 2 == 0:
                        dve.wait_ge(m_rank.sem, m_rank.of(g, t // 2 * 2 + 2))
                    dve.scalar_tensor_tensor(out=fits[:, t, :], in0=rank(t), scalar=float(CAP),
                                             in1=chosen[:, t, :], op0=ALU.is_lt, op1=ALU.mult).then_inc(s_fits.sem, 1)
                    dve.scalar_tensor_tensor(out=key[:, t, :], in0=rank(t), scalar=-1.0,
                                             in1=cs[:, C_KEY:C_KEY + EXPERTS], op0=ALU.mult, op1=ALU.add).then_inc(s_fits.sem, 1)
                for t in range(TILES):
                    dve.wait_ge(s_fits.sem, s_fits.of(g, 2 * t + 2))
                    dve.tensor_tensor(key[:, t, :], key[:, t, :], fits[:, t, :], ALU.mult).then_inc(s_key.sem, 1)
                for t in range(TILES):
                    dve.wait_ge(s_key.sem, s_key.of(g, t + 1))
                    dve.max(top_key[:, t, :], key[:, t, :]).then_inc(s_order.sem, 1)
                if g:
                    dve.wait_ge(sent.sem, sent.of(g - 1))
                for t in range(TILES):
                    dve.wait_ge(s_order.sem, s_order.of(g, t + 1))
                    dve.tensor_scalar(slot_i[:, t, :], top_key[:, t, :], -1.0, float(KEY), ALU.mult, ALU.add).then_inc(s_slot.sem, 1)

            def layer_out(g, tiles):
                for t in tiles:
                    if t % 2 == 0:
                        dve.wait_ge(m_sh.sem, m_sh.of(g, t // 2 * 2 + 2))
                    if g and t == 0:
                        dve.wait_ge(o_out.sem, o_out.of(g - 1))
                    dve.tensor_tensor(o_s[:, t, :], half_bank(C, t % 2), x2[:, t, :], ALU.add).then_inc(s_o.sem, 1)

            def tail_and_front(g, f):
                if f is not None:
                    halo(f)
                    conv_taps(f, 0)
                    conv_taps(f, 1)
                block_out(g)
                norm_stats(2, x1, g, s_x1, t_stats, t_mv, 0)
                if g:
                    dve.wait_ge(t_xl.sem, t_xl.of(g - 1))
                normed(xl, x1, 2, 3, g, t_rstd, 2, s_xl)
                if f is not None:
                    conv_taps(f, 2)
                attention_max(g)
                if f is not None:
                    dt_before(f)
                if g + 2 < GROUPS:
                    first_norm(g + 2)
                    first_apply(g + 2)
                attention_out(g)
                if g:
                    dve.wait_ge(xf_out.sem, xf_out.of(g - 1))
                if g:
                    dve.wait_ge(t_xf.sem, t_xf.of(g - 1))
                normed(xf, x2, 3, 4, g, t_rstd, 3, s_xf)
                if g + 2 < GROUPS:
                    second_apply(g + 2)
                if f is not None:
                    conv_taps(f, 3)
                choose_max(g)
                if f is not None:
                    dt_after(f)
                choose(g)
                shared_mult(g, 0)
                if f is not None:
                    conv_taps(f, 4)
                    shared_mult(g, 1)
                    place(g)
                    shared_mult(g, 2)
                    scan_in(f)
                else:
                    place(g)
                    shared_mult(g, 1)
                    shared_mult(g, 2)
                    layer_out(g, range(TILES))

            rounds(front, scan, tail_and_front)

            active, e_rank = e_num[:, 1:2], e_num[:, 2:3]
            dve.wait_ge(m_cnt.sem, m_cnt.of(0, 1))
            dve.tensor_scalar(active, A[0][0:EXPERTS, 0:1], 1.0, None, ALU.min).then_inc(s_elist.sem, 1)
            dve.wait_ge(m_cnt.sem, m_cnt.of(0, 2))
            dve.tensor_copy(e_rank, A[1][0:EXPERTS, 0:1]).then_inc(s_elist.sem, 1)
            dve.wait_ge(s_elist.sem, s_elist.of(0, 2))
            dve.tensor_scalar(e_hot[:], cs[0:EXPERTS, C_IOTA:C_IOTA + EXPERTS], e_rank, active,
                              ALU.is_equal, ALU.mult).then_inc(s_elist.sem, 1)
            dve.wait_ge(m_cnt.sem, m_cnt.of(0, 3))
            n_act = B[0][0:1, 128:129]
            dve.memset(e_list[:, LIST:2 * LIST], float(EXPERTS)).then_inc(s_elist.sem, 1)
            dve.tensor_copy(e_list[:, 0:EXPERTS], B[0][0:1, 0:EXPERTS]).then_inc(s_elist.sem, 1)
            dve.wait_ge(s_elist.sem, s_elist.of(0, 5))
            dve.tensor_copy(e_list[:, 2 * LIST:], n_act).then_inc(s_elist.sem, 1)
            dve.wait_ge(s_elist.sem, s_elist.of(0, 6))
            dve.tensor_scalar(e_list[:, LIST:LIST + EXPERTS], iota[0:1, :],
                              e_list[:, 2 * LIST:], float(EXPERTS), ALU.is_ge, ALU.mult).then_inc(s_elist.sem, 1)
            dve.wait_ge(s_elist.sem, s_elist.of(0, 7))
            dve.tensor_tensor(e_list[:, LIST:LIST + EXPERTS], e_list[:, LIST:LIST + EXPERTS],
                              e_list[:, 0:EXPERTS], ALU.add).then_inc(s_elist.sem, 1)
            dve.wait_ge(s_elist.sem, s_elist.of(0, 8))
            dve.tensor_copy(e_list_i[:], e_list[:]).then_inc(s_elist.sem, 1)
            dve.wait_ge(slots_in.sem, slots_in.of(0))
            dve.tensor_copy(slots_f[:], slots_i[:]).then_inc(s_slots.sem, 1)
            dve.wait_ge(m_slots.sem, m_slots.of(0))
            dve.tensor_copy(slots_t[:], C[0][:, 0:EXPERTS + 1]).then_inc(s_slots.sem, 1)
            dve.wait_ge(s_elist.sem, s_elist.of(0))
            n_active = number_of(dve, slice(2 * LIST, 2 * LIST + 1), EXPERTS, 1)
            dve.sem_inc(s_hx.sem, BATCH)
            dve.sem_inc(s_yo.sem, BATCH)
            with dve.Fori(0, TURNS) as i:
                with dve.If(i * BATCH < n_active):
                    def product(q):
                        dve.wait_ge(s_h1.sem, s_h1.turn(i, q + 1))
                        dve.tensor_tensor(hx[:, q].rearrange("p c t -> p (c t)"), h1[:, q, :],
                                          B[q % 2][0:FH, 2 * P:], ALU.mult).then_inc(s_hx.sem, 1)

                    def keep_weight(q):
                        e = number_of(dve, bass.ds(i * BATCH + q, 1), EXPERTS - 1)
                        dve.wait_ge(xb_in[q].sem, xb_in[q].turn(i))
                        dve.tensor_copy(weight[:, q:q + 1], xb[:, q, bass.ds(e + D, 1)]).then_inc(s_wt.sem, 1)

                    keep_weight(0)
                    product(0)
                    for q in range(BATCH):
                        if q + 1 < BATCH:
                            keep_weight(q + 1)
                            product(q + 1)
                        dve.wait_ge(m_yo.sem, m_yo.turn(i, q + 1))
                        dve.wait_ge(landed.sem, landed.turn(i, q + 2 - BATCH))
                        dve.tensor_scalar(yo[:, q, :], C[q % 2][:, 0:D], weight[:, q:q + 1], None, ALU.mult).then_inc(s_yo.sem, 1)
                with dve.Else():
                    dve.nop()

        @block.tensor
        def _(pe):

            def blocks(src, dst, n):
                for k in range(n):
                    ins = pe.transpose(dst[:, k * P:(k + 1) * P], src[:, k * P:(k + 1) * P], ident)
                return ins

            def turn_in(g):
                if g == 0:
                    pe.wait_ge(s_const.sem, s_const.of(0))
                for t in range(TILES):
                    pe.wait_ge(s_xh.sem, s_xh.of(g, t + 1))
                    if g and t == 0:
                        pe.wait_ge(s_drop.sem, s_drop.of(g - 1))
                    if t >= 2:
                        pe.wait_ge(s_xnt.sem, s_xnt.of(g, t - 1))
                    blocks(xh[:, t, :], DD[t % 2], KD).then_inc(t_xh.sem, 1)

            def project_z(g, tiles=range(TILES)):
                if g == 0:
                    pe.wait_ge(s_weights.sem, s_weights.of(0))
                for t in tiles:
                    if t == 0:
                        pe.wait_ge(s_raw.sem, s_raw.of(g))
                    if t == 1:
                        pe.wait_ge(s_dtv.sem, s_dtv.of(g, 1))
                    if t >= 2:
                        pe.wait_ge(s_z.sem, s_z.of(g, t - 1))
                    for k in range(KD):
                        ins = pe.matmul(DD[t % 2][:], xnt[:, k, t * P:(t + 1) * P], w_in_s[:, k, 0:INNER],
                                        start=(k == 0), stop=(k == KD - 1))
                    ins.then_inc(m_z.sem, 1)

            def project_x(g, c):
                if c == 0:
                    pe.wait_ge(s_xnt.sem, s_xnt.of(g))
                if c >= 2:
                    pe.wait_ge(s_raw.sem, s_raw.of(g, c - 1))
                for k in range(KD):
                    ins = pe.matmul(DD[c % 2][:], w_in_s[:, k, INNER + c * P:INNER + (c + 1) * P],
                                    xnt[:, k, :], start=(k == 0), stop=(k == KD - 1))
                ins.then_inc(m_x.sem, 1)

            def project_dt(g):
                pe.wait_ge(s_raw.sem, s_raw.of(g, CB - 1))
                for t in range(TILES):
                    for k in range(KD):
                        ins = pe.matmul(DD[1][:, t * HEADS:(t + 1) * HEADS], xnt[:, k, t * P:(t + 1) * P],
                                        w_in_s[:, k, PROJ - HEADS:], start=(k == 0), stop=(k == KD - 1))
                ins.then_inc(m_dt.sem, 1)

            def token_major(g):
                pe.wait_ge(s_z.sem, s_z.of(g))
                for t in range(TILES):
                    if t == 0:
                        pe.wait_ge(s_conv.sem, s_conv.of(g, CB - 1))
                    if t >= 2:
                        pe.wait_ge(s_xs.sem, s_xs.of(g, t - 1))
                    for c in range(INNER // P):
                        ins = pe.transpose(DD[t % 2][:, c * P:(c + 1) * P], conv[:, c, t * P:(t + 1) * P], ident)
                    ins.then_inc(t_x.sem, 1)
                pe.wait_ge(s_conv.sem, s_conv.of(g))
                if g:
                    pe.wait_ge(s_fits.sem, s_fits.of(g - 1))
                for t in range(TILES):
                    ins = pe.transpose(C[0][:, t * STATE:(t + 1) * STATE], conv[0:STATE, CB - 1, t * P:(t + 1) * P],
                                       ident[0:STATE, 0:STATE])
                ins.then_inc(t_b.sem, 1)

            def front(g):
                turn_in(g)
                for c in range(CB):
                    project_x(g, c)
                project_dt(g)
                project_z(g)
                token_major(g)
                scan_in(g)

            def scan_in(g):
                pe.wait_ge(s_dt.sem, s_dt.of(g))
                a_all = a_s[:].rearrange(flat)
                pe.matmul(C[1][:, 0:TH], le, a_all, start=True, stop=True).then_inc(m_cum.sem, 1)
                pe.matmul(C[1][:, TH:2 * TH], ones, a_all, start=True, stop=True).then_inc(m_cum.sem, 1)
                pe.matmul(C[1][0:TH, 2 * TH:2 * TH + P], a_all, le, start=True, stop=True).then_inc(m_cum.sem, 1)
                pe.wait_ge(c_moved.sem, c_moved.of(g))
                pe.wait_ge(s_btok.sem, s_btok.of(g))
                for t in range(TILES):
                    ins = pe.matmul(C[0][:, t * P:(t + 1) * P], conv[0:STATE, CB - 1, t * P:(t + 1) * P],
                                    c_t[:, t * P:(t + 1) * P], start=True, stop=True)
                ins.then_inc(m_g.sem, 1)

            def scan(g):
                def rows(t):
                    for half in range(2):
                        if t == 0:
                            if t == 0 and half == 0:
                                pe.wait_ge(s_xs.sem, s_xs.of(g))
                        else:
                            pe.wait_ge(s_drop.sem, s_drop.of(g, 2 * t - 1 + half))
                        for j in range(HEADS // 2):
                            h = t * HEADS + half * (HEADS // 2) + j
                            ins = pe.matmul(DD[half][:, j * P:(j + 1) * P], pick_s[:, h, :], cum_parts[:],
                                            start=True, stop=True)
                        ins.then_inc(m_rows.sem, 1)

                pe.wait_ge(s_parts.sem, s_parts.of(g))
                rows(0)
                for t in range(TILES):
                    pe.wait_ge(s_state.sem, s_state.of(g, t + 1))
                    if g and t == 0:
                        pe.wait_ge(s_hs.sem, s_hs.of(g - 1))
                    if t >= 2:
                        pe.wait_ge(s_yoff.sem, s_yoff.of(g, t - 1))
                    pe.matmul(A[t % 2][:], c_t[:, t * P:(t + 1) * P], state[:, t, :], start=True, stop=True).then_inc(m_off.sem, 1)
                    if t == 0:
                        rows(1)
                    pe.wait_ge(s_xdec.sem, s_xdec.of(g, t + 1))
                    if t == 0:
                        pe.wait_ge(s_ecum.sem, s_ecum.of(g))
                    if t == 0:
                        pe.wait_ge(s_cum.sem, s_cum.of(g))
                    pe.matmul(C[1][0:STATE, :], b_tok[:, t, :], xdec[:, t, :], start=True, stop=True).then_inc(m_state.sem, 1)
                    if g and t == 0:
                        pe.wait_ge(s_hm.sem, s_hm.of(g - 1))
                    if g == 0 and t == 0:
                        pe.wait_ge(s_diag.sem, s_diag.of(0))
                    if t >= 2:
                        pe.wait_ge(s_ysum.sem, s_ysum.of(g, t - 1))
                    for c in range(INNER // P):
                        pe.matmul(B[t % 2][:, c * P:(c + 1) * P], conv[:, c, t * P:(t + 1) * P],
                                  skip_diag[:, c, :], start=(c == 0), stop=False)
                    if t + 2 < TILES:
                        rows(t + 2)
                    if t % 2 and g:
                        shared_out(g - 1, (t - 1, t))
                    pe.wait_ge(s_m.sem, s_m.of(g, t + 1))
                    pe.wait_ge(s_xdt.sem, s_xdt.of(g, t + 1))
                    for h in range(HEADS):
                        ins = pe.matmul(B[t % 2][:, h * HEAD:(h + 1) * HEAD], m_s[:, t, h, :],
                                        xdt[:, t, h * HEAD:(h + 1) * HEAD], start=False, stop=(h == HEADS - 1))
                    ins.then_inc(m_y.sem, 1)
                    if t == TILES - 2 and g + 1 < GROUPS:
                        turn_in(g + 1)

            def block_out(g, f):
                if g == 0:
                    pe.wait_ge(s_wout.sem, s_wout.of(0))

                def turn_yg(t):
                    pe.wait_ge(s_yg.sem, s_yg.of(g, t + 1))
                    if t < 2:
                        pe.wait_ge(s_ysum.sem, s_ysum.of(g, min(t + 3, TILES)))
                    blocks(yg[:, t, :], B[t % 2], INNER // P).then_inc(t_yg.sem, 1)

                turn_yg(0)
                for t in range(TILES):
                    if f is not None and t < 2:
                        project_x(f, t)
                    if t + 1 < TILES:
                        turn_yg(t + 1)
                    pe.wait_ge(s_ygt.sem, s_ygt.of(g, t + 1))
                    if t == 0:
                        pe.wait_ge(s_yoff.sem, s_yoff.of(g))
                    for k in range(INNER // P):
                        ins = pe.matmul(half_bank(A, t), yg_t[:, t % 2, k, :], w_out_s[:, k, :],
                                        start=(k == 0), stop=(k == INNER // P - 1))
                    ins.then_inc(m_out.sem, 1)

            def scores(g):
                pe.wait_ge(ctx_loaded.sem, ctx_loaded.of(g))

                def turn_xl(t):
                    pe.wait_ge(s_xl.sem, s_xl.of(g, t + 1))
                    blocks(xl[:, t, :], B[t % 2], KD).then_inc(t_xl.sem, 1)

                turn_xl(0)
                for t in range(TILES):
                    if t + 1 < TILES:
                        turn_xl(t + 1)
                    pe.wait_ge(s_xlt.sem, s_xlt.of(g, t + 1))
                    if g == 0 and t == 0:
                        pe.wait_ge(s_gm.sem, s_gm.of(g))
                    if g and t == 0:
                        pe.wait_ge(s_o.sem, s_o.of(g - 1))
                    if t == 0:
                        pe.wait_ge(s_state.sem, s_state.of(g))
                    for k in range(KD):
                        ins = pe.matmul(score(t), xl_t[:, t % 2, k, :], ctx_t_s[:, k, :],
                                        start=(k == 0), stop=(k == KD - 1))
                    ins.then_inc(m_sc.sem, 1)

            def turn_probs(g):
                for t in range(TILES):
                    pe.wait_ge(s_probs.sem, s_probs.of(g, t + 1))
                    if t >= 2:
                        pe.wait_ge(s_prt.sem, s_prt.of(g, t - 1))
                    pe.transpose(B[t % 2][0:CTX, 0:P], probs[:, t, :], ident).then_inc(t_pr.sem, 1)

            def attend(g):
                for t in range(TILES):
                    if t >= 2:
                        pe.wait_ge(s_prt.sem, s_prt.of(g, t + 1))
                    if t == 0:
                        pe.wait_ge(s_x1.sem, s_x1.of(g))
                    pe.matmul(half_bank(A, t), probs_t[:, t, :], ctx_s[:], start=True, stop=True).then_inc(m_att.sem, 1)

            def turn_xf(g):
                for t in range(TILES):
                    pe.wait_ge(s_xf.sem, s_xf.of(g, t + 1))
                    if t >= 2:
                        pe.wait_ge(s_xft.sem, s_xft.of(g, t - 1))
                    blocks(xf[:, t, :], B[t % 2], KD).then_inc(t_xf.sem, 1)

            def logits(g):
                for t in range(TILES):
                    if t >= 2:
                        pe.wait_ge(s_xft.sem, s_xft.of(g, t + 1))
                    for k in range(KD):
                        ins = pe.matmul(logit(t), xf_t[:, k, t * P:(t + 1) * P], gate_s[:, k, :],
                                        start=(k == 0), stop=(k == KD - 1))
                    ins.then_inc(m_lg.sem, 1)

            def shared_in(g, n):
                lo, hi = SB[n]
                if g == 0 and n == 0:
                    pe.wait_ge(s_shared.sem, s_shared.of(0))
                if n == 0:
                    pe.wait_ge(s_x2.sem, s_x2.of(g))
                if n >= 2:
                    pe.wait_ge(s_hs.sem, s_hs.of(g, n - 1))
                for k in range(KD):
                    ins = pe.matmul(A[n % 2][0:hi - lo, :], ws1_s[:, k, lo:hi], xf_t[:, k, :],
                                    start=(k == 0), stop=(k == KD - 1))
                ins.then_inc(m_s1.sem, 1)
                if n >= 2:
                    pe.wait_ge(s_hm.sem, s_hm.of(g, n - 1))
                for k in range(KD):
                    ins = pe.matmul(B[n % 2][0:hi - lo, :], ws3_s[:, k, lo:hi], xf_t[:, k, :],
                                    start=(k == 0), stop=(k == KD - 1))
                ins.then_inc(m_s3.sem, 1)

            def ranks(g):
                if g == 0:
                    pe.wait_ge(s_small.sem, s_small.of(0))
                for t in range(TILES):
                    pe.wait_ge(s_chosen.sem, s_chosen.of(g, t + 1))
                    pe.wait_ge(s_counts.sem, s_counts.of(g, t + 1))
                    if t == 0:
                        pe.wait_ge(s_elg.sem, s_elg.of(g))
                    pe.matmul(rank(t), lt_b[:], chosen[:, t, :], start=True, stop=False)
                    pe.matmul(rank(t), ones_b[:], counts[:, t, :],
                              start=False, stop=True).then_inc(m_rank.sem, 1)

            def shared_out(g, tiles):
                if g:
                    pe.wait_ge(s_hm.sem, s_hm.of(g))
                if g:
                    pe.wait_ge(s_fits.sem, s_fits.of(g))
                pe.wait_ge(s_gm.sem, s_gm.of(min(g + 1, GROUPS - 1)))
                if tiles[0]:
                    pe.wait_ge(s_o.sem, s_o.of(g, tiles[0]))
                for t in tiles:
                    for n, (lo, hi) in enumerate(SB):
                        ins = pe.matmul(half_bank(C, t % 2), hs[0:hi - lo, n, t * P:(t + 1) * P],
                                        ws2_s[0:hi - lo, n, :], start=(n == 0), stop=(n == len(SB) - 1))
                    ins.then_inc(m_sh.sem, 1)

            def tail_and_front(g, f):
                block_out(g, f)
                if f is not None:
                    project_x(f, 2)
                    project_x(f, 3)
                scores(g)
                if f is not None:
                    project_dt(f)
                turn_probs(g)
                if f is not None:
                    project_x(f, 4)
                attend(g)
                if f is not None:
                    project_z(f)
                turn_xf(g)
                logits(g)
                shared_in(g, 0)
                if f is None:
                    ranks(g)
                shared_in(g, 1)
                if f is not None:
                    ranks(g)
                shared_in(g, 2)
                if f is not None:
                    token_major(f)
                    scan_in(f)
                else:
                    shared_out(g, (0, 1))
                    shared_out(g, (2, 3))

            rounds(front, scan, tail_and_front)

            pe.wait_ge(s_hs.sem, s_hs.of(GROUPS - 1))
            pe.matmul(A[0][0:EXPERTS, 0:1], counts[:, TILES, :], ones_b[:, 0:1], start=True, stop=True).then_inc(m_cnt.sem, 1)
            pe.wait_ge(s_elist.sem, s_elist.of(0, 1))
            pe.matmul(A[1][0:EXPERTS, 0:1], lt[0:EXPERTS, 0:EXPERTS], e_num[:, 1:2], start=True, stop=True).then_inc(m_cnt.sem, 1)
            pe.wait_ge(s_elist.sem, s_elist.of(0, 3))
            pe.matmul(B[0][0:1, 0:EXPERTS], cs[0:EXPERTS, C_PART:C_PART + 1], e_hot[:], start=True, stop=True)
            pe.matmul(B[0][0:1, 128:129], ones[0:EXPERTS, 0:1], e_num[:, 1:2], start=True, stop=True).then_inc(m_cnt.sem, 1)
            pe.wait_ge(s_slots.sem, s_slots.of(0, 1))
            pe.wait_ge(s_o.sem, s_o.of(GROUPS - 1))
            pe.transpose(C[0][:, 0:EXPERTS + 1], slots_f[:], ident[0:EXPERTS + 1, 0:EXPERTS + 1]).then_inc(m_slots.sem, 1)

            pe.wait_ge(s_elist.sem, s_elist.of(0))
            n_active = number_of(pe, slice(2 * LIST, 2 * LIST + 1), EXPERTS, 1)
            pe.sem_inc(m_yo.sem, BATCH)
            with pe.Fori(0, TURNS) as i:
                with pe.If(i * BATCH < n_active):
                    def rows_in(q):
                        pe.wait_ge(xb_in[q].sem, xb_in[q].turn(i))
                        pe.wait_ge(s_xbt.sem, s_xbt.turn(i, q - 1))
                        for k in range(KD):
                            ins = pe.transpose(A[q % 2][:, k * P:(k + 1) * P], xb[:, q, k * P:(k + 1) * P], ident)
                        ins.then_inc(t_xb.sem, 1)

                    def down(q):
                        pe.wait_ge(s_hx.sem, s_hx.turn(i, q + 1))
                        pe.wait_ge(s_yo.sem, s_yo.turn(i, q - 1))
                        for c in range(2):
                            ins = pe.matmul(C[q % 2][:, 0:D], hx[:, q, c, :], w2_s[:, q, c, :],
                                            start=(c == 0), stop=(c == 1))
                        ins.then_inc(m_yo.sem, 1)

                    rows_in(0)
                    for q in range(BATCH):
                        if q + 1 < BATCH:
                            rows_in(q + 1)
                        pe.wait_ge(s_xbt.sem, s_xbt.turn(i, q + 1))
                        pe.wait_ge(w_in_e[q].sem, w_in_e[q].turn(i))
                        pe.wait_ge(s_hx.sem, s_hx.turn(i, q - 1))
                        for m in range(2):
                            for c in range(2):
                                lo = m * FF + c * FH
                                for k in range(KD):
                                    ins = pe.matmul(B[q % 2][0:FH, (2 * m + c) * P:(2 * m + c + 1) * P],
                                                    w13_s[:, q, k, lo:lo + FH], xb_t[:, q, k, :],
                                                    start=(k == 0), stop=(k == KD - 1))
                        ins.then_inc(m_h.sem, 1)
                        if q:
                            down(q - 1)
                    down(BATCH - 1)
                with pe.Else():
                    pe.nop()


def kernel(x, ctx_1024, L0_attn_ln_w, L0_attn_ln_b, L0_attn_in_proj_w, L0_attn_conv_w, L0_attn_conv_b,
           L0_attn_dt_bias, L0_attn_A_log, L0_attn_D_skip, L0_attn_norm_w, L0_attn_out_proj_w, L0_ffn_gate_w,
           L0_ffn_gate_b, L0_ffn_w1, L0_ffn_w2, L0_ffn_w3, L0_ffn_ws1, L0_ffn_ws2, L0_ffn_ws3):
    import ml_dtypes

    import concourse.bacc as _bacc
    from concourse.bass_utils import run_bass_kernel_spmd as _run

    def lay(a):
        return np.ascontiguousarray(np.asarray(a))

    def on_partitions(a):
        a = np.asarray(a)
        return lay(np.swapaxes(a.reshape((a.shape[0] // P, P) + a.shape[1:]), 0, 1))

    ctx_rows = np.asarray(ctx_1024)
    of_group = np.arange(GROUPS) * GROUP // SEQ
    w13 = np.concatenate([np.asarray(L0_ffn_w1), np.asarray(L0_ffn_w3)], axis=1)
    arrays = {
        "x": lay(np.asarray(x).reshape(TOKENS, D)),
        "cst": constants(),
        "picks": row_pickers().astype(ml_dtypes.bfloat16),
        "lnwb": lay(np.stack([on_partitions(L0_attn_ln_w), on_partitions(L0_attn_ln_b)], axis=1)),
        "w_in": on_partitions(np.asarray(L0_attn_in_proj_w).T),
        "conv_w": on_partitions(np.asarray(L0_attn_conv_w)[:, 0, :]),
        "conv_b": on_partitions(L0_attn_conv_b),
        "rows8": lay(np.broadcast_to(np.stack([np.asarray(L0_attn_dt_bias), np.asarray(L0_attn_A_log)])[None],
                                     (P, 2, HEADS))),
        "skip_w": on_partitions(np.repeat(np.asarray(L0_attn_D_skip), HEAD)),
        "norm_w": on_partitions(L0_attn_norm_w),
        "w_out": on_partitions(np.asarray(L0_attn_out_proj_w).T),
        "ctx_in": lay(ctx_rows[of_group]),
        "ctx_t": lay(ctx_rows.transpose(0, 2, 1).reshape(2, KD, P, CTX).transpose(0, 2, 1, 3)[of_group]),
        "gate_t": on_partitions(np.asarray(L0_ffn_gate_w).T),
        "gate_b": lay(np.broadcast_to(np.asarray(L0_ffn_gate_b)[None], (P, EXPERTS))),
        "w13": lay(w13.transpose(0, 2, 1).reshape(EXPERTS, KD, P, 2 * FF).transpose(0, 2, 1, 3)),
        "w2": lay(np.asarray(L0_ffn_w2).transpose(0, 2, 1)),
        "ws1": on_partitions(np.asarray(L0_ffn_ws1).T),
        "ws3": on_partitions(np.asarray(L0_ffn_ws3).T),
        "ws2": lay(np.asarray(L0_ffn_ws2).T),
    }
    nc = _bacc.Bacc("TRN2", target_bir_lowering=False, num_devices=1)
    args = [nc.dram_tensor(name, a.shape, mybir.dt.from_np(a.dtype), kind="ExternalInput").ap()
            for name, a in arrays.items()]
    out = nc.dram_tensor("out", (TOKENS, D), F32, kind="ExternalOutput").ap()
    decoder_layer(nc, *args, out)
    r = _run(nc, [arrays], core_ids=[0])
    return r.results[0]["out"].reshape(2, SEQ, D)
```
